# Optimizing a Trainium2 kernel written in Bass

```python
import numpy as np
import jax
import jax.numpy as jnp

def _softmax(x, axis=-1):
    return jax.nn.softmax(x, axis=axis)

def _gelu(x):
    return jax.nn.gelu(x, approximate=True)

def _silu(x):
    return jax.nn.silu(x)

def _sigmoid(x):
    return jax.nn.sigmoid(x)

def _layernorm(x, axis=-1, eps=1e-05):
    m = jnp.mean(x, axis=axis, keepdims=True)
    v = jnp.var(x, axis=axis, keepdims=True)
    return (x - m) / jnp.sqrt(v + eps)

def _scatter_add(tgt, idx, src, axis=0):
    return tgt.at[idx].add(src)

def _segment_sum(src, seg, n):
    return jax.ops.segment_sum(src, seg, n)
kernel_name = 'mk_sandwich_d2_jaxref_r8_2873a3'

def setup_inputs(seed: int=0):
    np.random.seed(seed)
    _w = jnp.asarray

    def _L0_attn_setup():
        import jax, jax.numpy as jnp
        import numpy as np
        import math
        INPUT_WIDTH = 128
        KEY_WIDTH = 64
        VALUE_WIDTH = 64
        NUM_HEADS = 16
        NUM_GROUPS = 4
        HEADS_PER_GROUP = NUM_HEADS // NUM_GROUPS
        key = jax.random.key(seed)
        k_x, k_q, k_k, k_v, k_p = jax.random.split(key, 5)
        n, s = (2, 256)

        def lin(k, fan_in, fan_out):
            bound = 1.0 / math.sqrt(fan_in)
            return jax.random.uniform(k, (fan_in, fan_out), minval=-bound, maxval=bound, dtype=jnp.float32)
        return {'X': jax.random.normal(k_x, (n, s, INPUT_WIDTH), dtype=jnp.float32), 'Wq': lin(k_q, INPUT_WIDTH, NUM_HEADS * KEY_WIDTH), 'Wk': lin(k_k, INPUT_WIDTH, NUM_GROUPS * KEY_WIDTH), 'Wv': lin(k_v, INPUT_WIDTH, NUM_GROUPS * VALUE_WIDTH), 'Wpost': lin(k_p, NUM_HEADS * VALUE_WIDTH, INPUT_WIDTH)}
    _L0_attn_in = _L0_attn_setup()

    def _L0_ffn_setup():
        import jax, jax.numpy as jnp
        import numpy as np
        E = 16
        K = 4
        B, S, H, I = (4, 128, 128, 256)
        key = jax.random.key(seed)
        k0, k1, k2, k3 = jax.random.split(key, 4)
        scale = 0.02
        return {'hidden_states': jax.random.normal(k0, (B, S, H), jnp.float32), 'router_w': jax.random.normal(k1, (H, E), jnp.float32) * scale, 'router_b': jnp.zeros((E,), jnp.float32), 'w1': jax.random.normal(k2, (E, H, I), jnp.float32) * scale, 'b1': jnp.zeros((E, I), jnp.float32), 'w2': jax.random.normal(k3, (E, I, H), jnp.float32) * scale, 'b2': jnp.zeros((E, H), jnp.float32)}
    _L0_ffn_in = _L0_ffn_setup()

    def _L1_attn_setup():
        import jax, jax.numpy as jnp
        import numpy as np
        D_MODEL = 128
        NUM_LAYERS = 4
        D_STATE = 64
        D_CONV = 4
        EXPAND = 2
        HEADDIM = 64
        D_INNER = EXPAND * D_MODEL
        NHEADS = D_INNER // HEADDIM
        CONV_DIM = D_INNER + 2 * D_STATE
        D_IN_PROJ = 2 * D_INNER + 2 * D_STATE + NHEADS
        EPS = 1e-05

        def _layernorm(x, w, b):
            mu = jnp.mean(x, axis=-1, keepdims=True)
            xc = x - mu
            var = jnp.mean(xc * xc, axis=-1, keepdims=True)
            return xc * jax.lax.rsqrt(var + EPS) * w + b

        def _mamba2(x, in_w, conv_w, conv_b, dt_bias, A_log, Dp, norm_w, out_w):
            Bb, L, _ = x.shape
            zxbcdt = jnp.einsum('bld,de->ble', x, in_w)
            z = zxbcdt[..., :D_INNER]
            xBC = zxbcdt[..., D_INNER:D_INNER + CONV_DIM]
            dt = jax.nn.softplus(zxbcdt[..., -NHEADS:] + dt_bias)
            xp = jnp.pad(xBC, ((0, 0), (D_CONV - 1, 0), (0, 0)))
            conv = conv_b + sum((xp[:, k:k + L, :] * conv_w[k] for k in range(D_CONV)))
            xBC = jax.nn.silu(conv)
            xs = xBC[..., :D_INNER].reshape(Bb, L, NHEADS, HEADDIM)
            Bm = xBC[..., D_INNER:D_INNER + D_STATE]
            Cm = xBC[..., D_INNER + D_STATE:]
            A = -jnp.exp(A_log)
            dA = jnp.exp(dt * A)
            dBx = dt[..., None] * xs

            def step(h, t_in):
                dA_t, dBx_t, B_t, C_t = t_in
                h = h * dA_t[:, :, None, None] + dBx_t[..., None] * B_t[:, None, None, :]
                y = jnp.einsum('bhpn,bn->bhp', h, C_t)
                return (h, y)
            h0 = jnp.zeros((Bb, NHEADS, HEADDIM, D_STATE), x.dtype)
            xsT = (jnp.moveaxis(dA, 1, 0), jnp.moveaxis(dBx, 1, 0), jnp.moveaxis(Bm, 1, 0), jnp.moveaxis(Cm, 1, 0))
            _, yT = jax.lax.scan(step, h0, xsT)
            y = jnp.moveaxis(yT, 0, 1)
            y = y + Dp[None, None, :, None] * xs
            y = y.reshape(Bb, L, D_INNER)
            y = y * jax.nn.silu(z)
            y = y * jax.lax.rsqrt(jnp.mean(y * y, axis=-1, keepdims=True) + EPS) * norm_w
            return jnp.einsum('ble,ed->bld', y, out_w)
        key = jax.random.key(seed)
        ks = jax.random.split(key, 8)
        B, L = (4, 256)
        x = jax.random.normal(ks[0], (B, L, D_MODEL), dtype=jnp.float32)
        in_w = jax.random.normal(ks[1], (NUM_LAYERS, D_MODEL, D_IN_PROJ), dtype=jnp.float32) * 0.02
        conv_w = (jax.random.uniform(ks[2], (NUM_LAYERS, D_CONV, CONV_DIM), dtype=jnp.float32) - 0.5) * (2.0 / np.sqrt(D_CONV))
        conv_b = jnp.zeros((NUM_LAYERS, CONV_DIM), dtype=jnp.float32)
        u = jax.random.uniform(ks[3], (NUM_LAYERS, NHEADS), dtype=jnp.float32)
        dt = jnp.exp(u * (np.log(0.1) - np.log(0.001)) + np.log(0.001))
        dt_bias = dt + jnp.log(-jnp.expm1(-dt))
        A_log = jnp.log(jax.random.uniform(ks[4], (NUM_LAYERS, NHEADS), dtype=jnp.float32, minval=1.0, maxval=16.0))
        Dp = jnp.ones((NUM_LAYERS, NHEADS), dtype=jnp.float32)
        norm_w = jnp.ones((NUM_LAYERS, D_INNER), dtype=jnp.float32)
        out_w = jax.random.normal(ks[5], (NUM_LAYERS, D_INNER, D_MODEL), dtype=jnp.float32) * 0.02
        ln_w = jnp.ones((NUM_LAYERS, D_MODEL), dtype=jnp.float32)
        ln_b = jnp.zeros((NUM_LAYERS, D_MODEL), dtype=jnp.float32)
        return {'x': x, 'ln_w': ln_w, 'ln_b': ln_b, 'in_w': in_w, 'conv_w': conv_w, 'conv_b': conv_b, 'dt_bias': dt_bias, 'A_log': A_log, 'Dp': Dp, 'norm_w': norm_w, 'out_w': out_w}
    _L1_attn_in = _L1_attn_setup()

    def _L1_ffn_setup():
        import jax, jax.numpy as jnp
        import numpy as np
        TOP_K = 2
        EPS = 1e-05

        def layer_norm(x, g, b):
            mu = jnp.mean(x, axis=-1, keepdims=True)
            var = jnp.mean(jnp.square(x - mu), axis=-1, keepdims=True)
            return (x - mu) * jax.lax.rsqrt(var + EPS) * g + b
        key = jax.random.key(seed)
        ks = jax.random.split(key, 12)
        B, S, D, F, E = (2, 256, 128, 512, 8)
        std = 0.02
        return {'x': jax.random.normal(ks[0], (B, S, D), jnp.float32), 'g1': jnp.ones((D,), jnp.float32), 'be1': jnp.zeros((D,), jnp.float32), 'mix_w': jax.random.normal(ks[1], (D, D), jnp.float32) * std, 'mix_b': jnp.zeros((D,), jnp.float32), 'g2': jnp.ones((D,), jnp.float32), 'be2': jnp.zeros((D,), jnp.float32), 'router_w': jax.random.normal(ks[2], (D, E), jnp.float32) * std, 'w1': jax.random.normal(ks[3], (E, D, F), jnp.float32) * std, 'b1': jnp.zeros((E, F), jnp.float32), 'w2': jax.random.normal(ks[4], (E, F, D), jnp.float32) * std, 'b2': jnp.zeros((E, D), jnp.float32)}
    _L1_ffn_in = _L1_ffn_setup()
    _d = {'L0_attn_X': _L0_attn_in['X'], 'L0_attn_Wq': _L0_attn_in['Wq'], 'L0_attn_Wk': _L0_attn_in['Wk'], 'L0_attn_Wv': _L0_attn_in['Wv'], 'L0_attn_Wpost': _L0_attn_in['Wpost'], 'L0_ffn_router_w': _L0_ffn_in['router_w'], 'L0_ffn_router_b': _L0_ffn_in['router_b'], 'L0_ffn_w1': _L0_ffn_in['w1'], 'L0_ffn_b1': _L0_ffn_in['b1'], 'L0_ffn_w2': _L0_ffn_in['w2'], 'L0_ffn_b2': _L0_ffn_in['b2'], 'L1_attn_ln_w': _L1_attn_in['ln_w'], 'L1_attn_ln_b': _L1_attn_in['ln_b'], 'L1_attn_in_w': _L1_attn_in['in_w'], 'L1_attn_conv_w': _L1_attn_in['conv_w'], 'L1_attn_conv_b': _L1_attn_in['conv_b'], 'L1_attn_dt_bias': _L1_attn_in['dt_bias'], 'L1_attn_A_log': _L1_attn_in['A_log'], 'L1_attn_Dp': _L1_attn_in['Dp'], 'L1_attn_norm_w': _L1_attn_in['norm_w'], 'L1_attn_out_w': _L1_attn_in['out_w'], 'L1_ffn_g1': _L1_ffn_in['g1'], 'L1_ffn_be1': _L1_ffn_in['be1'], 'L1_ffn_mix_w': _L1_ffn_in['mix_w'], 'L1_ffn_mix_b': _L1_ffn_in['mix_b'], 'L1_ffn_g2': _L1_ffn_in['g2'], 'L1_ffn_be2': _L1_ffn_in['be2'], 'L1_ffn_router_w': _L1_ffn_in['router_w'], 'L1_ffn_w1': _L1_ffn_in['w1'], 'L1_ffn_b1': _L1_ffn_in['b1'], 'L1_ffn_w2': _L1_ffn_in['w2'], 'L1_ffn_b2': _L1_ffn_in['b2']}
    _x0 = _d['L0_attn_X']
    _d['L0_attn_X'] = jax.random.normal(jax.random.fold_in(jax.random.key(seed), 1), (8, 256, 128), dtype=_x0.dtype)
    del _x0
    return _d

def reference(L0_attn_X, L0_attn_Wq, L0_attn_Wk, L0_attn_Wv, L0_attn_Wpost, L0_ffn_router_w, L0_ffn_router_b, L0_ffn_w1, L0_ffn_b1, L0_ffn_w2, L0_ffn_b2, L1_attn_ln_w, L1_attn_ln_b, L1_attn_in_w, L1_attn_conv_w, L1_attn_conv_b, L1_attn_dt_bias, L1_attn_A_log, L1_attn_Dp, L1_attn_norm_w, L1_attn_out_w, L1_ffn_g1, L1_ffn_be1, L1_ffn_mix_w, L1_ffn_mix_b, L1_ffn_g2, L1_ffn_be2, L1_ffn_router_w, L1_ffn_w1, L1_ffn_b1, L1_ffn_w2, L1_ffn_b2):

    def _L0_attn_ref(X, Wq, Wk, Wv, Wpost):
        import jax, jax.numpy as jnp
        import numpy as np
        import math
        INPUT_WIDTH = 128
        KEY_WIDTH = 64
        VALUE_WIDTH = 64
        NUM_HEADS = 16
        NUM_GROUPS = 4
        HEADS_PER_GROUP = NUM_HEADS // NUM_GROUPS
        n, s, _ = X.shape
        Q = (X @ Wq).reshape(n, s, NUM_GROUPS, HEADS_PER_GROUP, KEY_WIDTH)
        K = (X @ Wk).reshape(n, s, NUM_GROUPS, KEY_WIDTH)
        V = (X @ Wv).reshape(n, s, NUM_GROUPS, VALUE_WIDTH)
        scale = 1.0 / math.sqrt(KEY_WIDTH)
        raw = jnp.einsum('bsgwe,btge->bstgw', Q, K * scale)
        attn = jax.nn.softmax(raw, axis=2)
        A = jnp.einsum('bstgw,btge->bsgwe', attn, V).reshape(n, s, NUM_HEADS * VALUE_WIDTH)
        P = A @ Wpost
        return X + P

    def _L0_ffn_ref(hidden_states, router_w, router_b, w1, b1, w2, b2):
        import jax, jax.numpy as jnp
        import numpy as np
        E = 16
        K = 4
        B, S, H, I = (4, 128, 128, 256)
        b, s, h = hidden_states.shape
        logits = hidden_states @ router_w + router_b
        probs = jax.nn.softmax(logits, axis=-1)
        topw, topi = jax.lax.top_k(probs, K)
        topw = topw / jnp.sum(topw, axis=-1, keepdims=True)
        combine = jnp.sum(jax.nn.one_hot(topi, E, dtype=hidden_states.dtype) * topw[..., None], axis=2)
        x = hidden_states.reshape(b * s, h)
        c = combine.reshape(b * s, E)

        def body(acc, expert):
            w1e, b1e, w2e, b2e, ce = expert
            hmid = jax.nn.gelu(x @ w1e + b1e, approximate=False)
            return (acc + (hmid @ w2e + b2e) * ce[:, None], None)
        out, _ = jax.lax.scan(body, jnp.zeros_like(x), (w1, b1, w2, b2, c.T))
        return out.reshape(b, s, h)

    def _L1_attn_ref(x, ln_w, ln_b, in_w, conv_w, conv_b, dt_bias, A_log, Dp, norm_w, out_w):
        import jax, jax.numpy as jnp
        import numpy as np
        D_MODEL = 128
        NUM_LAYERS = 4
        D_STATE = 64
        D_CONV = 4
        EXPAND = 2
        HEADDIM = 64
        D_INNER = EXPAND * D_MODEL
        NHEADS = D_INNER // HEADDIM
        CONV_DIM = D_INNER + 2 * D_STATE
        D_IN_PROJ = 2 * D_INNER + 2 * D_STATE + NHEADS
        EPS = 1e-05

        def _layernorm(x, w, b):
            mu = jnp.mean(x, axis=-1, keepdims=True)
            xc = x - mu
            var = jnp.mean(xc * xc, axis=-1, keepdims=True)
            return xc * jax.lax.rsqrt(var + EPS) * w + b

        def _mamba2(x, in_w, conv_w, conv_b, dt_bias, A_log, Dp, norm_w, out_w):
            Bb, L, _ = x.shape
            zxbcdt = jnp.einsum('bld,de->ble', x, in_w)
            z = zxbcdt[..., :D_INNER]
            xBC = zxbcdt[..., D_INNER:D_INNER + CONV_DIM]
            dt = jax.nn.softplus(zxbcdt[..., -NHEADS:] + dt_bias)
            xp = jnp.pad(xBC, ((0, 0), (D_CONV - 1, 0), (0, 0)))
            conv = conv_b + sum((xp[:, k:k + L, :] * conv_w[k] for k in range(D_CONV)))
            xBC = jax.nn.silu(conv)
            xs = xBC[..., :D_INNER].reshape(Bb, L, NHEADS, HEADDIM)
            Bm = xBC[..., D_INNER:D_INNER + D_STATE]
            Cm = xBC[..., D_INNER + D_STATE:]
            A = -jnp.exp(A_log)
            dA = jnp.exp(dt * A)
            dBx = dt[..., None] * xs

            def step(h, t_in):
                dA_t, dBx_t, B_t, C_t = t_in
                h = h * dA_t[:, :, None, None] + dBx_t[..., None] * B_t[:, None, None, :]
                y = jnp.einsum('bhpn,bn->bhp', h, C_t)
                return (h, y)
            h0 = jnp.zeros((Bb, NHEADS, HEADDIM, D_STATE), x.dtype)
            xsT = (jnp.moveaxis(dA, 1, 0), jnp.moveaxis(dBx, 1, 0), jnp.moveaxis(Bm, 1, 0), jnp.moveaxis(Cm, 1, 0))
            _, yT = jax.lax.scan(step, h0, xsT)
            y = jnp.moveaxis(yT, 0, 1)
            y = y + Dp[None, None, :, None] * xs
            y = y.reshape(Bb, L, D_INNER)
            y = y * jax.nn.silu(z)
            y = y * jax.lax.rsqrt(jnp.mean(y * y, axis=-1, keepdims=True) + EPS) * norm_w
            return jnp.einsum('ble,ed->bld', y, out_w)
        for i in range(NUM_LAYERS):
            xn = _layernorm(x, ln_w[i], ln_b[i])
            x = x + _mamba2(xn, in_w[i], conv_w[i], conv_b[i], dt_bias[i], A_log[i], Dp[i], norm_w[i], out_w[i])
        return x

    def _L1_ffn_ref(x, g1, be1, mix_w, mix_b, g2, be2, router_w, w1, b1, w2, b2):
        import jax, jax.numpy as jnp
        import numpy as np
        TOP_K = 2
        EPS = 1e-05

        def layer_norm(x, g, b):
            mu = jnp.mean(x, axis=-1, keepdims=True)
            var = jnp.mean(jnp.square(x - mu), axis=-1, keepdims=True)
            return (x - mu) * jax.lax.rsqrt(var + EPS) * g + b
        res = x
        n = layer_norm(x, g1, be1)
        x = res + n + (n @ mix_w + mix_b)
        res = x
        n = layer_norm(x, g2, be2)
        B, S, D = n.shape
        E = w1.shape[0]
        flat = n.reshape(-1, D)
        probs = jax.nn.softmax(flat @ router_w, axis=-1)
        topw, topi = jax.lax.top_k(probs, TOP_K)
        combine = jnp.sum(jax.nn.one_hot(topi, E, dtype=flat.dtype) * topw[..., None], axis=1)
        h = jax.nn.silu(jnp.einsum('td,edf->tef', flat, w1) + b1)
        y = jnp.einsum('tef,efd->ted', h, w2) + b2
        out = jnp.einsum('te,ted->td', combine, y)
        return res + out.reshape(B, S, D)
    x = L0_attn_X
    x = x + _layernorm(_L0_attn_ref(_layernorm(x, axis=-1), L0_attn_Wq, L0_attn_Wk, L0_attn_Wv, L0_attn_Wpost), axis=-1)
    x = x + _layernorm(_L0_ffn_ref(_layernorm(x, axis=-1), L0_ffn_router_w, L0_ffn_router_b, L0_ffn_w1, L0_ffn_b1, L0_ffn_w2, L0_ffn_b2), axis=-1)
    x = x + _layernorm(_L1_attn_ref(_layernorm(x, axis=-1), L1_attn_ln_w, L1_attn_ln_b, L1_attn_in_w, L1_attn_conv_w, L1_attn_conv_b, L1_attn_dt_bias, L1_attn_A_log, L1_attn_Dp, L1_attn_norm_w, L1_attn_out_w), axis=-1)
    x = x + _layernorm(_L1_ffn_ref(_layernorm(x, axis=-1), L1_ffn_g1, L1_ffn_be1, L1_ffn_mix_w, L1_ffn_mix_b, L1_ffn_g2, L1_ffn_be2, L1_ffn_router_w, L1_ffn_w1, L1_ffn_b1, L1_ffn_w2, L1_ffn_b2), axis=-1)
    return x

_drawn_inputs = setup_inputs


def setup_inputs(seed=0):
    import zlib

    import numpy as np

    out = dict(_drawn_inputs(seed))
    spreads = {'L0_ffn_router_b': (0.0, 0.1),
     'L0_ffn_b1': (0.0, 0.1),
     'L0_ffn_b2': (0.0, 0.1),
     'L1_attn_ln_w': (1.0, 0.2),
     'L1_attn_ln_b': (0.0, 0.365),
     'L1_attn_conv_b': (0.0, 0.1),
     'L1_attn_Dp': (1.0, 0.2),
     'L1_attn_norm_w': (1.0, 0.2),
     'L1_ffn_g1': (1.0, 0.6),
     'L1_ffn_be1': (0.0, 0.589),
     'L1_ffn_mix_b': (0.0, 0.669),
     'L1_ffn_g2': (1.0, 0.6),
     'L1_ffn_be2': (0.0, 0.8),
     'L1_ffn_b1': (0.0, 0.8),
     'L1_ffn_b2': (0.0, 0.8)}
    factors = {'L1_attn_dt_bias': 8.0,
     'L1_attn_A_log': 8.0,
     'L1_ffn_router_w': 8.0,
     'L1_ffn_w1': 8.0,
     'L1_ffn_w2': 8.0}
    for name, (base, spread) in spreads.items():
        noise = np.random.default_rng([zlib.crc32(name.encode()), seed]).standard_normal(out[name].shape)
        drawn = base * np.exp(spread * noise) if base else spread * noise
        out[name] = jnp.asarray(drawn.astype(out[name].dtype))
    for name, factor in factors.items():
        out[name] = (out[name] * factor).astype(out[name].dtype)
    return out
```

```python
from contextlib import ExitStack

import concourse.bass as bass
from concourse import mybir

F32 = mybir.dt.float32
ALU = mybir.AluOpType
ACT = mybir.ActivationFunctionType
AX = mybir.AxisListType

P = 128
EPS = 1e-5


def wait(eng, sem, value):
    if isinstance(value, int) and value <= 0:
        return
    eng.wait_ge(sem, value)


def rolled(eng, times, body):
    body(0)
    if times > 1:
        with eng.Fori(1, times) as i:
            body(i)


def chain(eng, sem, start=0):
    count = [start]

    def link(ins):
        count[0] += 1
        ins.then_inc(sem, 1)
        eng.wait_ge(sem, count[0])

    link.count = count
    return link


class Memory:

    def __init__(self, nc, ctx):
        self.nc, self.ctx, self.tensors, self.sems = nc, ctx, ctx, None

    def phase(self):
        self.tensors, self.sems = ExitStack(), []

    def end_phase(self):
        self.tensors.close()
        self.nc.clear_and_free_semaphores(self.sems)
        self.nc.all_engine_barrier()
        self.tensors, self.sems = self.ctx, None

    def sb(self, name, shape, dt=F32):
        return self.tensors.enter_context(self.nc.sbuf_tensor(name, shape, dt))

    def sem(self, name):
        if self.sems is None:
            return self.ctx.enter_context(self.nc.semaphore(name))
        self.sems.append(self.nc.alloc_semaphore(name=name))
        return self.sems[-1]


def layer_norm_stats(nc, v, mem, name, tiles, src, mean):
    stats = mem.stats
    half = P // 2
    link = chain(v, mem.sem(name + "_stats_step"))

    bn_done = mem.sem(name + "_bn")
    for t in range(tiles):
        v.bn_stats(stats[:, t, :], src(t)).then_inc(bn_done, 1)
    v.wait_ge(bn_done, tiles)
    me, mo, ve, vo = stats[:, 0:tiles, 1], stats[:, 0:tiles, 4], stats[:, 0:tiles, 2], stats[:, 0:tiles, 5]
    a, b, c = mem.ln_a[:, 0:tiles], mem.ln_b[:, 0:tiles], mem.ln_c[:, 0:tiles]
    link(v.tensor_tensor(a, me, mo, ALU.add))
    link(v.tensor_scalar(mean, a, 0.5, None, ALU.mult))
    link(v.tensor_tensor(b, me, mo, ALU.subtract))
    link(v.tensor_tensor(c, b, b, ALU.mult))
    link(v.tensor_tensor(a, ve, vo, ALU.add))
    link(v.tensor_scalar(b, a, 0.5 / half, EPS, ALU.mult, ALU.add))
    link(v.scalar_tensor_tensor(out=mem.var[:, 0:tiles], in0=c, scalar=0.25, in1=b, op0=ALU.mult, op1=ALU.add))
    v.sem_inc(mem.var_ready, 1)


def attention(nc, mem, x_all, w):
    NB, TPB = 8, 2
    NT = NB * TPB
    G, W, E = 4, 4, 64
    ps = mem.ps
    nT = mem.big_a[:, 0:NT * P]
    AT = mem.big_b[:].rearrange("p (c t) -> p c t", c=8)
    V = mem.big_c[:, 0:NT * G * E].rearrange("p (t g e) -> p t g e", t=NT, g=G)
    ident = mem.ident
    mean, rstd = mem.mean[:], mem.rstd[:]

    var_ready, rstd_ready = mem.sem("a0_var_ready"), mem.sem("a0_rstd_ready")
    mem.var_ready = var_ready
    n_ready, nT_mm, nT_sb, v_mm, v_sb = (mem.sem("a0_" + s) for s in ("n_ready", "nT_mm", "nT_sb", "v_mm", "v_sb"))
    ntile = mem.stage_a
    nTtile = mem.stage_b
    with nc.Block() as block:
        @block.vector
        def _(v):
            v.wait_ge(mem.x_in, 16)
            layer_norm_stats(nc, v, mem, "a0", NT, lambda t: x_all[:, t, :], mean)
            v.wait_ge(rstd_ready, 1)

            def body(i):
                for u in range(2):
                    t = i * 2 + u
                    wait(v, nT_mm, t - 1)
                    v.tensor_scalar(ntile[:, u, :], x_all[:, t, :], mean[:, bass.ds(t, 1)], rstd[:, bass.ds(t, 1)],
                                    ALU.subtract, ALU.mult).then_inc(n_ready, 1)
            rolled(v, NT // 2, body)

        @block.gpsimd
        def _(g):
            g.wait_ge(mem.consts_ready, 1)
            g.wait_ge(var_ready, 1)
            g.tensor_tensor(rstd, mem.var[:], mem.neg_half[:], ALU.pow).then_inc(rstd_ready, 1)

        @block.tensor
        def _(pe):
            pe.wait_ge(mem.consts_ready, 1)
            pe.wait_ge(w["attn_in"], w["attn_in_n"])

            def v_matmul(t, u):
                pe.wait_ge(nT_sb, 2 * t + 2)
                wait(pe, v_sb, t - 1)
                pe.matmul(ps[:, 2 + u, 0:G * E], nTtile[:, u, :], w["Wv"][:], start=True, stop=True).then_inc(v_mm, 1)

            def body(i):
                for u in range(2):
                    t = i * 2 + u
                    pe.wait_ge(n_ready, t + 1)
                    wait(pe, nT_sb, 2 * t - 2)
                    pe.transpose(ps[:, u, 0:P], ntile[:, u, :], ident[:]).then_inc(nT_mm, 1)
                    if u > 0 or not isinstance(i, int):
                        v_matmul(t - 1, 1 - u)
            rolled(pe, NT // 2, body)
            v_matmul(NT - 1, 1)

        @block.scalar
        def _(a):
            def v_copy(t, u):
                a.wait_ge(v_mm, t + 1)
                a.copy(V[:, t, :, :].rearrange("p g e -> p (g e)"), ps[:, 2 + u, 0:G * E]).then_inc(v_sb, 1)

            def body(i):
                for u in range(2):
                    t = i * 2 + u
                    a.wait_ge(nT_mm, t + 1)
                    wait(a, v_mm, t - 1)
                    a.copy(nTtile[:, u, :], ps[:, u, 0:P]).then_inc(nT_sb, 1)
                    a.copy(nT[:, bass.ts(t, P)], ps[:, u, 0:P]).then_inc(nT_sb, 1)
                    if u > 0 or not isinstance(i, int):
                        v_copy(t - 1, 1 - u)
            rolled(a, NT // 2, body)
            v_copy(NT - 1, 1)

    STEPS = G * TPB
    S = ps[:, 0:4, :].rearrange("p b (w t) -> p (b w) t", t=256).rearrange("p (s w) t -> p s w t", s=2)
    T = ps[:, 4:6, :].rearrange("p b (w s) -> p b w s", w=W)
    O = ps[:, 6, 0:256].rearrange("p (w e) -> p w e", w=W)
    ATp = ps[:, 6, 256:512].rearrange("p (c s) -> p c s", c=2)
    Qp, Kp = ps[:, 7, 0:256].rearrange("p (c s) -> p c s", c=2), ps[:, 7, 256:512]
    Q, K = mem.Q, mem.K
    pr, pT = mem.probs, mem.probsT
    At = mem.Atile
    nm, den, rden = mem.nm, mem.den, mem.rden
    names = "qk_mm q_sb k_sb s_mm max_ready p_ready t_mm pT_act pT_dve o_mm r_ready a_ready aT_mm aT_sb"
    s = {n: mem.sem("a1_" + n) for n in names.split()}
    with nc.Block() as block:
        def steps(eng, emit, lag):
            def body(b):
                for j in range(STEPS):
                    def back(l, j=j):
                        if j >= l:
                            return b * STEPS + (j - l), j - l, b
                        if isinstance(b, int) and b == 0:
                            return None
                        return b * STEPS + (j - l), j - l + STEPS, b - 1
                    emit(back, (b, j))
            body(0)
            with eng.Fori(1, NB - 1) as b:
                body(b)
            body(NB - 1)
            for j in range(lag):
                def back(l, j=j):
                    if l <= j:
                        return None
                    return NB * STEPS + j - l, STEPS + j - l, NB - 1
                emit(back, None)

        @block.tensor
        def _(pe):
            def project(k, j, b):
                g, st = j // 2, j % 2
                wait(pe, s["q_sb"], k)
                wait(pe, s["k_sb"], b * G + (j + 1) // 2)
                for c in range(2):
                    last = pe.matmul(Qp[:, c, :], w["Wq"][:, (g * 2 + c) * P:(g * 2 + c + 1) * P],
                                     nT[:, bass.ds(b * 256 + st * P, P)], start=True, stop=True)
                if st == 0:
                    last = pe.matmul(Kp, w["Wkk"][:, g, :, :].rearrange("p r e -> p (r e)"),
                                     nT[:, bass.ds(b * 256, 256)], start=True, stop=True)
                last.then_inc(s["qk_mm"], 1)

            def emit(back, here):
                now = back(0)
                if now:
                    k, j, b = now
                    if j + 1 < STEPS:
                        project(k + 1, j + 1, b)
                    elif not (isinstance(b, int) and b == NB - 1):
                        project(k + 1, 0, b + 1)
                    pe.wait_ge(s["q_sb"], k + 1)
                    pe.wait_ge(s["k_sb"], b * G + (j // 2 + 1))
                    wait(pe, s["p_ready"], k - 1)
                    for h in range(W):
                        o, c = 64 * (h % 2), h // 2
                        last = pe.matmul(S[:, j % 2, 2 * (h % 2) + c, :], Q[o:o + 64, j % 2, c, :], K[o:o + 64, (j // 2) % 2, :],
                                         start=True, stop=True)
                    last.then_inc(s["s_mm"], 1)
                if back(2):
                    k2, j2, b2 = back(2)
                    pe.wait_ge(s["pT_act"], k2 + 1)
                    pe.wait_ge(s["pT_dve"], k2 + 1)
                    wait(pe, s["aT_sb"], k2)
                    for h in range(W):
                        for tt in range(TPB):
                            last = pe.matmul(O[:, h, :], pT[:, j2 % 2, tt, h, :],
                                             V[:, b2 * TPB + tt, j2 // 2, :], start=(tt == 0), stop=(tt == 1))
                    last.then_inc(s["o_mm"], 1)
                if back(1):
                    k1, j1, b1 = back(1)
                    pe.wait_ge(s["p_ready"], k1 + 1)
                    wait(pe, s["pT_act"], k1)
                    wait(pe, s["pT_dve"], k1)
                    for tt in range(TPB):
                        for h in range(W):
                            last = pe.transpose(T[:, tt, h, :], pr[:, j1 % 2, h, tt * P:(tt + 1) * P], ident[:])
                    last.then_inc(s["t_mm"], 1)
                if back(2):
                    k2, j2, b2 = back(2)
                    pe.wait_ge(s["a_ready"], k2 + 1)
                    for c in range(2):
                        last = pe.transpose(ATp[:, c, :], At[:, j2 % 2, c * P:(c + 1) * P], ident[:])
                    last.then_inc(s["aT_mm"], 1)

            project(0, 0, 0)
            steps(pe, emit, 2)

        @block.scalar
        def _(a):
            def emit(back, here):
                if back(0):
                    k, j, b = back(0)
                    a.wait_ge(s["max_ready"], k + 1)
                    wait(a, s["t_mm"], k - 1)
                    wait(a, s["r_ready"], k - 1)
                    for h in range(W):
                        i = 2 * (h % 2) + h // 2
                        last = a.activation(pr[:, j % 2, h, :], S[:, j % 2, i, :], ACT.Exp,
                                            bias=nm[:, j % 2, i:i + 1], accum_out=den[:, j % 2, h:h + 1])
                    last.then_inc(s["p_ready"], 1)
                if back(1):
                    k1, j1, b1 = back(1)
                    a.wait_ge(s["t_mm"], k1 + 1)
                    wait(a, s["o_mm"], k1 - 1)
                    a.copy(pT[:, j1 % 2, 0, :, :], T[:, 0, :, :]).then_inc(s["pT_act"], 1)
            steps(a, emit, 1)

        @block.vector
        def _(v):
            def copies(k, j, b):
                wait(v, s["s_mm"], k - 1)
                v.wait_ge(s["qk_mm"], k + 1)
                v.tensor_copy(Q[:, j % 2, :, :], Qp).then_inc(s["q_sb"], 1)
                if j % 2 == 0:
                    wait(v, s["s_mm"], k - 2)
                    v.tensor_scalar(K[:, (j // 2) % 2, :], Kp, E ** -0.5, None, ALU.mult).then_inc(s["k_sb"], 1)

            def emit(back, here):
                if back(0):
                    k, j, b = back(0)
                    v.wait_ge(s["s_mm"], k + 1)
                    wait(v, s["p_ready"], k - 1)
                    v.tensor_reduce(nm[:, j % 2, :], S[:, j % 2, :, :], AX.X, ALU.max,
                                    negate=True).then_inc(s["max_ready"], 1)
                    if j + 1 < STEPS:
                        copies(k + 1, j + 1, b)
                    elif not (isinstance(b, int) and b == NB - 1):
                        copies(k + 1, 0, b + 1)
                if back(2):
                    k2, j2, b2 = back(2)
                    v.wait_ge(s["p_ready"], k2 + 1)
                    wait(v, s["a_ready"], k2)
                    v.reciprocal(rden[:], den[:, j2 % 2, :]).then_inc(s["r_ready"], 1)
                    v.wait_ge(s["r_ready"], k2 + 1)
                    v.wait_ge(s["o_mm"], k2 + 1)
                    wait(v, s["aT_mm"], k2 - 1)
                    v.tensor_tensor(At[:, j2 % 2, :].rearrange("p (w e) -> p w e", w=W), O,
                                    rden[:].rearrange("p (w o) -> p w o", o=1).broadcast_to([P, W, E]),
                                    ALU.mult).then_inc(s["a_ready"], 1)
                if back(1):
                    k1, j1, b1 = back(1)
                    v.wait_ge(s["t_mm"], k1 + 1)
                    wait(v, s["o_mm"], k1 - 1)
                    v.tensor_copy(pT[:, j1 % 2, 1, :, :], T[:, 1, :, :]).then_inc(s["pT_dve"], 1)
                if back(2):
                    v.wait_ge(s["aT_mm"], k2 + 1)
                    g, st = j2 // 2, j2 % 2
                    v.tensor_copy(AT[:, 2 * g:2 * g + 2, bass.ds(b2 * 256 + st * P, P)], ATp).then_inc(s["aT_sb"], 1)

            copies(0, 0, 0)
            steps(v, emit, 2)

    CH = NT // 4
    PTs = mem.stage_c
    r_all = mem.tokens_a
    n = {k: mem.sem("a2_" + k) for k in "p_mm p_sb pt_mm n_sb r_sb".split()}
    with nc.Block() as block:
        @block.tensor
        def _(pe):
            def body(c):
                for h in range(8):
                    last = pe.matmul(ps[:, 0, :], w["Wpost"][:, h, :], AT[:, h, bass.ds(c * 512, 512)],
                                     start=(h == 0), stop=(h == 7))
                last.then_inc(n["p_mm"], 1)
                pe.wait_ge(n["p_sb"], c + 1)
                wait(pe, n["r_sb"], c * 4)
                for u in range(4):
                    last = pe.transpose(ps[:, 1 + u, 0:P], PTs[:, u * P:(u + 1) * P], ident[:])
                last.then_inc(n["pt_mm"], 1)
            rolled(pe, CH, body)

        @block.scalar
        def _(a):
            def body(c):
                a.wait_ge(n["p_mm"], c + 1)
                wait(a, n["pt_mm"], c)
                a.copy(PTs[:], ps[:, 0, :]).then_inc(n["p_sb"], 1)
            rolled(a, CH, body)

        @block.vector
        def _(v):
            def body(c):
                for u in range(4):
                    t = c * 4 + u
                    v.tensor_scalar(r_all[:, t, :], x_all[:, t, :], mean[:, bass.ds(t, 1)], rstd[:, bass.ds(t, 1)],
                                    ALU.subtract, ALU.mult).then_inc(n["n_sb"], 1)
                v.wait_ge(n["pt_mm"], c + 1)
                v.wait_ge(n["n_sb"], c * 4 + 4)
                for u in range(4):
                    t = c * 4 + u
                    v.tensor_tensor(r_all[:, t, :], r_all[:, t, :], ps[:, 1 + u, 0:P], ALU.add).then_inc(n["r_sb"], 1)
            rolled(v, CH, body)
            v.wait_ge(n["r_sb"], NT)

    add_layer_norm(nc, mem, "a3", r_all, x_all)


def add_layer_norm(nc, mem, name, r_all, x_all):
    NT = 16
    mean, rstd = mem.mean[:], mem.rstd[:]
    rstd_ready, norm_step, x_step = mem.sem(name + "_rstd"), mem.sem(name + "_norm"), mem.sem(name + "_x")
    mem.var_ready = mem.sem(name + "_var")
    with nc.Block() as block:
        @block.vector
        def _(v):
            layer_norm_stats(nc, v, mem, name, NT, lambda t: r_all[:, t, :], mean)
            v.wait_ge(rstd_ready, 1)

            for t in range(NT):
                v.tensor_scalar(r_all[:, t, :], r_all[:, t, :], mean[:, t:t + 1], rstd[:, t:t + 1],
                                ALU.subtract, ALU.mult).then_inc(norm_step, 1)
            v.wait_ge(norm_step, NT)
            for q in range(4):
                v.tensor_tensor(x_all[:, 4 * q:4 * q + 4, :], x_all[:, 4 * q:4 * q + 4, :],
                                r_all[:, 4 * q:4 * q + 4, :], ALU.add).then_inc(x_step, 1)
            v.wait_ge(x_step, 4)

        @block.gpsimd
        def _(g):
            g.wait_ge(mem.var_ready, 1)
            g.tensor_tensor(rstd, mem.var[:], mem.neg_half[:], ALU.pow).then_inc(rstd_ready, 1)


def normalised_transposes(nc, mem, name, x_all, nT, width, products, weights_in, weights_n, pre=None):
    NT = 16
    ps, ident = mem.ps, mem.ident
    mean, rstd = mem.mean[:], mem.rstd[:]
    mem.var_ready = mem.sem(name + "_var_ready")
    rstd_ready = mem.sem(name + "_rstd_ready")
    n_ready, nT_mm, nT_sb, l_mm = (mem.sem(name + "_" + s) for s in ("n_ready", "nT_mm", "nT_sb", "l_mm"))
    ntile, nTtile = mem.stage_a, mem.stage_b
    copies = 1 if nT is None else 2
    results = ps[:, 2:6, :].rearrange("p b t -> p (b t)")
    with nc.Block() as block:
        @block.vector
        def _(v):
            layer_norm_stats(nc, v, mem, name, NT, lambda t: x_all[:, t, :], mean)
            v.wait_ge(rstd_ready, 1)

            def body(i):
                for u in range(2):
                    t = i * 2 + u
                    wait(v, nT_mm, t - 1)
                    v.tensor_scalar(ntile[:, u, :], x_all[:, t, :], mean[:, bass.ds(t, 1)], rstd[:, bass.ds(t, 1)],
                                    ALU.subtract, ALU.mult).then_inc(n_ready, 1)
            rolled(v, NT // 2, body)

        @block.gpsimd
        def _(g):
            g.wait_ge(mem.var_ready, 1)
            g.tensor_tensor(rstd, mem.var[:], mem.neg_half[:], ALU.pow).then_inc(rstd_ready, 1)

        @block.tensor
        def _(pe):
            pe.wait_ge(weights_in, weights_n)

            def product(t, u):
                pe.wait_ge(nT_sb, copies * t + copies)
                for j, (still, moving) in enumerate(products):
                    last = pe.matmul(results[:, bass.ds(t * width, width)], nTtile[:, u, :] if still is None else still,
                                     moving, start=(j == 0), stop=(j == len(products) - 1))
                last.then_inc(l_mm, 1)

            def body(i):
                for u in range(2):
                    t = i * 2 + u
                    pe.wait_ge(n_ready, t + 1)
                    wait(pe, nT_sb, copies * (t - 1))
                    pe.transpose(ps[:, u, 0:P], ntile[:, u, :], ident[:]).then_inc(nT_mm, 1)
                    if u > 0 or not isinstance(i, int):
                        product(t - 1, 1 - u)
            rolled(pe, NT // 2, body)
            product(NT - 1, 1)

        @block.scalar
        def _(a):
            def body(i):
                for u in range(2):
                    t = i * 2 + u
                    a.wait_ge(nT_mm, t + 1)
                    wait(a, l_mm, t - 1)
                    for dst in ([nTtile[:, u, :]] + ([] if nT is None else [nT[:, bass.ts(t, P)]])):
                        if pre is None:
                            a.copy(dst, ps[:, u, 0:P]).then_inc(nT_sb, 1)
                        else:
                            a.activation(dst, ps[:, u, 0:P], ACT.Identity, bias=pre[1], scale=pre[0]).then_inc(nT_sb, 1)
            rolled(a, NT // 2, body)


def route(nc, mem, name, experts, top, normalised, bias, b2, acc):
    NT = 16
    ps, ident = mem.ps, mem.ident
    N = NT * experts

    def tile3(x):
        return x[:, 0:N].rearrange("p (t e) -> p t e", e=experts)

    def over_experts(x):
        return x.rearrange("p (t o) -> p t o", o=1).broadcast_to([P, NT, experts])

    L, above, equal, seen, gates = (tile3(x) for x in (mem.r_logits, mem.r_above, mem.r_equal, mem.r_seen, mem.gates))
    best = mem.best
    small = mem.r_small
    centred, exp_ready, gates_ready = (mem.sem(name + "_" + s) for s in ("centred", "exp_ready", "gates_ready"))
    cT_mm, cT_sb, b_mm, acc_ready = (mem.sem(name + "_" + s) for s in ("cT_mm", "cT_sb", "b_mm", "acc_ready"))
    best_ready = mem.sem(name + "_best")
    cT = mem.gatesT
    with nc.Block() as block:
        @block.vector
        def _(v):
            link = chain(v, mem.sem(name + "_route_step"))
            flat = mem.r_logits[:, 0:N]
            if bias is not None:
                link(v.tensor_tensor(L, tile3(ps[:, 2, :]), bias.rearrange("p (o e) -> p o e", o=1).broadcast_to(
                    [P, NT, experts]), ALU.add))
            else:
                link(v.tensor_copy(flat, ps[:, 2, 0:N]))
            for t in range(NT):
                v.max(best[:, t, :], L[:, t, :]).then_inc(best_ready, 1)
            v.wait_ge(best_ready, NT)
            link(v.tensor_tensor(tile3(mem.r_exp), L, best[:, :, 0:1].broadcast_to([P, NT, experts]), ALU.subtract))
            v.sem_inc(centred, 1)
            kth = best[:, :, top - 1:top].broadcast_to([P, NT, experts])
            link(v.tensor_tensor(above, L, kth, ALU.is_gt))
            link(v.tensor_tensor(equal, L, kth, ALU.is_equal))
            link(v.tensor_reduce(small[:, 0, :], above, AX.X, ALU.add))
            link(v.tensor_scalar(small[:, 1, :], small[:, 0, :], -1.0, float(top), ALU.mult, ALU.add))
            link(v.tensor_tensor_scan(mem.r_seen[:, 0:N], mem.keep[experts][:, 0:N], mem.r_equal[:, 0:N], 0.0,
                                      ALU.mult, ALU.add))
            link(v.tensor_tensor(seen, seen, over_experts(small[:, 1, :]), ALU.is_le))
            link(v.tensor_tensor(seen, seen, equal, ALU.mult))
            link(v.tensor_tensor(seen, seen, above, ALU.add))
            v.wait_ge(exp_ready, 1)
            ex = tile3(mem.r_exp)
            link(v.tensor_tensor(gates, ex, seen, ALU.mult))
            link(v.tensor_reduce(small[:, 2, :], gates if normalised else ex, AX.X, ALU.add))
            link(v.reciprocal(small[:, 3, :], small[:, 2, :]))
            v.tensor_tensor(gates, gates, over_experts(small[:, 3, :]), ALU.mult).then_inc(gates_ready, 1)

        @block.scalar
        def _(a):
            a.wait_ge(centred, 1)
            a.activation(mem.r_exp[:, 0:N], mem.r_exp[:, 0:N], ACT.Exp).then_inc(exp_ready, 1)
            for q in range(4):
                a.wait_ge(cT_mm, q + 1)
                a.copy(cT[0:experts, q * 512:(q + 1) * 512], ps[0:experts, 3 + q % 2, :]).then_inc(cT_sb, 1)
            for q in range(4):
                a.wait_ge(b_mm, q + 1)
                a.copy(acc[:, 4 * q:4 * q + 4, :].rearrange("p t d -> p (t d)"), ps[:, 5 + q % 2, :]).then_inc(acc_ready, 1)

        @block.tensor
        def _(pe):
            pe.wait_ge(gates_ready, 1)
            for q in range(4):
                wait(pe, cT_sb, q - 1)
                for u in range(4):
                    last = pe.transpose(ps[0:experts, 3 + q % 2, u * P:(u + 1) * P], gates[:, 4 * q + u, :], ident[:])
                last.then_inc(cT_mm, 1)
            for q in range(4):
                pe.wait_ge(cT_sb, q + 1)
                wait(pe, acc_ready, q - 1)
                for u in range(4):
                    t = 4 * q + u
                    last = pe.matmul(ps[:, 5 + q % 2, u * P:(u + 1) * P], cT[0:experts, t * P:(t + 1) * P], b2,
                                     start=True, stop=True)
                last.then_inc(b_mm, 1)


def mixture(nc, mem, name, nT, acc, w1, w2, b1T, gate_of, func):
    ROUNDS, CH, HALF = 8, 4, 2
    ps = mem.ps
    W1, W2, Hs = mem.W1, mem.W2, mem.hidden
    H = ps[:, 0:4, :].rearrange("p (s h) t -> p s h t", s=2)
    Y = ps[:, 4:6, :]
    w_in = [mem.sem(f"{name}_w_in{u}") for u in range(2)]
    h_mm, h_sb, y_mm, acc_done = (mem.sem(name + "_" + s) for s in ("h_mm", "h_sb", "y_mm", "acc_done"))
    bias, bias_ready = mem.bias, mem.sem(name + "_bias_ready")
    with nc.Block() as block:
        def steps(eng, emit):
            def body(i):
                for u in range(2):
                    for c in range(CH):
                        k = i * (2 * CH) + (u * CH + c)
                        if u == 0 and c == 0:
                            back = None if isinstance(i, int) else (k - 1, i - 1, 1, CH - 1)
                        else:
                            back = (k - 1, i, u if c else u - 1, c - 1 if c else CH - 1)
                        emit((k, i, u, c), back)
            rolled(eng, ROUNDS, body)
            emit(None, (ROUNDS * 2 * CH - 1, ROUNDS - 1, 1, CH - 1))

        @block.sync
        def _(sp):
            def body(i):
                for u in range(2):
                    wait(sp, y_mm, (i - 1) * (2 * CH) + (u + 1) * CH)
                    sp.dma_start(W1[:, u, :], w1[i, u, :, :] if isinstance(i, int) else w1[bass.ds(i, 1), u, :, :].rearrange("a p f -> p (a f)")).then_inc(w_in[u], 16)
                    w2v = w2[i, u, :, :].rearrange("(h p) d -> p h d", p=P) if isinstance(i, int) else \
                        w2[bass.ds(i, 1), u, :, :].rearrange("a (h p) d -> p (a h) d", p=P)
                    sp.dma_start(W2[:, u, :, :], w2v).then_inc(w_in[u], 16)
            rolled(sp, ROUNDS, body)

        @block.tensor
        def _(pe):
            def emit(now, back):
                if now:
                    k, i, u, c = now
                    if c == 0:
                        pe.wait_ge(w_in[u], i * 32 + 32)
                    wait(pe, h_sb, k - 1)
                    for h in range(HALF):
                        last = pe.matmul(H[:, c % 2, h, :], W1[:, u, h * P:(h + 1) * P], nT[:, c * 512:(c + 1) * 512],
                                         start=True, stop=True)
                    last.then_inc(h_mm, 1)
                if back:
                    k, i, u, c = back
                    pe.wait_ge(h_sb, k + 1)
                    wait(pe, acc_done, k - 1)
                    for t in range(4):
                        for h in range(HALF):
                            last = pe.matmul(Y[:, c % 2, t * P:(t + 1) * P], Hs[:, c % 2, h, t * P:(t + 1) * P],
                                             W2[:, u, h, :], start=(h == 0), stop=(h == HALF - 1))
                    last.then_inc(y_mm, 1)
            steps(pe, emit)

        @block.scalar
        def _(a):
            def emit(now, back):
                if now:
                    k, i, u, c = now
                    a.wait_ge(h_mm, k + 1)
                    wait(a, y_mm, k - 1)
                    a.wait_ge(bias_ready, i * 2 + (u + 1))
                    for h in range(HALF):
                        last = a.activation(Hs[:, c % 2, h, :], H[:, c % 2, h, :], func,
                                            bias=bias[:, u, h:h + 1])
                    last.then_inc(h_sb, 1)
            steps(a, emit)

        @block.vector
        def _(v):
            def copy_bias(i, u):
                v.tensor_copy(bias[:, u, :], b1T[:, bass.ds(i * 4 + u * 2, 2)]).then_inc(bias_ready, 1)

            def emit(now, back):
                if back:
                    k, i, u, c = back
                    v.wait_ge(y_mm, k + 1)
                    wait(v, acc_done, k - 3)
                    for t in range(4):
                        tok = 4 * c + t
                        last = v.scalar_tensor_tensor(out=acc[:, tok, :], in0=Y[:, c % 2, t * P:(t + 1) * P],
                                                      scalar=gate_of(tok, i, u), in1=acc[:, tok, :],
                                                      op0=ALU.mult, op1=ALU.add)
                    last.then_inc(acc_done, 1)
                    if c == CH - 1:
                        copy_bias(i + 1, u)
            for u in range(2):
                copy_bias(0, u)
            steps(v, emit)


def add_mixed(nc, mem, name, tokens):
    done = mem.sem(name + "_done")
    with nc.Block() as block:
        @block.vector
        def _(v):
            for q in range(4):
                v.tensor_tensor(tokens[:, 4 * q:4 * q + 4, :].rearrange("p t d -> p (t d)"),
                                tokens[:, 4 * q:4 * q + 4, :].rearrange("p t d -> p (t d)"),
                                mem.ps[:, 2 + q, :], ALU.add).then_inc(done, 1)
            v.wait_ge(done, 4)


def add_tokens(nc, mem, name, tokens, more):
    done = mem.sem(name + "_done")
    with nc.Block() as block:
        @block.vector
        def _(v):
            for q in range(4):
                part = slice(4 * q, 4 * q + 4)
                v.tensor_tensor(tokens[:, part, :], tokens[:, part, :], more[:, part, :], ALU.add).then_inc(done, 1)
            v.wait_ge(done, 4)


LOG1P = (0.9999999954, -0.4999990399, 0.3333000404, -0.2495455887, 0.1967811726, -0.153118631,
         0.1061426468, -0.05706420072, 0.0199071609, -0.003256378468)

C_DTB, C_A, C_DP, C_CW, C_CB, C_LNW, C_LNB = 0, 4, 8, 12, 24, 27, 28
C_ALL = 32


class Steps:

    def __init__(self, eng, sem, per):
        self.eng, self.sem, self.per = eng, sem, per

    def at(self, turn):
        self.turn, self.j = turn, 0

    def link(self, ins):
        self.mark(ins)
        self.join()

    def mark(self, ins):
        self.j += 1
        assert self.j <= self.per
        ins.then_inc(self.sem, 1)

    def join(self):
        self.eng.wait_ge(self.sem, self.turn * self.per + self.j)

    def end(self):
        assert self.j == self.per, (self.j, self.per)


def mamba_constants(nc, mem, t, cols, at):
    L = 4
    tab, in_all, out_all = mem.layers, mem.in_all, mem.out_all
    zeroed, loaded, step, mask_step = (mem.sem("mc_" + s) for s in ("zeroed", "loaded", "step", "mask_step"))
    exp_ready, masks = mem.sem("mc_exp"), mem.sem("mc_masks")
    raw = mem.layer_rows
    with nc.Block() as block:
        @block.sync
        def _(sp):
            for i, name in enumerate(("dt_bias", "A_log", "Dp")):
                sp.dma_start(raw[:, i, :, :], t["L1_attn_" + name].rearrange("(o l) h -> o l h", o=1).broadcast_to(
                    [P, L, 4])).then_inc(loaded, 16)
            sp.dma_start(in_all[:], t["L1_attn_in_w"].rearrange("l d e -> d l e")).then_inc(loaded, 16)
            sp.dma_start(out_all[:], t["L1_attn_out_w"].rearrange("l (c p) d -> p (l c) d", p=P)).then_inc(loaded, 16)
            sp.wait_ge(loaded, 5 * 16)

        @block.scalar
        def _(a):
            a.wait_ge(loaded, 5 * 16)
            a.activation(raw[:, 1, :, :], raw[:, 1, :, :], ACT.Exp).then_inc(exp_ready, 1)

        @block.gpsimd
        def _(g):
            for m in (mem.upto, mem.after):
                g.memset(m[:], 1.0).then_inc(mask_step, 1)
            g.memset(mem.eps4[:], 4 * EPS).then_inc(mask_step, 1)
            g.wait_ge(mask_step, 3)
            g.affine_select(out=mem.upto[:], in_=mem.upto[:], pattern=[[1, P]], compare_op=ALU.is_ge, fill=0.0,
                            base=0, channel_multiplier=-1).then_inc(masks, 1)
            g.affine_select(out=mem.after[:], in_=mem.after[:], pattern=[[-1, P]], compare_op=ALU.is_gt, fill=0.0,
                            base=0, channel_multiplier=1).then_inc(masks, 1)
            g.wait_ge(masks, 2)

        @block.vector
        def _(v):
            link = chain(v, step)
            v.wait_ge(mem.vec_sb, 2)
            link(v.memset(tab[:], 0.0))
            link(v.memset(mem.xp[:], 0.0))
            link(v.tensor_scalar(tab[:, :, C_CW:C_CW + 12], at["conv_w"].rearrange("p (l k) -> p l k", l=L), 0.5, None, ALU.mult))
            link(v.tensor_scalar(tab[:, :, C_CB:C_CB + 3], at["conv_b"].rearrange("p (l k) -> p l k", l=L), 0.5, None, ALU.mult))
            link(v.tensor_copy(tab[:, :, C_LNW], at["ln_w"]))
            link(v.tensor_copy(tab[:, :, C_LNB], at["ln_b"]))
            v.wait_ge(loaded, 5 * 16)
            link(v.tensor_copy(tab[:, :, C_DTB:C_DTB + 4], raw[:, 0, :, :]))
            link(v.tensor_copy(tab[:, :, C_DP:C_DP + 4], raw[:, 2, :, :]))
            v.wait_ge(exp_ready, 1)
            link(v.tensor_scalar(tab[:, :, C_A:C_A + 4], raw[:, 1, :, :], -1.0, None, ALU.mult))
            for c in range(2 * L):
                link(v.tensor_scalar(out_all[:, c, :], out_all[:, c, :], at["norm_w"][:, c:c + 1], None, ALU.mult))


def mamba(nc, mem, xm):
    UNITS, Q = 16, 4
    IN = 644
    ps, ident = mem.ps, mem.ident
    xnp, dtp = ps[:, 0, :], ps[:, 0, 0:4 * Q]
    Xp = [ps[:, 1, :], ps[:, 2, :], ps[:, 1, :]]
    Zp = [ps[:, 2, :], ps[:, 1, :]]
    Dps = ps[:, 3, :].rearrange("p (h t) -> p h t", h=4)
    Gp, outp = ps[:, 4, 0:P], ps[:, 4, 256:256 + P]
    xBp, cump = ps[:, 5, 0:320], ps[:, 5, 320:328]
    Yp, Ip = ps[:, 6, 0:256], ps[:, 6, 256:512]
    Sp, yTp = ps[0:64, 7, 0:256], ps[:, 7, 256:512]
    tab, in_all, out_all = mem.layers, mem.in_all, mem.out_all
    m = mem.m
    s = {n: mem.sem("m_" + n) for n in (
        "lc_ready wx_ready stat_step var_ready rstd_ready xn_ready xnT_mm xnT_sb x_mm x_sb dt_mm dt_step ax_ready "
        "u_ready a_ready z_mm zt_ready g_ready conv_step conv_ready th_ready silu_ready am_ready d_mm g_mm xb_mm "
        "e_ready ec_ready xb_sb gm_ready m_ready dtx_ready dtxw_ready y0_ready y_mm s_sb y1_step y1_ready y2_ready "
        "sq_ready rs_step rs_ready yT_mm yT_sb out_mm x_done").split()}

    def heads(x, n=64):
        return x.rearrange("p (h n) -> p h n", h=4)

    def over(x, n):
        return x.rearrange("p (h o) -> p h o", o=1).broadcast_to([P, 4, n])

    def schedule(eng, front, tile):
        for piece in range(Q):
            front(0, 0, 0, piece)

        def body(i):
            last = isinstance(i, int) and i == UNITS // 2 - 1
            for u in range(2):
                for q in range(Q):
                    def back(l, u=u, q=q):
                        j = u * Q + q - l
                        if j >= 0:
                            return i * 2 * Q + j, j % Q, j // Q, i * 2 + j // Q, i
                        if isinstance(i, int) and i == 0:
                            return None
                        j += 2 * Q
                        return (i - 1) * 2 * Q + j, j % Q, j // Q, (i - 1) * 2 + j // Q, i - 1
                    tile(back)
                    if not (last and u == 1):
                        if u == 0:
                            front(i * 2 + 1, i, 1, q)
                        else:
                            front(i * 2 + 2, i + 1, 0, q)
        body(0)
        with eng.Fori(1, UNITS // 2 - 1) as i:
            body(i)
        body(UNITS // 2 - 1)
        for l0 in range(2):
            def back(l, l0=l0):
                if l <= l0:
                    return None
                k = UNITS * Q + l0 - l
                return k, k % Q, (k // Q) % 2, k // Q, UNITS // 2 - 1
            tile(back)

    with nc.Block() as block:
        @block.tensor
        def _(pe):
            def front(M, i, u, piece):
                l = i // 2
                if piece == 0:
                    pe.wait_ge(s["xn_ready"], M * Q + Q)
                    wait(pe, s["dt_step"], M * 1)
                    for q in range(Q):
                        last = pe.transpose(xnp[:, q * P:(q + 1) * P], m.xn[:, q, :], ident[:])
                    last.then_inc(s["xnT_mm"], 1)
                if piece == 1:
                    pe.wait_ge(s["xnT_sb"], M + 1)
                    pe.wait_ge(s["wx_ready"], M + 1)
                    wait(pe, s["g_ready"], M * 2)
                    for c in range(2):
                        pe.matmul(Xp[c], m.Wx[:, u, c * P:(c + 1) * P], m.xnT[:, u, :], start=True,
                                  stop=True).then_inc(s["x_mm"], 1)
                    for q in range(Q):
                        last = pe.matmul(dtp[:, 4 * q:4 * q + 4], m.xnT[:, u, q * P:(q + 1) * P],
                                         in_all[:, l, 640:644], start=True, stop=True)
                    last.then_inc(s["dt_mm"], 1)
                if piece == 2:
                    pe.wait_ge(s["x_sb"], M * 3 + 1)
                    pe.matmul(Xp[2], m.Wx[:, u, 2 * P:3 * P], m.xnT[:, u, :], start=True, stop=True).then_inc(s["x_mm"], 1)
                if piece in (2, 3):
                    pe.wait_ge(s["x_sb"], M * 3 + piece)
                    for q in (2 * piece - 4, 2 * piece - 3):
                        last = pe.matmul(Zp[piece - 2][:, (q % 2) * 256:(q % 2) * 256 + 256],
                                         m.xnT[:, u, q * P:(q + 1) * P], in_all[:, l, 0:256], start=True, stop=True)
                    last.then_inc(s["z_mm"], 1)

            def tile(back):
                if back(0):
                    k, q, u, M, i = back(0)
                    tok = slice(q * P, (q + 1) * P)
                    pe.wait_ge(s["am_ready"], k + 1)
                    wait(pe, s["e_ready"], k)
                    for h in range(4):
                        last = pe.matmul(Dps[:, h, :], m.am[:, q % 2, h, :], mem.upto[:], start=True, stop=True)
                    last.then_inc(s["d_mm"], 1)
                    pe.wait_ge(s["silu_ready"], M * 4 + 4)
                    wait(pe, s["x_done"], k - 2)
                    wait(pe, s["gm_ready"], k)
                    pe.matmul(Gp, m.xs[0:64, u, 2, tok], m.CT[0:64, u, tok], start=True, stop=True).then_inc(s["g_mm"], 1)
                    wait(pe, s["xb_sb"], k)
                    for c in range(2):
                        pe.transpose(xBp[:, c * P:(c + 1) * P], m.xs[:, u, c, tok], ident[:])
                    pe.transpose(xBp[:, 256:320], m.xs[0:64, u, 2, tok], ident[0:64, 0:64])
                    pe.matmul(cump[:, 0:4], mem.upto[:], m.a[:, u, q, :], start=True, stop=True)
                    pe.matmul(cump[:, 4:8], mem.after[:], m.a[:, u, q, :], start=True, stop=True).then_inc(s["xb_mm"], 1)
                if back(1):
                    k, q, u, M, i = back(1)
                    tok = slice(q * P, (q + 1) * P)
                    pe.wait_ge(s["m_ready"], k + 1)
                    pe.wait_ge(s["dtx_ready"], k + 1)
                    wait(pe, s["y1_ready"], k)
                    for h in range(4):
                        last = pe.matmul(Yp[:, h * 64:(h + 1) * 64], m.M[:, q % 2, h, :],
                                         m.dtx[:, q % 2, h * 64:(h + 1) * 64], start=True, stop=True)
                    if q % 2 == 0:
                        pe.wait_ge(s["dtxw_ready"], (M * 2) + (q // 2 + 1))
                        wait(pe, s["yT_sb"], k - 1)
                        last = pe.matmul(Sp, m.xB[:, q % 2, 256:320], m.dtxw[:], start=True, stop=True)
                    else:
                        pe.wait_ge(s["s_sb"], (M * 2) + (q // 2 + 1))
                        last = pe.matmul(Ip, m.CT[0:64, u, tok], m.state[:], start=True, stop=True)
                    last.then_inc(s["y_mm"], 1)
                if back(2):
                    k, q, u, M, i = back(2)
                    l = i // 2
                    pe.wait_ge(s["y2_ready"], k + 1)
                    newer = 1 if q % 2 == 0 or back(1) else 0
                    pe.wait_ge(s["s_sb"], M * 2 + ((q + 1) // 2 + newer))
                    for c in range(2):
                        last = pe.transpose(yTp[:, c * P:(c + 1) * P], m.y2[:, q % 2, c * P:(c + 1) * P], ident[:])
                    last.then_inc(s["yT_mm"], 1)
                    pe.wait_ge(s["yT_sb"], k + 1)
                    if not back(0):
                        pe.wait_ge(s["x_done"], k)
                    pe.wait_ge(s["gm_ready"], k + 3 if back(0) else UNITS * Q)
                    for c in range(2):
                        last = pe.matmul(outp, m.yT[:, q % 2, c, :],
                                         out_all[:, l * 2 + c, :],
                                         start=(c == 0), stop=(c == 1))
                    last.then_inc(s["out_mm"], 1)
            schedule(pe, front, tile)

        @block.scalar
        def _(a):
            def front(M, i, u, piece):
                lc = m.lc[:, u, :]

                def evacuate(c):
                    a.wait_ge(s["x_mm"], M * 3 + (c + 1))
                    if c == 0:
                        wait(a, s["silu_ready"], M * 4)
                    src = Xp[c]
                    a.activation(m.xc[:, c, :], src, ACT.Identity, bias=lc[:, C_CB + c:C_CB + c + 1],
                                 scale=lc[:, C_CW + 9 + c:C_CW + 10 + c])
                    a.copy(mem.xp[:, c, :, 3:259], src.rearrange("p (b t) -> p b t", b=2)).then_inc(s["x_sb"], 1)

                if piece == 0:
                    a.wait_ge(s["xnT_mm"], M + 1)
                    a.wait_ge(s["lc_ready"], M + 1)
                    a.activation(m.xnT[:, u, :], xnp, ACT.Identity, bias=lc[:, C_LNB:C_LNB + 1],
                                 scale=lc[:, C_LNW:C_LNW + 1]).then_inc(s["xnT_sb"], 1)
                if piece == 1:
                    evacuate(0)
                    evacuate(1)
                    a.wait_ge(s["ax_ready"], M + 1)
                    a.activation(m.eu[:], m.ax[:], ACT.Exp, scale=-1.0).then_inc(s["u_ready"], 1)
                if piece == 2:
                    evacuate(2)
                if piece in (2, 3):
                    a.wait_ge(s["z_mm"], M * 2 + (piece - 1))
                    wait(a, s["g_ready"], M * 2 + (piece - 2))
                    a.activation(m.zt[:], Zp[piece - 2], ACT.Tanh, scale=0.5).then_inc(s["zt_ready"], 1)
                if piece == 3:
                    for c in range(3):
                        a.wait_ge(s["conv_ready"], M * 3 + (c + 1))
                        a.activation(m.th[:, c, :], m.xc[:, c, :], ACT.Tanh).then_inc(s["th_ready"], 1)

            def tile(back):
                if back(0):
                    k, q, u, M, i = back(0)
                    a.wait_ge(s["d_mm"], k + 1)
                    wait(a, s["m_ready"], k - 1)
                    a.activation(m.E[:, q % 2, :], ps[:, 3, :], ACT.Exp).then_inc(s["e_ready"], 1)
                    a.wait_ge(s["xb_mm"], k + 1)
                    wait(a, s["y1_ready"], k - 1)
                    a.activation(m.ec[:, q % 2, :], cump, ACT.Exp).then_inc(s["ec_ready"], 1)
                    wait(a, s["y_mm"], k - 1)
                    wait(a, s["y0_ready"], k - 1)
                    a.copy(m.xB[:, q % 2, :], xBp).then_inc(s["xb_sb"], 1)
                if back(1):
                    k, q, u, M, i = back(1)
                    if q % 2 == 0:
                        a.wait_ge(s["y_mm"], k + 1)
                        a.copy(m.state[:], Sp).then_inc(s["s_sb"], 1)
                if back(2):
                    k, q, u, M, i = back(2)
                    a.wait_ge(s["yT_mm"], k + 1)
                    wait(a, s["out_mm"], k - 1)
                    a.copy(m.yT[:, q % 2, :, :].rearrange("p c t -> p (c t)"), yTp).then_inc(s["yT_sb"], 1)
                    wait(a, s["rs_ready"], k - 1)
                    a.activation(m.junk[:, q % 2, :], m.y2[:, q % 2, :], ACT.Square, scale=1.0 / 16,
                                 accum_out=m.ssq[:, q % 2, :]).then_inc(s["sq_ready"], 1)
            schedule(a, front, tile)

        @block.vector
        def _(v):
            st = Steps(v, s["stat_step"], 8)
            cs = Steps(v, s["conv_step"], 6)
            dt = Steps(v, mem.sem("m_dt_chain"), 11)
            ys = Steps(v, s["y1_step"], 2)

            def front(M, i, u, piece):
                lc = m.lc[:, u, :]
                l, base = i // 2, (i % 2) * 8 + u * 4

                def conv(c):
                    v.wait_ge(s["x_sb"], M * 3 + (c + 1))
                    xc = m.xc[:, c, :].rearrange("p (b t) -> p b t", b=2)
                    for tap in range(3):
                        ins = v.scalar_tensor_tensor(out=xc, in0=mem.xp[:, c, :, tap:tap + 256],
                                                     scalar=lc[:, C_CW + tap * 3 + c:C_CW + tap * 3 + c + 1], in1=xc,
                                                     op0=ALU.mult, op1=ALU.add)
                        if tap < 2:
                            cs.link(ins)
                        else:
                            ins.then_inc(s["conv_ready"], 1)

                def silu(c, rows, out):
                    v.scalar_tensor_tensor(out=out, in0=m.th[rows, c, :], scalar=1.0, in1=m.xc[rows, c, :],
                                           op0=ALU.add, op1=ALU.mult).then_inc(s["silu_ready"], 1)

                def gate(half):
                    v.wait_ge(s["zt_ready"], M * 2 + (half + 1))
                    v.scalar_tensor_tensor(out=m.g[:, u, 2 * half:2 * half + 2, :].rearrange("p q e -> p (q e)"),
                                           in0=m.zt[:], scalar=1.0, in1=Zp[half], op0=ALU.add,
                                           op1=ALU.mult).then_inc(s["g_ready"], 1)

                if piece == 0:
                    st.at(M)
                    wait(v, s["x_done"], M * Q - 12)
                    wait(v, s["y0_ready"], M * Q - 4)
                    v.tensor_scalar(lc, tab[:, l, :], 1.0, None, ALU.mult).then_inc(s["lc_ready"], 1)
                    for q in range(Q):
                        st.mark(v.bn_stats(m.stats[:, q, :], xm[:, base + q, :]))
                    st.join()
                    wait(v, s["x_mm"], M * 3 - 3)
                    v.tensor_scalar(m.Wx[:, u, :], in_all[:, l, 256:640], 1.0, None, ALU.mult).then_inc(s["wx_ready"], 1)
                    for q in range(Q):
                        st.mark(v.bn_aggr(m.mv[:, q, :], m.stats[:, q, :]))
                    st.join()
                    v.tensor_scalar(m.veps[:], m.mv[:, :, 1], EPS, None, ALU.add).then_inc(s["var_ready"], 1)
                    wait(v, s["xnT_mm"], M)
                    v.wait_ge(s["rstd_ready"], M + 1)
                    for q in range(Q):
                        v.tensor_scalar(m.xn[:, q, :], xm[:, base + q, :], m.mv[:, q, 0:1], m.rstd[:, q:q + 1],
                                        ALU.subtract, ALU.mult).then_inc(s["xn_ready"], 1)
                    st.end()
                if piece == 1:
                    dt.at(M)
                    v.wait_ge(s["dt_mm"], M + 1)
                    v.tensor_tensor(m.x4[:], dtp.rearrange("p (q h) -> p q h", q=Q),
                                    lc[:, C_DTB:C_DTB + 4].rearrange("p (o h) -> p o h", o=1).broadcast_to([P, Q, 4]),
                                    ALU.add).then_inc(s["dt_step"], 1)
                    v.wait_ge(s["dt_step"], M + 1)
                    v.scalar_tensor_tensor(out=m.ax[:], in0=m.x4[:], scalar=-1.0, in1=m.x4[:], op0=ALU.mult,
                                           op1=ALU.max).then_inc(s["ax_ready"], 1)
                if piece == 2:
                    v.wait_ge(s["u_ready"], M + 1)
                    dt.link(v.tensor_scalar(m.poly[:], m.eu[:], LOG1P[9], None, ALU.mult))
                    for c in LOG1P[8::-1]:
                        dt.link(v.scalar_tensor_tensor(out=m.poly[:], in0=m.poly[:], scalar=c, in1=m.eu[:],
                                                       op0=ALU.add, op1=ALU.mult))
                    dt.link(v.scalar_tensor_tensor(out=m.sp[:, u, :, :], in0=m.x4[:], scalar=0.0, in1=m.poly[:],
                                                   op0=ALU.max, op1=ALU.add))
                    dt.end()
                    wait(v, s["am_ready"], M * Q - 4)
                    v.tensor_tensor(m.a[:, u, :, :], m.sp[:, u, :, :],
                                    lc[:, C_A:C_A + 4].rearrange("p (o h) -> p o h", o=1).broadcast_to([P, Q, 4]),
                                    ALU.mult).then_inc(s["a_ready"], 1)
                    cs.at(M)
                    conv(0)
                    conv(1)
                    wait(v, s["y2_ready"], M * Q - 4)
                    gate(0)
                if piece == 3:
                    conv(2)
                    v.wait_ge(s["th_ready"], M * 3 + 1)
                    wait(v, s["y_mm"], M * Q - 4)
                    silu(0, slice(0, P), m.xs[:, u, 0, :])
                    v.wait_ge(s["th_ready"], M * 3 + 2)
                    silu(1, slice(0, P), m.xs[:, u, 1, :])
                    gate(1)
                    v.wait_ge(s["th_ready"], M * 3 + 3)
                    silu(2, slice(0, 64), m.xs[0:64, u, 2, :])
                    silu(2, slice(64, P), m.CT[0:64, u, :])

            def tile(back):
                if back(0):
                    k, q, u, M, i = back(0)
                    v.wait_ge(s["g_mm"], k + 1)
                    v.tensor_tensor(m.Gm[:], Gp, mem.upto[:], ALU.mult).then_inc(s["gm_ready"], 1)
                    v.wait_ge(s["gm_ready"], k + 1)
                    v.wait_ge(s["e_ready"], k + 1)
                    wait(v, s["y_mm"], k - 1)
                    v.tensor_tensor(m.M[:, q % 2, :, :], heads(m.E[:, q % 2, :]),
                                    m.Gm[:].rearrange("p (o t) -> p o t", o=1).broadcast_to([P, 4, P]),
                                    ALU.mult).then_inc(s["m_ready"], 1)
                if back(1):
                    k, q, u, M, i = back(1)
                    v.wait_ge(s["y_mm"], k + 1)
                    v.wait_ge(s["y0_ready"], k + 1)
                    wait(v, s["y2_ready"], k - 1)
                    y1 = m.y1[:, q % 2, :]
                    if q % 2 == 0:
                        v.tensor_tensor(y1, m.y0[:, q % 2, :], Yp, ALU.add).then_inc(s["y1_ready"], 1)
                    else:
                        ys.at(M * 2 + q // 2)
                        ys.link(v.tensor_tensor(heads(m.yi[:]), heads(Ip), over(m.ec[:, q % 2, 0:4], 64), ALU.mult))
                        ys.link(v.tensor_tensor(m.yi[:], m.yi[:], m.y0[:, q % 2, :], ALU.add))
                        v.tensor_tensor(y1, m.yi[:], Yp, ALU.add).then_inc(s["y1_ready"], 1)
                if back(2):
                    k, q, u, M, i = back(2)
                    v.wait_ge(s["out_mm"], k + 1)
                    v.wait_ge(s["rs_ready"], k + 1)
                    tok = (i % 2) * 8 + (u * 4 + q)
                    v.scalar_tensor_tensor(out=xm[:, tok, :], in0=outp, scalar=m.rs[:, q % 2, :], in1=xm[:, tok, :],
                                           op0=ALU.mult, op1=ALU.add).then_inc(s["x_done"], 1)
            schedule(v, front, tile)
            v.wait_ge(s["x_done"], UNITS * Q)

        @block.gpsimd
        def _(g):
            rs = Steps(g, s["rs_step"], 1)

            def scale_decays(k, q, u, M):
                g.wait_ge(s["a_ready"], M + 1)
                wait(g, s["d_mm"], k - 1)
                g.tensor_tensor(m.am[:, q % 2, :, :], mem.after[:].rearrange("p (o t) -> p o t", o=1).broadcast_to([P, 4, P]),
                                over(m.a[:, u, q, :], P), ALU.mult).then_inc(s["am_ready"], 1)

            def front(M, i, u, piece):
                if piece == 0:
                    g.wait_ge(s["var_ready"], M + 1)
                    wait(g, s["xn_ready"], M * Q)
                    g.tensor_tensor(m.rstd[:], m.veps[:], mem.neg_half[:, 0:Q], ALU.pow).then_inc(s["rstd_ready"], 1)
                if piece == 3:
                    scale_decays(M * Q, 0, u, M)

            def tile(back):
                if back(0):
                    k, q, u, M, i = back(0)
                    if q < Q - 1:
                        scale_decays(k + 1, q + 1, u, M)
                    g.wait_ge(s["xb_sb"], k + 1)
                    wait(g, s["y_mm"], k - 1)
                    g.tensor_tensor(heads(m.dtx[:, q % 2, :]), heads(m.xB[:, q % 2, 0:256]), over(m.sp[:, u, q, :], 64),
                                    ALU.mult).then_inc(s["dtx_ready"], 1)
                    if q % 2 == 0:
                        g.wait_ge(s["dtx_ready"], k + 1)
                        g.wait_ge(s["ec_ready"], k + 1)
                        g.tensor_tensor(heads(m.dtxw[:]), heads(m.dtx[:, q % 2, :]), over(m.ec[:, q % 2, 4:8], 64),
                                        ALU.mult).then_inc(s["dtxw_ready"], 1)
                    wait(g, s["y1_ready"], k - 1)
                    g.tensor_tensor(heads(m.y0[:, q % 2, :]), heads(m.xB[:, q % 2, 0:256]),
                                    over(m.lc[:, u, C_DP:C_DP + 4], 64), ALU.mult).then_inc(s["y0_ready"], 1)
                if back(1):
                    k, q, u, M, i = back(1)
                    g.wait_ge(s["y1_ready"], k + 1)
                    wait(g, s["sq_ready"], k - 1)
                    g.tensor_tensor(m.y2[:, q % 2, :], m.y1[:, q % 2, :], m.g[:, u, q, :], ALU.mult).then_inc(s["y2_ready"], 1)
                if back(2):
                    k, q, u, M, i = back(2)
                    rs.at(k)
                    g.wait_ge(s["sq_ready"], k + 1)
                    wait(g, s["x_done"], k - 1)
                    rs.link(g.tensor_tensor(m.rt[:, q % 2, :], m.ssq[:, q % 2, :], mem.eps4[:, 0:1], ALU.add))
                    g.tensor_tensor(m.rs[:, q % 2, :], m.rt[:, q % 2, :], mem.neg_half[:, 0:1], ALU.pow).then_inc(s["rs_ready"], 1)
            schedule(g, front, tile)


def normalise(nc, mem, name, src, dst):
    NT = 16
    mean, rstd = mem.mean[:], mem.rstd[:]
    rstd_ready, done = mem.sem(name + "_rstd"), mem.sem(name + "_done")
    mem.var_ready = mem.sem(name + "_var")
    with nc.Block() as block:
        @block.vector
        def _(v):
            layer_norm_stats(nc, v, mem, name, NT, lambda t: src[:, t, :], mean)
            v.wait_ge(rstd_ready, 1)

            for t in range(NT):
                v.tensor_scalar(dst[:, t, :], src[:, t, :], mean[:, t:t + 1], rstd[:, t:t + 1],
                                ALU.subtract, ALU.mult).then_inc(done, 1)
            v.wait_ge(done, NT)

        @block.gpsimd
        def _(g):
            g.wait_ge(mem.var_ready, 1)
            g.tensor_tensor(rstd, mem.var[:], mem.neg_half[:], ALU.pow).then_inc(rstd_ready, 1)


class Buffers:
    pass


def program(nc, t, out):
    with ExitStack() as ctx:
        mem = Memory(nc, ctx)
        NT = 16
        x_all = mem.sb("x_all", [P, NT, P])
        mem.ps = ctx.enter_context(nc.psum_tensor("ps", [P, 8, 512], F32))
        mem.big_a = mem.sb("big_a", [P, 2048])
        mem.tokens_b = mem.sb("tokens_b", [P, NT, P])
        mem.tokens_a = mem.sb("tokens_a", [P, NT, P])
        mem.ident = mem.sb("ident", [P, P])
        mem.neg_half = mem.sb("neg_half", [P, NT])
        mem.stats = mem.sb("stats", [P, NT, 6])
        mem.ln_a, mem.ln_b, mem.ln_c, mem.var, mem.mean, mem.rstd = (
            mem.sb(n, [P, NT]) for n in ("ln_a", "ln_b", "ln_c", "var", "mean", "rstd"))
        mem.stage_a, mem.stage_b = mem.sb("stage_a", [P, 2, P]), mem.sb("stage_b", [P, 2, P])
        w = {}
        mem.r_logits, mem.r_above, mem.r_equal, mem.r_seen, mem.r_exp, mem.gates = (
            mem.sb(n, [P, 256]) for n in ("r_logits", "r_above", "r_equal", "r_seen", "r_exp", "gates"))
        mem.best, mem.r_small, mem.gatesT = mem.sb("best", [P, NT, 8]), mem.sb("r_small", [P, 4, NT]), mem.sb("gatesT", [16, NT * P])
        mem.keep = {e: mem.sb(f"keep{e}", [P, NT * e]) for e in (16, 8)}
        mem.layers, mem.layer_rows = mem.sb("layers", [P, 4, C_ALL]), mem.sb("layer_rows", [P, 3, 4, 4])
        mem.in_all, mem.out_all = mem.sb("in_all", [P, 4, 644]), mem.sb("out_all", [P, 8, P])
        mem.upto, mem.after, mem.eps4 = mem.sb("upto", [P, P]), mem.sb("after", [P, P]), mem.sb("eps4", [P, 1])
        mem.xp = mem.sb("xp", [P, 3, 2, 259])
        mem.W1, mem.W2 = mem.sb("W1", [P, 2, 256]), mem.sb("W2", [P, 2, 2, P])
        mem.bias = mem.sb("bias", [P, 2, 2])
        mem.hidden = mem.sb("hidden", [P, 2, 2, 512])
        w["router0"], w["router1"] = mem.sb("router0", [P, 16]), mem.sb("router1", [P, 8])
        w["mix_w"], w["mix_b"], w["ones"] = mem.sb("mix_w", [P, P]), mem.sb("mix_b", [1, P]), mem.sb("ones", [1, P])
        w["rb0"] = mem.sb("rb0", [P, 16])
        w["b2_0"], w["b2_1"] = mem.sb("b2_0", [16, P]), mem.sb("b2_1", [8, P])
        rows = [mem.sb(f"rows{i}", [P, P]) for i in range(2)]
        cols = [mem.sb(f"cols{i}", [P, P]) for i in range(2)]
        mem.vec_in, mem.vec_mm, mem.vec_sb = mem.sem("vec_in"), mem.sem("vec_mm"), mem.sem("vec_sb")
        rows_zero, keep_zero = mem.sem("rows_zero"), mem.sem("keep_zero")
        mem.x_in, mem.consts_ready = mem.sem("x_in"), mem.sem("consts_ready")
        w["attn_in"], w["attn_in_n"] = mem.sem("attn_in"), 5 * 16
        ident_zero = mem.sem("ident_zero")
        out_done = mem.sem("out_done")

        mem.phase()
        w["Wq"] = mem.sb("Wq", [P, 1024])
        w["Wkk"] = mem.sb("Wkk", [P, 4, 2, 64])
        w["Wv"] = mem.sb("Wv", [P, 256])
        w["Wpost"] = mem.sb("Wpost", [P, 8, P])
        mem.stage_c = mem.sb("stage_c", [P, 512])
        mem.Q, mem.K = mem.sb("Q", [P, 2, 2, P]), mem.sb("K", [P, 2, 256])
        mem.probs, mem.probsT = mem.sb("probs", [P, 2, 4, 256]), mem.sb("probsT", [P, 2, 2, 4, P])
        mem.Atile = mem.sb("Atile", [P, 2, 256])
        mem.nm, mem.den, mem.rden = mem.sb("nm", [P, 2, 4]), mem.sb("den", [P, 2, 4]), mem.sb("rden", [P, 4])
        mem.big_b, mem.big_c = mem.sb("big_b", [P, 8 * 2048]), mem.sb("big_c", [P, 4096])
        vector_rows, at = [], {}
        place = [0, 0]

        def vector(name, tile, src):
            n = src.shape[0]
            vector_rows.append((tile, place[tile], src))
            at[name] = cols[tile][:, place[tile]:place[tile] + n]
            place[tile] += n

        vector("b1_0", 0, t["L0_ffn_b1"].rearrange("e (h p) -> (e h) p", p=P))
        vector("b1_1", 0, t["L1_ffn_b1"].rearrange("e (h p) -> (e h) p", p=P))
        for n in ("g1", "be1", "g2", "be2"):
            vector(n, 1, t["L1_ffn_" + n].rearrange("(o d) -> o d", o=1))
        vector("conv_w", 1, t["L1_attn_conv_w"].rearrange("l k (c p) -> (l k c) p", p=P))
        vector("conv_b", 1, t["L1_attn_conv_b"].rearrange("l (c p) -> (l c) p", p=P))
        vector("ln_w", 1, t["L1_attn_ln_w"])
        vector("ln_b", 1, t["L1_attn_ln_b"])
        vector("norm_w", 1, t["L1_attn_norm_w"].rearrange("l (c p) -> (l c) p", p=P))
        b1_at = [0, 32]
        vec_in_n = 16 * (len(vector_rows) + 7)

        with nc.Block() as block:
            @block.sync
            def _(sp):
                sp.dma_start(x_all[:], t["L0_attn_X"].rearrange("b (t p) d -> p (b t) d", p=P)).then_inc(mem.x_in, 16)
                sp.dma_start(w["Wv"][:], t["L0_attn_Wv"]).then_inc(w["attn_in"], 16)
                wk = t["L0_attn_Wk"].rearrange("d (g e) -> d g e", g=4)
                for r in range(2):
                    sp.dma_start(w["Wkk"][:, :, r, :], wk).then_inc(w["attn_in"], 16)
                sp.dma_start(w["Wq"][:], t["L0_attn_Wq"]).then_inc(w["attn_in"], 16)
                sp.dma_start(w["Wpost"][:], t["L0_attn_Wpost"].rearrange("(c p) d -> p c d", p=P)).then_inc(w["attn_in"], 16)

                sp.wait_ge(rows_zero, 2)
                for tile, at, src in vector_rows:
                    n = src.shape[0]
                    sp.dma_start(rows[tile][at:at + n, :], src).then_inc(mem.vec_in, 16)
                sp.dma_start(w["router0"][:], t["L0_ffn_router_w"]).then_inc(mem.vec_in, 16)
                sp.dma_start(w["router1"][:], t["L1_ffn_router_w"]).then_inc(mem.vec_in, 16)
                sp.dma_start(w["rb0"][:], t["L0_ffn_router_b"].rearrange("(o e) -> o e", o=1).broadcast_to([P, 16])).then_inc(mem.vec_in, 16)
                sp.dma_start(w["b2_0"][:], t["L0_ffn_b2"]).then_inc(mem.vec_in, 16)
                sp.dma_start(w["mix_w"][:], t["L1_ffn_mix_w"]).then_inc(mem.vec_in, 16)
                sp.dma_start(w["mix_b"][:], t["L1_ffn_mix_b"].rearrange("(o d) -> o d", o=1)).then_inc(mem.vec_in, 16)
                sp.dma_start(w["b2_1"][:], t["L1_ffn_b2"]).then_inc(mem.vec_in, 16)

            @block.tensor
            def _(pe):
                pe.wait_ge(mem.consts_ready, 1)
                pe.wait_ge(mem.vec_in, vec_in_n)
                for i in range(2):
                    pe.transpose(mem.ps[:, i, 0:P], rows[i][:], mem.ident[:]).then_inc(mem.vec_mm, 1)

            @block.scalar
            def _(a):
                for i in range(2):
                    a.wait_ge(mem.vec_mm, i + 1)
                    a.copy(cols[i][:], mem.ps[:, i, 0:P]).then_inc(mem.vec_sb, 1)

            @block.vector
            def _(v):
                for i in range(2):
                    v.memset(rows[i][:], 0.0).then_inc(rows_zero, 1)
                v.memset(w["ones"][:], 1.0)
                for e in (16, 8):
                    v.memset(mem.keep[e][:], 1.0).then_inc(keep_zero, 1)
                v.wait_ge(keep_zero, 2)
                for e in (16, 8):
                    v.memset(mem.keep[e][:].rearrange("p (t e) -> p t e", e=e)[:, :, 0:1], 0.0).then_inc(keep_zero, 1)
                v.wait_ge(keep_zero, 4)

            @block.gpsimd
            def _(g):
                g.memset(mem.neg_half[:], -0.5)
                g.memset(mem.ident[:], 0.0).then_inc(ident_zero, 1)
                g.wait_ge(ident_zero, 1)
                g.affine_select(out=mem.ident[:], in_=mem.ident[:], pattern=[[-1, P]], compare_op=ALU.not_equal,
                                fill=1.0, base=0, channel_multiplier=1).then_inc(mem.consts_ready, 1)

        attention(nc, mem, x_all, w)
        mem.end_phase()
        nT, acc = mem.big_a[:], mem.tokens_a
        mem.phase()
        normalised_transposes(nc, mem, "e0", x_all, nT, 16, [(None, w["router0"][:])], mem.vec_in, vec_in_n)
        route(nc, mem, "e1", 16, 4, True, w["rb0"][:], w["b2_0"][:], acc)
        gates0 = mem.gates[:, 0:NT * 16]
        mixture(nc, mem, "e2", nT, acc, t["L0_ffn_w1"].rearrange("(i u) h f -> i u h f", u=2),
                t["L0_ffn_w2"].rearrange("(i u) f h -> i u f h", u=2), cols[0][:, b1_at[0]:b1_at[0] + 36],
                lambda tok, i, u: gates0[:, bass.ds(i * 2 + (tok * 16 + u), 1)], ACT.Gelu)
        add_layer_norm(nc, mem, "e3", acc, x_all)
        mem.end_phase()
        mamba_constants(nc, mem, t, cols, at)
        xm = mem.tokens_a
        normalise(nc, mem, "m0", x_all, xm)
        mem.phase()
        mem.m = m = Buffers()
        m.lc = mem.sb("m_lc", [P, 2, C_ALL])
        m.Wx = mem.sb("m_Wx", [P, 2, 384])
        m.stats = mem.sb("m_stats", [P, 4, 6])
        m.mv = mem.sb("m_mv", [P, 4, 2])
        m.veps = mem.sb("m_veps", [P, 4])
        m.rstd = mem.sb("m_rstd", [P, 4])
        m.xn = mem.sb("m_xn", [P, 4, P])
        m.xnT = mem.sb("m_xnT", [P, 2, 512])
        m.xc = mem.sb("m_xc", [P, 3, 512])
        m.th = mem.sb("m_th", [P, 3, 512])
        m.xs = mem.sb("m_xs", [P, 2, 3, 512])
        m.CT = mem.sb("m_CT", [64, 2, 512])
        m.zt = mem.sb("m_zt", [P, 512])
        m.g = mem.sb("m_g", [P, 2, 4, 256])
        m.x4 = mem.sb("m_x4", [P, 4, 4])
        m.ax = mem.sb("m_ax", [P, 4, 4])
        m.eu = mem.sb("m_eu", [P, 4, 4])
        m.poly = mem.sb("m_poly", [P, 4, 4])
        m.sp = mem.sb("m_sp", [P, 2, 4, 4])
        m.a = mem.sb("m_a", [P, 2, 4, 4])
        m.am = mem.sb("m_am", [P, 2, 4, P])
        m.E = mem.sb("m_E", [P, 2, 512])
        m.Gm = mem.sb("m_Gm", [P, P])
        m.M = mem.sb("m_M", [P, 2, 4, P])
        m.ec = mem.sb("m_ec", [P, 2, 8])
        m.xB = mem.sb("m_xB", [P, 2, 320])
        m.dtx = mem.sb("m_dtx", [P, 2, 256])
        m.dtxw = mem.sb("m_dtxw", [P, 256])
        m.y0 = mem.sb("m_y0", [P, 2, 256])
        m.state = mem.sb("m_state", [64, 256])
        m.yi = mem.sb("m_yi", [P, 256])
        m.y1 = mem.sb("m_y1", [P, 2, 256])
        m.y2 = mem.sb("m_y2", [P, 2, 256])
        m.junk = mem.sb("m_junk", [P, 2, 256])
        m.ssq = mem.sb("m_ssq", [P, 2, 1])
        m.rt = mem.sb("m_rt", [P, 2, 1])
        m.rs = mem.sb("m_rs", [P, 2, 1])
        m.yT = mem.sb("m_yT", [P, 2, 2, P])
        mamba(nc, mem, xm)
        mem.end_phase()
        add_layer_norm(nc, mem, "m2", xm, x_all)
        x2 = mem.tokens_b
        normalise(nc, mem, "f0", x_all, x2)
        normalised_transposes(nc, mem, "f1", x2, None, P,
                              [(None, mem.ident[:]), (None, w["mix_w"][:]), (w["ones"][:], w["mix_b"][:])],
                              mem.vec_in, vec_in_n, pre=(at["g1"], at["be1"]))
        add_mixed(nc, mem, "f2", x2)
        normalised_transposes(nc, mem, "f3", x2, nT, 8, [(None, w["router1"][:])], mem.vec_in, vec_in_n,
                              pre=(at["g2"], at["be2"]))
        route(nc, mem, "f4", 8, 2, False, None, w["b2_1"][:], acc)
        gates1 = mem.gates[:, 0:NT * 8]
        mixture(nc, mem, "f5", nT, acc, t["L1_ffn_w1"].rearrange("e h (s f) -> e s h f", s=2),
                t["L1_ffn_w2"].rearrange("e (s f) h -> e s f h", s=2), cols[0][:, b1_at[1]:b1_at[1] + 36],
                lambda tok, i, u: gates1[:, bass.ds(i + tok * 8, 1)], ACT.Silu)
        add_tokens(nc, mem, "f6", acc, x2)
        add_layer_norm(nc, mem, "f7", acc, x_all)

        with nc.Block() as block:
            @block.sync
            def _(sp):
                sp.dma_start(out.rearrange("b (t p) d -> p (b t) d", p=P), x_all[:]).then_inc(out_done, 16)
                sp.wait_ge(out_done, 16)


_INS = ['L0_attn_X', 'L0_attn_Wq', 'L0_attn_Wk', 'L0_attn_Wv', 'L0_attn_Wpost', 'L0_ffn_router_w', 'L0_ffn_router_b',
        'L0_ffn_w1', 'L0_ffn_b1', 'L0_ffn_w2', 'L0_ffn_b2', 'L1_attn_ln_w', 'L1_attn_ln_b', 'L1_attn_in_w',
        'L1_attn_conv_w', 'L1_attn_conv_b', 'L1_attn_dt_bias', 'L1_attn_A_log', 'L1_attn_Dp', 'L1_attn_norm_w',
        'L1_attn_out_w', 'L1_ffn_g1', 'L1_ffn_be1', 'L1_ffn_mix_w', 'L1_ffn_mix_b', 'L1_ffn_g2', 'L1_ffn_be2',
        'L1_ffn_router_w', 'L1_ffn_w1', 'L1_ffn_b1', 'L1_ffn_w2', 'L1_ffn_b2']
_OUTS = [((8, 256, 128), 'float32')]


def kernel(**inputs):
    import numpy as _np
    import concourse.bacc as _bacc
    from concourse import mybir as _mybir
    from concourse.bass_utils import run_bass_kernel_spmd as _run

    nc = _bacc.Bacc("TRN2", target_bir_lowering=False, num_devices=1)
    arrays, tensors = {}, {}
    for name in _INS:
        a = _np.ascontiguousarray(inputs[name])
        arrays[f"in_{name}_dram"] = a
        tensors[name] = nc.dram_tensor(f"in_{name}_dram", a.shape, _mybir.dt.from_np(a.dtype), kind="ExternalInput").ap()
    shape, dtype = _OUTS[0]
    out = nc.dram_tensor("out_0_dram", shape, _mybir.dt.from_np(_np.dtype(dtype)), kind="ExternalOutput").ap()
    program(nc, tensors, out)
    r = _run(nc, [arrays], core_ids=[0])
    return r.results[0]["out_0_dram"]
```

```python
from contextlib import ExitStack

import concourse.bass as bass
from concourse import mybir

F32 = mybir.dt.float32
F32R = mybir.dt.float32r
ALU = mybir.AluOpType
ACT = mybir.ActivationFunctionType
AX = mybir.AxisListType

P = 128
EPS = 1e-5


def wait(eng, sem, value):
    if isinstance(value, int) and value <= 0:
        return
    eng.wait_ge(sem, value)


def rolled(eng, times, body):
    body(0)
    if times > 1:
        with eng.Fori(1, times) as i:
            body(i)


def chain(eng, sem, start=0):
    count = [start]

    def link(ins):
        count[0] += 1
        ins.then_inc(sem, 1)
        eng.wait_ge(sem, count[0])

    link.count = count
    return link


class Memory:

    def __init__(self, nc, ctx):
        self.nc, self.ctx, self.tensors, self.sems = nc, ctx, ctx, None

    def phase(self):
        self.tensors, self.sems = ExitStack(), []

    def end_phase(self):
        self.tensors.close()
        self.nc.clear_and_free_semaphores(self.sems)
        self.nc.all_engine_barrier()
        self.tensors, self.sems = self.ctx, None

    def sb(self, name, shape, dt=F32):
        return self.tensors.enter_context(self.nc.sbuf_tensor(name, shape, dt))

    def sem(self, name):
        if self.sems is None:
            return self.ctx.enter_context(self.nc.semaphore(name))
        self.sems.append(self.nc.alloc_semaphore(name=name))
        return self.sems[-1]


def layer_norm_stats(v, mem, name, src, ready=lambda t: None):
    bn, merged = mem.sem(name + "_bn"), mem.sem(name + "_merged")
    for half in range(2):
        tiles = range(8 * half, 8 * half + 8)
        for t in tiles:
            ready(t)
            v.bn_stats(mem.stats[:, t, :], src(t)).then_inc(bn, 1)
        v.wait_ge(bn, 8 * half + 8)
        for t in tiles:
            v.bn_aggr(mem.mv[:, t, :], mem.stats[:, t, :]).then_inc(merged, 1)
        v.wait_ge(merged, 8 * half + 8)
        v.tensor_scalar(mem.var[:, 8 * half:8 * half + 8], mem.mv[:, 8 * half:8 * half + 8, 1], EPS, None,
                        ALU.add).then_inc(mem.var_ready, 1)


def layer_norm_power(g, mem, rstd_ready):
    for half in range(2):
        cols = slice(8 * half, 8 * half + 8)
        g.wait_ge(mem.var_ready, half + 1)
        g.tensor_tensor(mem.rstd[:, cols], mem.var[:, cols], mem.neg_half[:, cols], ALU.pow).then_inc(rstd_ready, 1)


def attention(nc, mem, x_all, w):
    NB, TPB = 8, 2
    NT = NB * TPB
    G, W, E = 4, 4, 64
    ps = mem.ps
    nT = mem.big_a[:, 0:NT * P]
    AT = mem.big_b[:].rearrange("p (c t) -> p c t", c=8)
    V = mem.big_c[:, 0:NT * G * E].rearrange("p (t g e) -> p t g e", t=NT, g=G)
    ident = mem.ident
    rstd = mem.rstd[:]

    var_ready, rstd_ready = mem.sem("a0_var_ready"), mem.sem("a0_rstd_ready")
    mem.var_ready = var_ready
    n_ready, nT_mm, nT_sb, v_mm, v_sb = (mem.sem("a0_" + s) for s in ("n_ready", "nT_mm", "nT_sb", "v_mm", "v_sb"))
    ntile = mem.stage_a[:, :, 0, :]
    nTtile = mem.stage_b
    with nc.Block() as block:
        @block.vector
        def _(v):
            v.wait_ge(mem.x_in, 16)
            layer_norm_stats(v, mem, "a0", lambda t: x_all[:, t, :])
            v.wait_ge(rstd_ready, 2)

            def body(i):
                for u in range(2):
                    t = i * 2 + u
                    wait(v, nT_mm, t - 1)
                    v.tensor_scalar(ntile[:, u, :], x_all[:, t, :], mem.mv[:, bass.ds(t, 1), 0], rstd[:, bass.ds(t, 1)],
                                    ALU.subtract, ALU.mult).then_inc(n_ready, 1)
            rolled(v, NT // 2, body)

        @block.gpsimd
        def _(g):
            g.wait_ge(mem.consts_ready, 1)
            layer_norm_power(g, mem, rstd_ready)

        @block.tensor
        def _(pe):
            pe.wait_ge(mem.consts_ready, 1)
            pe.wait_ge(w["attn_in"], w["attn_in_n"])

            def v_matmul(t, u):
                pe.wait_ge(nT_sb, 2 * t + 2)
                wait(pe, v_sb, t - 1)
                pe.matmul(ps[:, 2 + u, 0:G * E], nTtile[:, u, :], w["Wv"][:], start=True, stop=True).then_inc(v_mm, 1)

            def body(i):
                for u in range(2):
                    t = i * 2 + u
                    pe.wait_ge(n_ready, t + 1)
                    wait(pe, nT_sb, 2 * t - 2)
                    pe.transpose(ps[:, u, 0:P], ntile[:, u, :], ident[:]).then_inc(nT_mm, 1)
                    if u > 0 or not isinstance(i, int):
                        v_matmul(t - 1, 1 - u)
            rolled(pe, NT // 2, body)
            v_matmul(NT - 1, 1)

        @block.scalar
        def _(a):
            def v_copy(t, u):
                a.wait_ge(v_mm, t + 1)
                a.copy(V[:, t, :, :].rearrange("p g e -> p (g e)"), ps[:, 2 + u, 0:G * E]).then_inc(v_sb, 1)

            def body(i):
                for u in range(2):
                    t = i * 2 + u
                    a.wait_ge(nT_mm, t + 1)
                    wait(a, v_mm, t - 1)
                    a.copy(nTtile[:, u, :], ps[:, u, 0:P]).then_inc(nT_sb, 1)
                    a.copy(nT[:, bass.ts(t, P)], ps[:, u, 0:P]).then_inc(nT_sb, 1)
                    if u > 0 or not isinstance(i, int):
                        v_copy(t - 1, 1 - u)
            rolled(a, NT // 2, body)
            v_copy(NT - 1, 1)

    STEPS = G * TPB
    S = ps[:, 0:4, :].rearrange("p b (w t) -> p (b w) t", t=256).rearrange("p (s w) t -> p s w t", s=2)
    T = ps[:, 4:6, :].rearrange("p b (w s) -> p b w s", w=W)
    O = ps[:, 6, 0:256].rearrange("p (w e) -> p w e", w=W)
    ATp = ps[:, 6, 256:512].rearrange("p (c s) -> p c s", c=2)
    Qp, Kp = ps[:, 7, 0:256].rearrange("p (c s) -> p c s", c=2), ps[:, 7, 256:512]
    Q, K = mem.Q, mem.K
    pr, pT = mem.probs, mem.probsT
    At = mem.Atile
    nm, den, rden = mem.nm, mem.den, mem.rden
    names = "qk_mm q_sb k_sb s_mm max_ready p_ready t_mm pT_act pT_dve o_mm r_ready a_ready aT_mm aT_sb"
    s = {n: mem.sem("a1_" + n) for n in names.split()}
    with nc.Block() as block:
        def steps(eng, emit, lag):
            def body(b):
                for j in range(STEPS):
                    def back(l, j=j):
                        if j >= l:
                            return b * STEPS + (j - l), j - l, b
                        if isinstance(b, int) and b == 0:
                            return None
                        return b * STEPS + (j - l), j - l + STEPS, b - 1
                    emit(back, (b, j))
            body(0)
            with eng.Fori(1, NB - 1) as b:
                body(b)
            body(NB - 1)
            for j in range(lag):
                def back(l, j=j):
                    if l <= j:
                        return None
                    return NB * STEPS + j - l, STEPS + j - l, NB - 1
                emit(back, None)

        @block.tensor
        def _(pe):
            def project(k, j, b):
                g, st = j // 2, j % 2
                wait(pe, s["q_sb"], k)
                wait(pe, s["k_sb"], b * G + (j + 1) // 2)
                for c in range(2):
                    last = pe.matmul(Qp[:, c, :], w["Wq"][:, (g * 2 + c) * P:(g * 2 + c + 1) * P],
                                     nT[:, bass.ds(b * 256 + st * P, P)], start=True, stop=True)
                if st == 0:
                    last = pe.matmul(Kp, w["Wkk"][:, g, :, :].rearrange("p r e -> p (r e)"),
                                     nT[:, bass.ds(b * 256, 256)], start=True, stop=True)
                last.then_inc(s["qk_mm"], 1)

            def emit(back, here):
                now = back(0)
                if now:
                    k, j, b = now
                    if j + 1 < STEPS:
                        project(k + 1, j + 1, b)
                    elif not (isinstance(b, int) and b == NB - 1):
                        project(k + 1, 0, b + 1)
                    pe.wait_ge(s["q_sb"], k + 1)
                    pe.wait_ge(s["k_sb"], b * G + (j // 2 + 1))
                    wait(pe, s["p_ready"], k - 1)
                    for h in range(W):
                        o, c = 64 * (h % 2), h // 2
                        last = pe.matmul(S[:, j % 2, 2 * (h % 2) + c, :], Q[o:o + 64, j % 2, c, :], K[o:o + 64, (j // 2) % 2, :],
                                         start=True, stop=True)
                    last.then_inc(s["s_mm"], 1)
                if back(2):
                    k2, j2, b2 = back(2)
                    pe.wait_ge(s["pT_act"], k2 + 1)
                    pe.wait_ge(s["pT_dve"], k2 + 1)
                    wait(pe, s["aT_sb"], k2)
                    for h in range(W):
                        for tt in range(TPB):
                            last = pe.matmul(O[:, h, :], pT[:, j2 % 2, tt, h, :],
                                             V[:, b2 * TPB + tt, j2 // 2, :], start=(tt == 0), stop=(tt == 1))
                    last.then_inc(s["o_mm"], 1)
                if back(1):
                    k1, j1, b1 = back(1)
                    pe.wait_ge(s["p_ready"], k1 + 1)
                    wait(pe, s["pT_act"], k1)
                    wait(pe, s["pT_dve"], k1)
                    for tt in range(TPB):
                        for h in range(W):
                            last = pe.transpose(T[:, tt, h, :], pr[:, j1 % 2, h, tt * P:(tt + 1) * P], ident[:])
                    last.then_inc(s["t_mm"], 1)
                if back(2):
                    k2, j2, b2 = back(2)
                    pe.wait_ge(s["a_ready"], k2 + 1)
                    for c in range(2):
                        last = pe.transpose(ATp[:, c, :], At[:, j2 % 2, c * P:(c + 1) * P], ident[:])
                    last.then_inc(s["aT_mm"], 1)

            project(0, 0, 0)
            steps(pe, emit, 2)

        @block.scalar
        def _(a):
            def emit(back, here):
                if back(0):
                    k, j, b = back(0)
                    a.wait_ge(s["max_ready"], k + 1)
                    wait(a, s["t_mm"], k - 1)
                    wait(a, s["r_ready"], k - 1)
                    for h in range(W):
                        i = 2 * (h % 2) + h // 2
                        last = a.activation(pr[:, j % 2, h, :], S[:, j % 2, i, :], ACT.Exp,
                                            bias=nm[:, j % 2, i:i + 1], accum_out=den[:, j % 2, h:h + 1])
                    last.then_inc(s["p_ready"], 1)
                if back(1):
                    k1, j1, b1 = back(1)
                    a.wait_ge(s["t_mm"], k1 + 1)
                    wait(a, s["o_mm"], k1 - 1)
                    a.copy(pT[:, j1 % 2, 0, :, :], T[:, 0, :, :]).then_inc(s["pT_act"], 1)
            steps(a, emit, 1)

        @block.vector
        def _(v):
            def copies(k, j, b):
                wait(v, s["s_mm"], k - 1)
                v.wait_ge(s["qk_mm"], k + 1)
                v.tensor_copy(Q[:, j % 2, :, :], Qp).then_inc(s["q_sb"], 1)
                if j % 2 == 0:
                    wait(v, s["s_mm"], k - 2)
                    v.tensor_scalar(K[:, (j // 2) % 2, :], Kp, E ** -0.5, None, ALU.mult).then_inc(s["k_sb"], 1)

            def emit(back, here):
                if back(0):
                    k, j, b = back(0)
                    v.wait_ge(s["s_mm"], k + 1)
                    wait(v, s["p_ready"], k - 1)
                    v.tensor_reduce(nm[:, j % 2, :], S[:, j % 2, :, :], AX.X, ALU.max,
                                    negate=True).then_inc(s["max_ready"], 1)
                    if j + 1 < STEPS:
                        copies(k + 1, j + 1, b)
                    elif not (isinstance(b, int) and b == NB - 1):
                        copies(k + 1, 0, b + 1)
                if back(2):
                    k2, j2, b2 = back(2)
                    v.wait_ge(s["p_ready"], k2 + 1)
                    wait(v, s["a_ready"], k2)
                    v.reciprocal(rden[:], den[:, j2 % 2, :]).then_inc(s["r_ready"], 1)
                    v.wait_ge(s["r_ready"], k2 + 1)
                    v.wait_ge(s["o_mm"], k2 + 1)
                    wait(v, s["aT_mm"], k2 - 1)
                    v.tensor_tensor(At[:, j2 % 2, :].rearrange("p (w e) -> p w e", w=W), O,
                                    rden[:].rearrange("p (w o) -> p w o", o=1).broadcast_to([P, W, E]),
                                    ALU.mult).then_inc(s["a_ready"], 1)
                if back(1):
                    k1, j1, b1 = back(1)
                    v.wait_ge(s["t_mm"], k1 + 1)
                    wait(v, s["o_mm"], k1 - 1)
                    v.tensor_copy(pT[:, j1 % 2, 1, :, :], T[:, 1, :, :]).then_inc(s["pT_dve"], 1)
                if back(2):
                    v.wait_ge(s["aT_mm"], k2 + 1)
                    g, st = j2 // 2, j2 % 2
                    v.tensor_copy(AT[:, 2 * g:2 * g + 2, bass.ds(b2 * 256 + st * P, P)], ATp).then_inc(s["aT_sb"], 1)

            copies(0, 0, 0)
            steps(v, emit, 2)

    CH = NT // 4
    PTs = mem.stage_c
    r_all = mem.tokens_a
    n = {k: mem.sem("a2_" + k) for k in "p_mm p_sb pt_mm n_sb r_sb".split()}
    with nc.Block() as block:
        @block.tensor
        def _(pe):
            def body(c):
                for h in range(8):
                    last = pe.matmul(ps[:, 0, :], w["Wpost"][:, h, :], AT[:, h, bass.ds(c * 512, 512)],
                                     start=(h == 0), stop=(h == 7))
                last.then_inc(n["p_mm"], 1)
                pe.wait_ge(n["p_sb"], c + 1)
                wait(pe, n["r_sb"], c * 4)
                for u in range(4):
                    last = pe.transpose(ps[:, 1 + u, 0:P], PTs[:, u * P:(u + 1) * P], ident[:])
                last.then_inc(n["pt_mm"], 1)
            rolled(pe, CH, body)

        @block.scalar
        def _(a):
            def body(c):
                a.wait_ge(n["p_mm"], c + 1)
                wait(a, n["pt_mm"], c)
                a.copy(PTs[:], ps[:, 0, :]).then_inc(n["p_sb"], 1)
            rolled(a, CH, body)

        @block.vector
        def _(v):
            def body(c):
                for u in range(4):
                    t = c * 4 + u
                    v.tensor_scalar(r_all[:, t, :], x_all[:, t, :], mem.mv[:, bass.ds(t, 1), 0], rstd[:, bass.ds(t, 1)],
                                    ALU.subtract, ALU.mult).then_inc(n["n_sb"], 1)
                v.wait_ge(n["pt_mm"], c + 1)
                v.wait_ge(n["n_sb"], c * 4 + 4)
                for u in range(4):
                    t = c * 4 + u
                    v.tensor_tensor(r_all[:, t, :], r_all[:, t, :], ps[:, 1 + u, 0:P], ALU.add).then_inc(n["r_sb"], 1)
            rolled(v, CH, body)
            v.wait_ge(n["r_sb"], NT)

    add_layer_norm(nc, mem, "a3", r_all, x_all)


def add_layer_norm(nc, mem, name, r_all, x_all):
    rstd_ready, norm_step, x_step = mem.sem(name + "_rstd"), mem.sem(name + "_norm"), mem.sem(name + "_x")
    mem.var_ready = mem.sem(name + "_var")

    def add(eng, q):
        eng.wait_ge(norm_step, 4 * q + 4)
        part = slice(4 * q, 4 * q + 4)
        return eng.tensor_tensor(x_all[:, part, :], x_all[:, part, :], r_all[:, part, :], ALU.add).then_inc(x_step, 1)

    with nc.Block() as block:
        @block.vector
        def _(v):
            layer_norm_stats(v, mem, name, lambda t: r_all[:, t, :])
            for t in range(16):
                v.wait_ge(rstd_ready, t // 8 + 1)
                v.tensor_scalar(r_all[:, t, :], r_all[:, t, :], mem.mv[:, t, 0:1], mem.rstd[:, t:t + 1],
                                ALU.subtract, ALU.mult).then_inc(norm_step, 1)
            for q in (2, 3):
                add(v, q)
            v.wait_ge(x_step, 4)

        @block.gpsimd
        def _(g):
            layer_norm_power(g, mem, rstd_ready)
            for q in (0, 1):
                add(g, q)
            g.wait_ge(x_step, 4)


def normalised_transposes(nc, mem, name, x_all, nT, parts, width, products, weights_in, weights_n, pre=None,
                          add_to=None):
    GROUPS = 4
    ps, ident = mem.ps, mem.ident
    mem.var_ready = mem.sem(name + "_var_ready")
    rstd_ready = mem.sem(name + "_rstd_ready")
    n_ready, nT_mm, nT_sb, high_sb, low_sb, l_mm, sum_sb = (
        mem.sem(name + "_" + s) for s in ("n_ready", "nT_mm", "nT_sb", "high_sb", "low_sb", "l_mm", "sum_sb"))
    ntile = mem.stage_a
    results = ps[:, 2:6, :].rearrange("p b t -> p (b t)")

    def group(g):
        return slice(g * 512, (g + 1) * 512)

    with nc.Block() as block:
        @block.vector
        def _(v):
            layer_norm_stats(v, mem, name, lambda t: x_all[:, t, :])

            def low(g):
                v.wait_ge(nT_sb, g + 1)
                v.wait_ge(high_sb, g + 1)
                v.tensor_tensor(parts[1][:, group(g)], nT[:, group(g)], parts[0][:, group(g)].bitcast(F32),
                                ALU.subtract).then_inc(low_sb, 1)

            for g in range(GROUPS):
                v.wait_ge(rstd_ready, g // 2 + 1)
                wait(v, nT_mm, g - 1)
                for u in range(4):
                    t = 4 * g + u
                    v.tensor_scalar(ntile[:, g % 2, u, :], x_all[:, t, :], mem.mv[:, t, 0:1], mem.rstd[:, t:t + 1],
                                    ALU.subtract, ALU.mult).then_inc(n_ready, 1)
                if parts and g:
                    low(g - 1)
            if parts:
                low(GROUPS - 1)
                v.wait_ge(low_sb, GROUPS)
            if add_to is not None:
                for g in range(GROUPS):
                    v.wait_ge(l_mm, g + 1)
                    tiles = add_to[:, 4 * g:4 * g + 4, :].rearrange("p t d -> p (t d)")
                    v.tensor_tensor(tiles, tiles, results[:, group(g)], ALU.add).then_inc(sum_sb, 1)
                v.wait_ge(sum_sb, GROUPS)

        @block.gpsimd
        def _(g):
            layer_norm_power(g, mem, rstd_ready)

        @block.tensor
        def _(pe):
            pe.wait_ge(weights_in, weights_n)

            def product(g):
                pe.wait_ge(nT_sb, g + 1)
                for t in range(4 * g, 4 * g + 4):
                    for j, (still, moving) in enumerate(products):
                        last = pe.matmul(results[:, t * width:(t + 1) * width],
                                         nT[:, t * P:(t + 1) * P] if still is None else still,
                                         moving, start=(j == 0), stop=(j == len(products) - 1))
                last.then_inc(l_mm, 1)

            for g in range(GROUPS):
                pe.wait_ge(n_ready, 4 * g + 4)
                wait(pe, nT_sb, g - 1)
                if parts:
                    wait(pe, high_sb, g - 1)
                for u in range(4):
                    last = pe.transpose(ps[:, g % 2, u * P:(u + 1) * P], ntile[:, g % 2, u, :], ident[:])
                last.then_inc(nT_mm, 1)
                if g:
                    product(g - 1)
            product(GROUPS - 1)

        @block.scalar
        def _(a):
            def copied(dst, g, done):
                if pre is None:
                    a.copy(dst, ps[:, g % 2, :]).then_inc(done, 1)
                else:
                    a.activation(dst, ps[:, g % 2, :], ACT.Identity, bias=pre[1], scale=pre[0]).then_inc(done, 1)

            for g in range(GROUPS):
                a.wait_ge(nT_mm, g + 1)
                copied(nT[:, group(g)], g, nT_sb)
                if parts:
                    copied(parts[0][:, group(g)], g, high_sb)


def route(nc, mem, name, experts, top, normalised, bias, b2, acc):
    NT = 16
    ps, ident = mem.ps, mem.ident
    N = NT * experts

    def tile3(x):
        return x[:, 0:N].rearrange("p (t e) -> p t e", e=experts)

    def over_experts(x):
        return x.rearrange("p (t o) -> p t o", o=1).broadcast_to([P, NT, experts])

    L, above, equal, seen, gates = (tile3(x) for x in (mem.r_logits, mem.r_above, mem.r_equal, mem.r_seen, mem.gates))
    best = mem.best
    small = mem.r_small
    centred, exp_ready, gates_ready = (mem.sem(name + "_" + s) for s in ("centred", "exp_ready", "gates_ready"))
    cT_mm, cT_sb, b_mm, acc_ready = (mem.sem(name + "_" + s) for s in ("cT_mm", "cT_sb", "b_mm", "acc_ready"))
    best_ready = mem.sem(name + "_best")
    cT = mem.gatesT
    with nc.Block() as block:
        @block.vector
        def _(v):
            link = chain(v, mem.sem(name + "_route_step"))
            flat = mem.r_logits[:, 0:N]
            if bias is not None:
                link(v.tensor_tensor(L, tile3(ps[:, 2, :]), bias.rearrange("p (o e) -> p o e", o=1).broadcast_to(
                    [P, NT, experts]), ALU.add))
            else:
                link(v.tensor_copy(flat, ps[:, 2, 0:N]))
            for t in range(NT):
                v.max(best[:, t, :], L[:, t, :]).then_inc(best_ready, 1)
            v.wait_ge(best_ready, NT)
            link(v.tensor_tensor(tile3(mem.r_exp), L, best[:, :, 0:1].broadcast_to([P, NT, experts]), ALU.subtract))
            v.sem_inc(centred, 1)
            kth = best[:, :, top - 1:top].broadcast_to([P, NT, experts])
            link(v.tensor_tensor(above, L, kth, ALU.is_gt))
            link(v.tensor_tensor(equal, L, kth, ALU.is_equal))
            link(v.tensor_reduce(small[:, 0, :], above, AX.X, ALU.add))
            link(v.tensor_scalar(small[:, 1, :], small[:, 0, :], -1.0, float(top), ALU.mult, ALU.add))
            link(v.tensor_tensor_scan(mem.r_seen[:, 0:N], mem.keep[experts][:, 0:N], mem.r_equal[:, 0:N], 0.0,
                                      ALU.mult, ALU.add))
            link(v.tensor_tensor(seen, seen, over_experts(small[:, 1, :]), ALU.is_le))
            link(v.tensor_tensor(seen, seen, equal, ALU.mult))
            link(v.tensor_tensor(seen, seen, above, ALU.add))
            v.wait_ge(exp_ready, 1)
            ex = tile3(mem.r_exp)
            link(v.tensor_tensor(gates, ex, seen, ALU.mult))
            link(v.tensor_reduce(small[:, 2, :], gates if normalised else ex, AX.X, ALU.add))
            link(v.reciprocal(small[:, 3, :], small[:, 2, :]))
            v.tensor_tensor(gates, gates, over_experts(small[:, 3, :]), ALU.mult).then_inc(gates_ready, 1)

        @block.scalar
        def _(a):
            a.wait_ge(centred, 1)
            a.activation(mem.r_exp[:, 0:N], mem.r_exp[:, 0:N], ACT.Exp).then_inc(exp_ready, 1)
            for q in range(4):
                a.wait_ge(cT_mm, q + 1)
                a.copy(cT[0:experts, q * 512:(q + 1) * 512], ps[0:experts, 3 + q % 2, :]).then_inc(cT_sb, 1)
            for q in range(4):
                a.wait_ge(b_mm, q + 1)
                a.copy(acc[:, 4 * q:4 * q + 4, :].rearrange("p t d -> p (t d)"), ps[:, 5 + q % 2, :]).then_inc(acc_ready, 1)

        @block.tensor
        def _(pe):
            pe.wait_ge(gates_ready, 1)
            for q in range(4):
                wait(pe, cT_sb, q - 1)
                for u in range(4):
                    last = pe.transpose(ps[0:experts, 3 + q % 2, u * P:(u + 1) * P], gates[:, 4 * q + u, :], ident[:])
                last.then_inc(cT_mm, 1)
            for q in range(4):
                pe.wait_ge(cT_sb, q + 1)
                wait(pe, acc_ready, q - 1)
                for u in range(4):
                    t = 4 * q + u
                    last = pe.matmul(ps[:, 5 + q % 2, u * P:(u + 1) * P], cT[0:experts, t * P:(t + 1) * P], b2,
                                     start=True, stop=True)
                last.then_inc(b_mm, 1)


def mixture(nc, mem, name, parts, acc, w1, w2, b1T, gate_of, func):
    ROUNDS, CH, HALF = 8, 4, 2
    xh, xl = parts
    W1h, W1l = mem.W1h, mem.W1l
    ps = mem.ps
    W1, W2, Hs = mem.W1, mem.W2, mem.hidden
    H = ps[:, 0:4, :].rearrange("p (s h) t -> p s h t", s=2)
    Y = ps[:, 4:6, :]
    w_in = [mem.sem(f"{name}_w_in{u}") for u in range(2)]
    h_mm, h_sb, y_mm, acc_done = (mem.sem(name + "_" + s) for s in ("h_mm", "h_sb", "y_mm", "acc_done"))
    w_split = mem.sem(name + "_w_split")
    bias, bias_ready = mem.bias, mem.sem(name + "_bias_ready")
    with nc.Block() as block:
        def steps(eng, emit):
            def body(i):
                for u in range(2):
                    for c in range(CH):
                        k = i * (2 * CH) + (u * CH + c)
                        if u == 0 and c == 0:
                            back = None if isinstance(i, int) and i == 0 else (k - 1, i - 1, 1, CH - 1)
                        else:
                            back = (k - 1, i, u if c else u - 1, c - 1 if c else CH - 1)
                        emit((k, i, u, c), back)
            body(0)
            with eng.Fori(1, ROUNDS - 1) as i:
                body(i)
            body(ROUNDS - 1)
            emit(None, (ROUNDS * 2 * CH - 1, ROUNDS - 1, 1, CH - 1))

        @block.sync
        def _(sp):
            def body(i):
                for u in range(2):
                    wait(sp, y_mm, (i - 1) * (2 * CH) + (u + 1) * CH)
                    sp.dma_start(W1[:, u, :], w1[i, u, :, :] if isinstance(i, int) else w1[bass.ds(i, 1), u, :, :].rearrange("a p f -> p (a f)")).then_inc(w_in[u], 16)
                    w2v = w2[i, u, :, :].rearrange("(h p) d -> p h d", p=P) if isinstance(i, int) else \
                        w2[bass.ds(i, 1), u, :, :].rearrange("a (h p) d -> p (a h) d", p=P)
                    sp.dma_start(W2[:, u, :, :], w2v).then_inc(w_in[u], 16)
            rolled(sp, ROUNDS, body)

        @block.tensor
        def _(pe):
            def emit(now, back):
                if now:
                    k, i, u, c = now
                    if c == 0:
                        pe.wait_ge(w_split, i * 4 + (u * 2 + 2))
                    wait(pe, h_sb, k - 1)
                    for h in range(HALF):
                        half, chunk = slice(h * P, (h + 1) * P), slice(c * 512, (c + 1) * 512)
                        pe.matmul(H[:, c % 2, h, :], W1h[:, u, half], xh[:, chunk], start=True, stop=False)
                        pe.matmul(H[:, c % 2, h, :], W1l[:, u, half], xh[:, chunk], start=False, stop=False)
                        last = pe.matmul(H[:, c % 2, h, :], W1h[:, u, half], xl[:, chunk], start=False, stop=True)
                    last.then_inc(h_mm, 1)
                if back:
                    k, i, u, c = back
                    pe.wait_ge(h_sb, k + 1)
                    wait(pe, acc_done, k - 1)
                    for t in range(4):
                        for h in range(HALF):
                            last = pe.matmul(Y[:, c % 2, t * P:(t + 1) * P], Hs[:, c % 2, h, t * P:(t + 1) * P],
                                             W2[:, u, h, :], start=(h == 0), stop=(h == HALF - 1))
                    last.then_inc(y_mm, 1)
            steps(pe, emit)

        @block.scalar
        def _(a):
            def emit(now, back):
                if now:
                    k, i, u, c = now
                    a.wait_ge(h_mm, k + 1)
                    wait(a, y_mm, k - 1)
                    a.wait_ge(bias_ready, i * 2 + (u + 1))
                    for h in range(HALF):
                        last = a.activation(Hs[:, c % 2, h, :], H[:, c % 2, h, :], func,
                                            bias=bias[:, u, h:h + 1])
                    last.then_inc(h_sb, 1)
            steps(a, emit)

        @block.vector
        def _(v):
            def split(i, u):
                v.wait_ge(w_in[u], i * 32 + 32)
                v.tensor_copy(W1h[:, u, :], W1[:, u, :]).then_inc(w_split, 1)
                v.wait_ge(w_split, i * 4 + (u * 2 + 1))
                v.tensor_tensor(W1l[:, u, :], W1[:, u, :], W1h[:, u, :].bitcast(F32), ALU.subtract).then_inc(w_split, 1)

            def copy_bias(i, u):
                v.tensor_copy(bias[:, u, :], b1T[:, bass.ds(i * 4 + u * 2, 2)]).then_inc(bias_ready, 1)

            def emit(now, back):
                if back:
                    k, i, u, c = back
                    v.wait_ge(y_mm, k + 1)
                    wait(v, acc_done, k - 3)
                    for t in range(4):
                        tok = 4 * c + t
                        last = v.scalar_tensor_tensor(out=acc[:, tok, :], in0=Y[:, c % 2, t * P:(t + 1) * P],
                                                      scalar=gate_of(tok, i, u), in1=acc[:, tok, :],
                                                      op0=ALU.mult, op1=ALU.add)
                    last.then_inc(acc_done, 1)
                    if c == 0 and not (isinstance(i, int) and i == ROUNDS - 1 and u == 1):
                        split(i + u, 1 - u)
                    if c == CH - 1:
                        copy_bias(i + 1, u)
            split(0, 0)
            for u in range(2):
                copy_bias(0, u)
            steps(v, emit)


def add_tokens(nc, mem, name, tokens, more):
    done = mem.sem(name + "_done")
    with nc.Block() as block:
        @block.vector
        def _(v):
            for q in range(4):
                part = slice(4 * q, 4 * q + 4)
                v.tensor_tensor(tokens[:, part, :], tokens[:, part, :], more[:, part, :], ALU.add).then_inc(done, 1)
            v.wait_ge(done, 4)


LOG1P = (0.9999999954, -0.4999990399, 0.3333000404, -0.2495455887, 0.1967811726, -0.153118631,
         0.1061426468, -0.05706420072, 0.0199071609, -0.003256378468)

C_DTB, C_A, C_DP, C_CW, C_CB, C_LNW, C_LNB = 0, 4, 8, 12, 24, 27, 28
C_ALL = 32


class Steps:

    def __init__(self, eng, sem, per):
        self.eng, self.sem, self.per = eng, sem, per

    def at(self, turn):
        self.turn, self.j = turn, 0

    def link(self, ins):
        self.mark(ins)
        self.join()

    def mark(self, ins):
        self.j += 1
        assert self.j <= self.per
        ins.then_inc(self.sem, 1)

    def join(self):
        self.eng.wait_ge(self.sem, self.turn * self.per + self.j)

    def end(self):
        assert self.j == self.per, (self.j, self.per)


def mamba_constants(nc, mem, t, cols, at):
    L = 4
    tab, in_all, out_all = mem.layers, mem.in_all, mem.out_all
    zeroed, loaded, step, mask_step = (mem.sem("mc_" + s) for s in ("zeroed", "loaded", "step", "mask_step"))
    exp_ready, masks = mem.sem("mc_exp"), mem.sem("mc_masks")
    raw = mem.layer_rows
    with nc.Block() as block:
        @block.sync
        def _(sp):
            for i, name in enumerate(("dt_bias", "A_log", "Dp")):
                sp.dma_start(raw[:, i, :, :], t["L1_attn_" + name].rearrange("(o l) h -> o l h", o=1).broadcast_to(
                    [P, L, 4])).then_inc(loaded, 16)
            sp.dma_start(in_all[:], t["L1_attn_in_w"].rearrange("l d e -> d l e")).then_inc(loaded, 16)
            sp.dma_start(out_all[:], t["L1_attn_out_w"].rearrange("l (c p) d -> p (l c) d", p=P)).then_inc(loaded, 16)
            sp.wait_ge(loaded, 5 * 16)

        @block.scalar
        def _(a):
            a.wait_ge(loaded, 5 * 16)
            a.activation(raw[:, 1, :, :], raw[:, 1, :, :], ACT.Exp).then_inc(exp_ready, 1)

        @block.gpsimd
        def _(g):
            for m in (mem.upto, mem.after):
                g.memset(m[:], 1.0).then_inc(mask_step, 1)
            g.memset(mem.eps4[:], 4 * EPS).then_inc(mask_step, 1)
            g.wait_ge(mask_step, 3)
            g.affine_select(out=mem.upto[:], in_=mem.upto[:], pattern=[[1, P]], compare_op=ALU.is_ge, fill=0.0,
                            base=0, channel_multiplier=-1).then_inc(masks, 1)
            g.affine_select(out=mem.after[:], in_=mem.after[:], pattern=[[-1, P]], compare_op=ALU.is_gt, fill=0.0,
                            base=0, channel_multiplier=1).then_inc(masks, 1)
            g.wait_ge(masks, 2)

        @block.vector
        def _(v):
            link = chain(v, step)
            v.wait_ge(mem.vec_sb, 2)
            link(v.memset(tab[:], 0.0))
            link(v.memset(mem.xp[:], 0.0))
            link(v.tensor_scalar(tab[:, :, C_CW:C_CW + 12], at["conv_w"].rearrange("p (l k) -> p l k", l=L), 0.5, None, ALU.mult))
            link(v.tensor_scalar(tab[:, :, C_CB:C_CB + 3], at["conv_b"].rearrange("p (l k) -> p l k", l=L), 0.5, None, ALU.mult))
            link(v.tensor_copy(tab[:, :, C_LNW], at["ln_w"]))
            link(v.tensor_copy(tab[:, :, C_LNB], at["ln_b"]))
            v.wait_ge(loaded, 5 * 16)
            link(v.tensor_copy(tab[:, :, C_DTB:C_DTB + 4], raw[:, 0, :, :]))
            link(v.tensor_copy(tab[:, :, C_DP:C_DP + 4], raw[:, 2, :, :]))
            v.wait_ge(exp_ready, 1)
            link(v.tensor_scalar(tab[:, :, C_A:C_A + 4], raw[:, 1, :, :], -1.0, None, ALU.mult))
            for c in range(2 * L):
                link(v.tensor_scalar(out_all[:, c, :], out_all[:, c, :], at["norm_w"][:, c:c + 1], None, ALU.mult))


def mamba(nc, mem, xm):
    UNITS, Q = 16, 4
    IN = 644
    ps, ident = mem.ps, mem.ident
    xnp, dtp = ps[:, 0, :], ps[:, 0, 0:4 * Q]
    Xp = [ps[:, 1, :], ps[:, 2, :], ps[:, 1, :]]
    Zp = [ps[:, 0, :], ps[:, 2, :]]
    Dps = ps[:, 3, :].rearrange("p (h t) -> p h t", h=4)
    Gp = ps[:, 4, 0:P]
    xBp, cump, outp = ps[:, 5, 0:320], ps[:, 5, 320:328], ps[:, 5, 384:384 + P]
    Yp, Ip = ps[:, 6, 0:256], ps[:, 6, 256:512]
    Sp, yTp = ps[0:64, 7, 0:256], ps[:, 7, 256:512]
    tab, in_all, out_all = mem.layers, mem.in_all, mem.out_all
    m = mem.m
    s = {n: mem.sem("m_" + n) for n in (
        "lc_ready dp_ready wx_ready stat_step var_ready rstd_ready xn_ready xnT_mm xnT_sb x_mm x_sb dt_mm dt_step ax_ready "
        "u_ready a_ready z_mm zt_ready g_ready conv_step conv_ready th_ready silu_ready am_ready d_mm g_mm xb_mm "
        "e_ready ec_ready xb_sb gm_ready m_ready dtx_ready dtxw_ready y0_ready y_mm s_sb y1_step y1_ready y2_ready "
        "sq_ready rs_step rs_ready yT_mm yT_sb out_mm x_done").split()}

    def heads(x, n=64):
        return x.rearrange("p (h n) -> p h n", h=4)

    def over(x, n):
        return x.rearrange("p (h o) -> p h o", o=1).broadcast_to([P, 4, n])

    def schedule(eng, norm, front, tile, late):
        for piece in range(Q):
            norm(0, 0, 0, piece)
        for piece in range(Q):
            front(0, 0, 0, piece)
            norm(1, 0, 1, piece)

        def body(i):
            last = isinstance(i, int) and i == UNITS // 2 - 1
            for u in range(2):
                for q in range(Q):
                    def back(l, u=u, q=q):
                        j = u * Q + q - l
                        if j >= 0:
                            return i * 2 * Q + j, j % Q, j // Q, i * 2 + j // Q, i
                        if isinstance(i, int) and i == 0:
                            return None
                        j += 2 * Q
                        return (i - 1) * 2 * Q + j, j % Q, j // Q, (i - 1) * 2 + j // Q, i - 1
                    tile(back)
                    if u == 0:
                        front(i * 2 + 1, i, 1, q)
                        if not last:
                            norm(i * 2 + 2, i + 1, 0, q)
                    elif not last:
                        front(i * 2 + 2, i + 1, 0, q)
                        norm(i * 2 + 3, i + 1, 1, q)
                    late(back)
        body(0)
        with eng.Fori(1, UNITS // 2 - 1) as i:
            body(i)
        body(UNITS // 2 - 1)
        for l0 in range(2):
            def back(l, l0=l0):
                if l <= l0:
                    return None
                k = UNITS * Q + l0 - l
                return k, k % Q, (k // Q) % 2, k // Q, UNITS // 2 - 1
            tile(back)
            late(back)

    with nc.Block() as block:
        @block.tensor
        def _(pe):
            def norm(M, i, u, piece):
                if piece == 3:
                    pe.wait_ge(s["xn_ready"], M * Q + Q)
                    wait(pe, s["g_ready"], M * 2 - 1)
                    for q in range(Q):
                        last = pe.transpose(xnp[:, q * P:(q + 1) * P], m.xn[:, q, :], ident[:])
                    last.then_inc(s["xnT_mm"], 1)

            def front(M, i, u, piece):
                l = i // 2
                if piece == 0:
                    pe.wait_ge(s["xnT_sb"], M + 1)
                    pe.wait_ge(s["wx_ready"], M + 1)
                    wait(pe, s["g_ready"], M * 2)
                    wait(pe, s["x_sb"], M * 3)
                    for c in range(2):
                        pe.matmul(Xp[c], m.Wx[:, u, c * P:(c + 1) * P], m.xnT[:, u, :], start=True,
                                  stop=True).then_inc(s["x_mm"], 1)
                    for q in range(Q):
                        last = pe.matmul(dtp[:, 4 * q:4 * q + 4], m.xnT[:, u, q * P:(q + 1) * P],
                                         in_all[:, l, 640:644], start=True, stop=True)
                    last.then_inc(s["dt_mm"], 1)
                if piece == 1:
                    pe.wait_ge(s["x_sb"], M * 3 + 1)
                    pe.matmul(Xp[2], m.Wx[:, u, 2 * P:3 * P], m.xnT[:, u, :], start=True, stop=True).then_inc(s["x_mm"], 1)
                if piece == 2:
                    pe.wait_ge(s["dt_step"], M + 1)
                    pe.wait_ge(s["x_sb"], M * 3 + 2)
                    for half in range(2):
                        for q in (2 * half, 2 * half + 1):
                            last = pe.matmul(Zp[half][:, (q % 2) * 256:(q % 2) * 256 + 256],
                                             m.xnT[:, u, q * P:(q + 1) * P], in_all[:, l, 0:256], start=True, stop=True)
                        last.then_inc(s["z_mm"], 1)

            def tile(back):
                if back(2):
                    k, q, u, M, i = back(2)
                    pe.wait_ge(s["y2_ready"], k + 1)
                    pe.wait_ge(s["s_sb"], M * 2 + (q // 2 + 1))
                    for c in range(2):
                        last = pe.transpose(yTp[:, c * P:(c + 1) * P], m.y2[:, q % 2, c * P:(c + 1) * P], ident[:])
                    last.then_inc(s["yT_mm"], 1)
                if back(1):
                    k, q, u, M, i = back(1)
                    pe.wait_ge(s["m_ready"], k + 1)
                    pe.wait_ge(s["dtx_ready"], k + 1)
                    wait(pe, s["y1_ready"], k)
                    for h in range(4):
                        pe.matmul(Yp[:, h * 64:(h + 1) * 64], m.M[:, q % 2, h, :],
                                  m.dtx[:, q % 2, h * 64:(h + 1) * 64], start=True, stop=True)
                    if q % 2 == 1:
                        pe.wait_ge(s["s_sb"], (M * 2) + (q // 2 + 1))
                        pe.matmul(Ip, m.CT[0:64, u, q * P:(q + 1) * P], m.state[:], start=True,
                                  stop=True).then_inc(s["y_mm"], 1)
                if back(0):
                    k, q, u, M, i = back(0)
                    tok = slice(q * P, (q + 1) * P)
                    pe.wait_ge(s["am_ready"], k + 1)
                    wait(pe, s["e_ready"], k)
                    for h in range(4):
                        last = pe.matmul(Dps[:, h, :], m.am[:, q % 2, h, :], mem.upto[:], start=True, stop=True)
                    last.then_inc(s["d_mm"], 1)
                if back(1):
                    k, q, u, M, i = back(1)
                    if q % 2 == 0:
                        pe.wait_ge(s["dtxw_ready"], (M * 2) + (q // 2 + 1))
                        wait(pe, s["yT_sb"], k)
                        pe.matmul(Sp, m.xB[:, q % 2, 256:320], m.dtxw[:], start=True, stop=True).then_inc(s["y_mm"], 1)
                if back(0):
                    k, q, u, M, i = back(0)
                    tok = slice(q * P, (q + 1) * P)
                    pe.wait_ge(s["silu_ready"], M * 4 + 4)
                    wait(pe, s["gm_ready"], k)
                    pe.matmul(Gp, m.xs[0:64, u, 2, tok], m.CT[0:64, u, tok], start=True, stop=True).then_inc(s["g_mm"], 1)
                    wait(pe, s["xb_sb"], k)
                    wait(pe, s["x_done"], k - 2)
                    for c in range(2):
                        pe.transpose(xBp[:, c * P:(c + 1) * P], m.xs[:, u, c, tok], ident[:])
                    pe.transpose(xBp[:, 256:320], m.xs[0:64, u, 2, tok], ident[0:64, 0:64])
                    pe.matmul(cump[:, 0:4], mem.upto[:], m.a[:, u, q, :], start=True, stop=True)
                    pe.matmul(cump[:, 4:8], mem.after[:], m.a[:, u, q, :], start=True, stop=True).then_inc(s["xb_mm"], 1)

            def late(back):
                if back(2):
                    k, q, u, M, i = back(2)
                    l = i // 2
                    pe.wait_ge(s["yT_sb"], k + 1)
                    if not back(0):
                        pe.wait_ge(s["x_done"], k)
                    pe.wait_ge(s["xb_sb"], k + 3 if back(0) else UNITS * Q)
                    for c in range(2):
                        last = pe.matmul(outp, m.yT[:, q % 2, c, :],
                                         out_all[:, l * 2 + c, :],
                                         start=(c == 0), stop=(c == 1))
                    last.then_inc(s["out_mm"], 1)
            schedule(pe, norm, front, tile, late)

        @block.scalar
        def _(a):
            def norm(M, i, u, piece):
                if piece == 3:
                    lc = m.lc[:, u, :]
                    a.wait_ge(s["xnT_mm"], M + 1)
                    a.wait_ge(s["lc_ready"], M + 1)
                    a.activation(m.xnT[:, u, :], xnp, ACT.Identity, bias=lc[:, C_LNB:C_LNB + 1],
                                 scale=lc[:, C_LNW:C_LNW + 1]).then_inc(s["xnT_sb"], 1)

            def front(M, i, u, piece):
                lc = m.lc[:, u, :]

                def evacuate(c):
                    a.wait_ge(s["x_mm"], M * 3 + (c + 1))
                    if c == 0:
                        wait(a, s["silu_ready"], M * 4)
                    src = Xp[c]
                    a.activation(m.xc[:, c, :], src, ACT.Identity, bias=lc[:, C_CB + c:C_CB + c + 1],
                                 scale=lc[:, C_CW + 9 + c:C_CW + 10 + c])
                    a.copy(mem.xp[:, c, :, 3:259], src.rearrange("p (b t) -> p b t", b=2)).then_inc(s["x_sb"], 1)

                def tanh(c):
                    a.wait_ge(s["conv_ready"], M * 3 + (c + 1))
                    a.activation(m.th[:, c, :], m.xc[:, c, :], ACT.Tanh).then_inc(s["th_ready"], 1)

                def tanh_z(half):
                    a.wait_ge(s["z_mm"], M * 2 + (half + 1))
                    wait(a, s["g_ready"], M * 2 + half)
                    a.activation(m.zt[:], Zp[half], ACT.Tanh, scale=0.5).then_inc(s["zt_ready"], 1)

                if piece == 0:
                    evacuate(0)
                if piece == 1:
                    evacuate(1)
                    a.wait_ge(s["ax_ready"], M + 1)
                    a.activation(m.eu[:], m.ax[:], ACT.Exp, scale=-1.0).then_inc(s["u_ready"], 1)
                if piece == 2:
                    evacuate(2)
                    tanh(0)
                    tanh_z(0)
                if piece == 3:
                    tanh(1)
                    tanh_z(1)
                    tanh(2)

            def tile(back):
                if back(2):
                    k, q, u, M, i = back(2)
                    a.wait_ge(s["yT_mm"], k + 1)
                    wait(a, s["out_mm"], k - 1)
                    a.copy(m.yT[:, q % 2, :, :].rearrange("p c t -> p (c t)"), yTp).then_inc(s["yT_sb"], 1)
                if back(0):
                    k, q, u, M, i = back(0)
                    a.wait_ge(s["d_mm"], k + 1)
                    wait(a, s["m_ready"], k - 1)
                    a.activation(m.E[:, q % 2, :], ps[:, 3, :], ACT.Exp).then_inc(s["e_ready"], 1)
                if back(1):
                    k, q, u, M, i = back(1)
                    if q % 2 == 0:
                        a.wait_ge(s["y_mm"], k + 1)
                        a.copy(m.state[:], Sp).then_inc(s["s_sb"], 1)
                if back(0):
                    k, q, u, M, i = back(0)
                    a.wait_ge(s["xb_mm"], k + 1)
                    wait(a, s["y1_ready"], k - 1)
                    a.activation(m.ec[:, q % 2, :], cump, ACT.Exp).then_inc(s["ec_ready"], 1)
                    wait(a, s["y_mm"], k - 1)
                    wait(a, s["y0_ready"], k - 1)
                    a.copy(m.xB[:, q % 2, :], xBp).then_inc(s["xb_sb"], 1)
                if back(2):
                    k, q, u, M, i = back(2)
                    wait(a, s["rs_ready"], k - 1)
                    a.activation(m.junk[:, q % 2, :], m.y2[:, q % 2, :], ACT.Square, scale=1.0 / 16,
                                 accum_out=m.ssq[:, q % 2, :]).then_inc(s["sq_ready"], 1)
            schedule(a, norm, front, tile, lambda back: None)

        @block.vector
        def _(v):
            st = Steps(v, s["stat_step"], 8)
            cs = Steps(v, s["conv_step"], 6)
            dt = Steps(v, mem.sem("m_dt_chain"), 11)
            ys = Steps(v, s["y1_step"], 2)

            def norm(M, i, u, piece):
                l, base = i // 2, (i % 2) * 8 + u * 4
                if piece == 0:
                    st.at(M)
                    wait(v, s["x_done"], M * Q - 12)
                    wait(v, s["a_ready"], M - 1)
                    v.tensor_scalar(m.lc[:, u, :], tab[:, l, :], 1.0, None, ALU.mult).then_inc(s["lc_ready"], 1)
                    for q in range(Q):
                        st.mark(v.bn_stats(m.stats[:, q, :], xm[:, base + q, :]))
                    st.join()
                    wait(v, s["x_mm"], M * 3 - 3)
                    v.tensor_scalar(m.Wx[:, u, :], in_all[:, l, 256:640], 1.0, None, ALU.mult).then_inc(s["wx_ready"], 1)
                    for q in range(Q):
                        st.mark(v.bn_aggr(m.mv[:, q, :], m.stats[:, q, :]))
                    st.join()
                    v.tensor_scalar(m.veps[:], m.mv[:, :, 1], EPS, None, ALU.add).then_inc(s["var_ready"], 1)
                    st.end()
                if piece == 1:
                    wait(v, s["xnT_mm"], M)
                    v.wait_ge(s["rstd_ready"], M + 1)
                    for q in range(Q):
                        v.tensor_scalar(m.xn[:, q, :], xm[:, base + q, :], m.mv[:, q, 0:1], m.rstd[:, q:q + 1],
                                        ALU.subtract, ALU.mult).then_inc(s["xn_ready"], 1)

            def front(M, i, u, piece):
                lc = m.lc[:, u, :]
                l = i // 2

                def conv(c):
                    v.wait_ge(s["x_sb"], M * 3 + (c + 1))
                    xc = m.xc[:, c, :].rearrange("p (b t) -> p b t", b=2)
                    for tap in range(3):
                        ins = v.scalar_tensor_tensor(out=xc, in0=mem.xp[:, c, :, tap:tap + 256],
                                                     scalar=lc[:, C_CW + tap * 3 + c:C_CW + tap * 3 + c + 1], in1=xc,
                                                     op0=ALU.mult, op1=ALU.add)
                        if tap < 2:
                            cs.link(ins)
                        else:
                            ins.then_inc(s["conv_ready"], 1)

                def silu(c, rows, out):
                    v.scalar_tensor_tensor(out=out, in0=m.th[rows, c, :], scalar=1.0, in1=m.xc[rows, c, :],
                                           op0=ALU.add, op1=ALU.mult).then_inc(s["silu_ready"], 1)

                def gate(half):
                    v.wait_ge(s["zt_ready"], M * 2 + (half + 1))
                    v.scalar_tensor_tensor(out=m.g[:, u, 2 * half:2 * half + 2, :].rearrange("p q e -> p (q e)"),
                                           in0=m.zt[:], scalar=1.0, in1=Zp[half], op0=ALU.add,
                                           op1=ALU.mult).then_inc(s["g_ready"], 1)

                if piece == 0:
                    wait(v, s["y0_ready"], M * Q - 4)
                    v.tensor_scalar(m.Dp[:, u, :], tab[:, l, C_DP:C_DP + 4], 1.0, None, ALU.mult).then_inc(s["dp_ready"], 1)
                if piece == 1:
                    v.wait_ge(s["dt_mm"], M + 1)
                    v.tensor_tensor(m.x4[:], dtp.rearrange("p (q h) -> p q h", q=Q),
                                    lc[:, C_DTB:C_DTB + 4].rearrange("p (o h) -> p o h", o=1).broadcast_to([P, Q, 4]),
                                    ALU.add).then_inc(s["dt_step"], 1)
                    v.wait_ge(s["dt_step"], M + 1)
                    v.scalar_tensor_tensor(out=m.ax[:], in0=m.x4[:], scalar=-1.0, in1=m.x4[:], op0=ALU.mult,
                                           op1=ALU.max).then_inc(s["ax_ready"], 1)
                    cs.at(M)
                    conv(0)
                    conv(1)
                if piece == 2:
                    dt.at(M)
                    v.wait_ge(s["u_ready"], M + 1)
                    dt.link(v.tensor_scalar(m.poly[:], m.eu[:], LOG1P[9], None, ALU.mult))
                    for c in LOG1P[8::-1]:
                        dt.link(v.scalar_tensor_tensor(out=m.poly[:], in0=m.poly[:], scalar=c, in1=m.eu[:],
                                                       op0=ALU.add, op1=ALU.mult))
                    dt.link(v.scalar_tensor_tensor(out=m.sp[:, u, :, :], in0=m.x4[:], scalar=0.0, in1=m.poly[:],
                                                   op0=ALU.max, op1=ALU.add))
                    dt.end()
                    wait(v, s["am_ready"], M * Q - 4)
                    v.tensor_tensor(m.a[:, u, :, :], m.sp[:, u, :, :],
                                    lc[:, C_A:C_A + 4].rearrange("p (o h) -> p o h", o=1).broadcast_to([P, Q, 4]),
                                    ALU.mult).then_inc(s["a_ready"], 1)
                    conv(2)
                    v.wait_ge(s["th_ready"], M * 3 + 1)
                    wait(v, s["y_mm"], M * Q - 4)
                    silu(0, slice(0, P), m.xs[:, u, 0, :])
                    wait(v, s["y2_ready"], M * Q - 4)
                    gate(0)
                if piece == 3:
                    v.wait_ge(s["th_ready"], M * 3 + 2)
                    silu(1, slice(0, P), m.xs[:, u, 1, :])
                    gate(1)
                    v.wait_ge(s["th_ready"], M * 3 + 3)
                    silu(2, slice(0, 64), m.xs[0:64, u, 2, :])
                    silu(2, slice(64, P), m.CT[0:64, u, :])

            def tile(back):
                if back(1):
                    k, q, u, M, i = back(1)
                    v.wait_ge(s["y_mm"], k + 1)
                    v.wait_ge(s["y0_ready"], k + 1)
                    wait(v, s["y2_ready"], k - 1)
                    y1 = m.y1[:, q % 2, :]
                    if q % 2 == 0:
                        v.tensor_tensor(y1, m.y0[:, q % 2, :], Yp, ALU.add).then_inc(s["y1_ready"], 1)
                    else:
                        ys.at(M * 2 + q // 2)
                        ys.link(v.tensor_tensor(heads(m.yi[:]), heads(Ip), over(m.ec[:, q % 2, 0:4], 64), ALU.mult))
                        ys.link(v.tensor_tensor(m.yi[:], m.yi[:], m.y0[:, q % 2, :], ALU.add))
                        v.tensor_tensor(y1, m.yi[:], Yp, ALU.add).then_inc(s["y1_ready"], 1)
                if back(0):
                    k, q, u, M, i = back(0)
                    v.wait_ge(s["g_mm"], k + 1)
                    v.tensor_tensor(m.Gm[:], Gp, mem.upto[:], ALU.mult).then_inc(s["gm_ready"], 1)
                    v.wait_ge(s["gm_ready"], k + 1)
                    v.wait_ge(s["e_ready"], k + 1)
                    wait(v, s["y_mm"], k - 1)
                    v.tensor_tensor(m.M[:, q % 2, :, :], heads(m.E[:, q % 2, :]),
                                    m.Gm[:].rearrange("p (o t) -> p o t", o=1).broadcast_to([P, 4, P]),
                                    ALU.mult).then_inc(s["m_ready"], 1)

            def late(back):
                if back(2):
                    k, q, u, M, i = back(2)
                    v.wait_ge(s["out_mm"], k + 1)
                    v.wait_ge(s["rs_ready"], k + 1)
                    tok = (i % 2) * 8 + (u * 4 + q)
                    v.scalar_tensor_tensor(out=xm[:, tok, :], in0=outp, scalar=m.rs[:, q % 2, :], in1=xm[:, tok, :],
                                           op0=ALU.mult, op1=ALU.add).then_inc(s["x_done"], 1)
            schedule(v, norm, front, tile, late)
            v.wait_ge(s["x_done"], UNITS * Q)

        @block.gpsimd
        def _(g):
            rs = Steps(g, s["rs_step"], 1)

            def scale_decays(k, q, u, M):
                g.wait_ge(s["a_ready"], M + 1)
                wait(g, s["d_mm"], k - 1)
                g.tensor_tensor(m.am[:, q % 2, :, :], mem.after[:].rearrange("p (o t) -> p o t", o=1).broadcast_to([P, 4, P]),
                                over(m.a[:, u, q, :], P), ALU.mult).then_inc(s["am_ready"], 1)

            def norm(M, i, u, piece):
                if piece == 0:
                    g.wait_ge(s["var_ready"], M + 1)
                    wait(g, s["xn_ready"], M * Q)
                    g.tensor_tensor(m.rstd[:], m.veps[:], mem.neg_half[:, 0:Q], ALU.pow).then_inc(s["rstd_ready"], 1)

            def front(M, i, u, piece):
                if piece == 3:
                    scale_decays(M * Q, 0, u, M)

            def tile(back):
                if back(1):
                    k, q, u, M, i = back(1)
                    g.wait_ge(s["y1_ready"], k + 1)
                    wait(g, s["sq_ready"], k - 1)
                    g.tensor_tensor(m.y2[:, q % 2, :], m.y1[:, q % 2, :], m.g[:, u, q, :], ALU.mult).then_inc(s["y2_ready"], 1)
                if back(0):
                    k, q, u, M, i = back(0)
                    if q < Q - 1:
                        scale_decays(k + 1, q + 1, u, M)
                    g.wait_ge(s["xb_sb"], k + 1)
                    wait(g, s["y_mm"], k - 1)
                    g.tensor_tensor(heads(m.dtx[:, q % 2, :]), heads(m.xB[:, q % 2, 0:256]), over(m.sp[:, u, q, :], 64),
                                    ALU.mult).then_inc(s["dtx_ready"], 1)
                    if q % 2 == 0:
                        g.wait_ge(s["dtx_ready"], k + 1)
                        g.wait_ge(s["ec_ready"], k + 1)
                        wait(g, s["y_mm"], k - 1)
                        g.tensor_tensor(heads(m.dtxw[:]), heads(m.dtx[:, q % 2, :]), over(m.ec[:, q % 2, 4:8], 64),
                                        ALU.mult).then_inc(s["dtxw_ready"], 1)
                if back(2):
                    k, q, u, M, i = back(2)
                    rs.at(k)
                    g.wait_ge(s["sq_ready"], k + 1)
                    wait(g, s["x_done"], k - 1)
                    rs.link(g.tensor_tensor(m.rt[:, q % 2, :], m.ssq[:, q % 2, :], mem.eps4[:, 0:1], ALU.add))
                    g.tensor_tensor(m.rs[:, q % 2, :], m.rt[:, q % 2, :], mem.neg_half[:, 0:1], ALU.pow).then_inc(s["rs_ready"], 1)
                if back(0):
                    k, q, u, M, i = back(0)
                    g.wait_ge(s["dp_ready"], M + 1)
                    wait(g, s["y1_ready"], k - 1)
                    g.tensor_tensor(heads(m.y0[:, q % 2, :]), heads(m.xB[:, q % 2, 0:256]),
                                    over(m.Dp[:, u, :], 64), ALU.mult).then_inc(s["y0_ready"], 1)
            schedule(g, norm, front, tile, lambda back: None)


def normalise(nc, mem, name, src, dst):
    rstd_ready, done = mem.sem(name + "_rstd"), mem.sem(name + "_done")
    mem.var_ready = mem.sem(name + "_var")
    with nc.Block() as block:
        @block.vector
        def _(v):
            layer_norm_stats(v, mem, name, lambda t: src[:, t, :])
            for t in range(16):
                v.wait_ge(rstd_ready, t // 8 + 1)
                v.tensor_scalar(dst[:, t, :], src[:, t, :], mem.mv[:, t, 0:1], mem.rstd[:, t:t + 1],
                                ALU.subtract, ALU.mult).then_inc(done, 1)
            v.wait_ge(done, 16)

        @block.gpsimd
        def _(g):
            layer_norm_power(g, mem, rstd_ready)


class Buffers:
    pass


def mixture_buffers(mem, name):
    mem.hidden = mem.sb(name + "_hidden", [P, 2, 2, 512])
    mem.W1h, mem.W1l = mem.sb(name + "_W1h", [P, 2, 256], F32R), mem.sb(name + "_W1l", [P, 2, 256], F32R)
    return mem.sb(name + "_high", [P, 2048], F32R), mem.sb(name + "_low", [P, 2048], F32R)


def program(nc, t, out):
    with ExitStack() as ctx:
        mem = Memory(nc, ctx)
        NT = 16
        x_all = mem.sb("x_all", [P, NT, P])
        mem.ps = ctx.enter_context(nc.psum_tensor("ps", [P, 8, 512], F32))
        mem.big_a = mem.sb("big_a", [P, 2048])
        mem.tokens_b = mem.sb("tokens_b", [P, NT, P])
        mem.tokens_a = mem.sb("tokens_a", [P, NT, P])
        mem.ident = mem.sb("ident", [P, P])
        mem.neg_half = mem.sb("neg_half", [P, NT])
        mem.stats = mem.sb("stats", [P, NT, 6])
        mem.mv, mem.var, mem.rstd = mem.sb("mv", [P, NT, 2]), mem.sb("var", [P, NT]), mem.sb("rstd", [P, NT])
        mem.stage_a, mem.stage_b = mem.sb("stage_a", [P, 2, 4, P]), mem.sb("stage_b", [P, 2, P])
        w = {}
        mem.r_logits, mem.r_above, mem.r_equal, mem.r_seen, mem.r_exp, mem.gates = (
            mem.sb(n, [P, 256]) for n in ("r_logits", "r_above", "r_equal", "r_seen", "r_exp", "gates"))
        mem.best, mem.r_small, mem.gatesT = mem.sb("best", [P, NT, 8]), mem.sb("r_small", [P, 4, NT]), mem.sb("gatesT", [16, NT * P])
        mem.keep = {e: mem.sb(f"keep{e}", [P, NT * e]) for e in (16, 8)}
        mem.layers, mem.layer_rows = mem.sb("layers", [P, 4, C_ALL]), mem.sb("layer_rows", [P, 3, 4, 4])
        mem.in_all, mem.out_all = mem.sb("in_all", [P, 4, 644]), mem.sb("out_all", [P, 8, P])
        mem.upto, mem.after, mem.eps4 = mem.sb("upto", [P, P]), mem.sb("after", [P, P]), mem.sb("eps4", [P, 1])
        mem.xp = mem.sb("xp", [P, 3, 2, 259])
        mem.W1, mem.W2 = mem.sb("W1", [P, 2, 256]), mem.sb("W2", [P, 2, 2, P])

        mem.bias = mem.sb("bias", [P, 2, 2])
        w["router0"], w["router1"] = mem.sb("router0", [P, 16]), mem.sb("router1", [P, 8])
        w["mix_w"], w["mix_b"], w["ones"] = mem.sb("mix_w", [P, P]), mem.sb("mix_b", [1, P]), mem.sb("ones", [1, P])
        w["rb0"] = mem.sb("rb0", [P, 16])
        w["b2_0"], w["b2_1"] = mem.sb("b2_0", [16, P]), mem.sb("b2_1", [8, P])
        rows = [mem.sb(f"rows{i}", [P, P]) for i in range(2)]
        cols = [mem.sb(f"cols{i}", [P, P]) for i in range(2)]
        mem.vec_in, mem.vec_mm, mem.vec_sb = mem.sem("vec_in"), mem.sem("vec_mm"), mem.sem("vec_sb")
        rows_zero, keep_zero = mem.sem("rows_zero"), mem.sem("keep_zero")
        mem.x_in, mem.consts_ready = mem.sem("x_in"), mem.sem("consts_ready")
        w["attn_in"], w["attn_in_n"] = mem.sem("attn_in"), 5 * 16
        ident_zero = mem.sem("ident_zero")
        out_done = mem.sem("out_done")

        mem.phase()
        w["Wq"] = mem.sb("Wq", [P, 1024])
        w["Wkk"] = mem.sb("Wkk", [P, 4, 2, 64])
        w["Wv"] = mem.sb("Wv", [P, 256])
        w["Wpost"] = mem.sb("Wpost", [P, 8, P])
        mem.stage_c = mem.sb("stage_c", [P, 512])
        mem.Q, mem.K = mem.sb("Q", [P, 2, 2, P]), mem.sb("K", [P, 2, 256])
        mem.probs, mem.probsT = mem.sb("probs", [P, 2, 4, 256]), mem.sb("probsT", [P, 2, 2, 4, P])
        mem.Atile = mem.sb("Atile", [P, 2, 256])
        mem.nm, mem.den, mem.rden = mem.sb("nm", [P, 2, 4]), mem.sb("den", [P, 2, 4]), mem.sb("rden", [P, 4])
        mem.big_b, mem.big_c = mem.sb("big_b", [P, 8 * 2048]), mem.sb("big_c", [P, 4096])
        vector_rows, at = [], {}
        place = [0, 0]

        def vector(name, tile, src):
            n = src.shape[0]
            vector_rows.append((tile, place[tile], src))
            at[name] = cols[tile][:, place[tile]:place[tile] + n]
            place[tile] += n

        vector("b1_0", 0, t["L0_ffn_b1"].rearrange("e (h p) -> (e h) p", p=P))
        vector("b1_1", 0, t["L1_ffn_b1"].rearrange("e (h p) -> (e h) p", p=P))
        for n in ("g1", "be1", "g2", "be2"):
            vector(n, 1, t["L1_ffn_" + n].rearrange("(o d) -> o d", o=1))
        vector("conv_w", 1, t["L1_attn_conv_w"].rearrange("l k (c p) -> (l k c) p", p=P))
        vector("conv_b", 1, t["L1_attn_conv_b"].rearrange("l (c p) -> (l c) p", p=P))
        vector("ln_w", 1, t["L1_attn_ln_w"])
        vector("ln_b", 1, t["L1_attn_ln_b"])
        vector("norm_w", 1, t["L1_attn_norm_w"].rearrange("l (c p) -> (l c) p", p=P))
        b1_at = [0, 32]
        vec_in_n = 16 * (len(vector_rows) + 7)

        with nc.Block() as block:
            @block.sync
            def _(sp):
                sp.dma_start(x_all[:], t["L0_attn_X"].rearrange("b (t p) d -> p (b t) d", p=P)).then_inc(mem.x_in, 16)
                sp.dma_start(w["Wv"][:], t["L0_attn_Wv"]).then_inc(w["attn_in"], 16)
                wk = t["L0_attn_Wk"].rearrange("d (g e) -> d g e", g=4)
                for r in range(2):
                    sp.dma_start(w["Wkk"][:, :, r, :], wk).then_inc(w["attn_in"], 16)
                sp.dma_start(w["Wq"][:], t["L0_attn_Wq"]).then_inc(w["attn_in"], 16)
                sp.dma_start(w["Wpost"][:], t["L0_attn_Wpost"].rearrange("(c p) d -> p c d", p=P)).then_inc(w["attn_in"], 16)

                sp.wait_ge(rows_zero, 2)
                for tile, at, src in vector_rows:
                    n = src.shape[0]
                    sp.dma_start(rows[tile][at:at + n, :], src).then_inc(mem.vec_in, 16)
                sp.dma_start(w["router0"][:], t["L0_ffn_router_w"]).then_inc(mem.vec_in, 16)
                sp.dma_start(w["router1"][:], t["L1_ffn_router_w"]).then_inc(mem.vec_in, 16)
                sp.dma_start(w["rb0"][:], t["L0_ffn_router_b"].rearrange("(o e) -> o e", o=1).broadcast_to([P, 16])).then_inc(mem.vec_in, 16)
                sp.dma_start(w["b2_0"][:], t["L0_ffn_b2"]).then_inc(mem.vec_in, 16)
                sp.dma_start(w["mix_w"][:], t["L1_ffn_mix_w"]).then_inc(mem.vec_in, 16)
                sp.dma_start(w["mix_b"][:], t["L1_ffn_mix_b"].rearrange("(o d) -> o d", o=1)).then_inc(mem.vec_in, 16)
                sp.dma_start(w["b2_1"][:], t["L1_ffn_b2"]).then_inc(mem.vec_in, 16)

            @block.tensor
            def _(pe):
                pe.wait_ge(mem.consts_ready, 1)
                pe.wait_ge(mem.vec_in, vec_in_n)
                for i in range(2):
                    pe.transpose(mem.ps[:, i, 0:P], rows[i][:], mem.ident[:]).then_inc(mem.vec_mm, 1)

            @block.scalar
            def _(a):
                for i in range(2):
                    a.wait_ge(mem.vec_mm, i + 1)
                    a.copy(cols[i][:], mem.ps[:, i, 0:P]).then_inc(mem.vec_sb, 1)

            @block.vector
            def _(v):
                for i in range(2):
                    v.memset(rows[i][:], 0.0).then_inc(rows_zero, 1)
                v.memset(w["ones"][:], 1.0)
                for e in (16, 8):
                    v.memset(mem.keep[e][:], 1.0).then_inc(keep_zero, 1)
                v.wait_ge(keep_zero, 2)
                for e in (16, 8):
                    v.memset(mem.keep[e][:].rearrange("p (t e) -> p t e", e=e)[:, :, 0:1], 0.0).then_inc(keep_zero, 1)
                v.wait_ge(keep_zero, 4)

            @block.gpsimd
            def _(g):
                g.memset(mem.neg_half[:], -0.5)
                g.memset(mem.ident[:], 0.0).then_inc(ident_zero, 1)
                g.wait_ge(ident_zero, 1)
                g.affine_select(out=mem.ident[:], in_=mem.ident[:], pattern=[[-1, P]], compare_op=ALU.not_equal,
                                fill=1.0, base=0, channel_multiplier=1).then_inc(mem.consts_ready, 1)

        attention(nc, mem, x_all, w)
        mem.end_phase()
        nT, acc = mem.big_a[:], mem.tokens_a
        mem.phase()
        parts = mixture_buffers(mem, "e")
        normalised_transposes(nc, mem, "e0", x_all, nT, parts, 16, [(None, w["router0"][:])], mem.vec_in, vec_in_n)
        route(nc, mem, "e1", 16, 4, True, w["rb0"][:], w["b2_0"][:], acc)
        gates0 = mem.gates[:, 0:NT * 16]
        mixture(nc, mem, "e2", parts, acc, t["L0_ffn_w1"].rearrange("(i u) h f -> i u h f", u=2),
                t["L0_ffn_w2"].rearrange("(i u) f h -> i u f h", u=2), cols[0][:, b1_at[0]:b1_at[0] + 36],
                lambda tok, i, u: gates0[:, bass.ds(i * 2 + (tok * 16 + u), 1)], ACT.Gelu)
        add_layer_norm(nc, mem, "e3", acc, x_all)
        mem.end_phase()
        mamba_constants(nc, mem, t, cols, at)
        xm = mem.tokens_a
        normalise(nc, mem, "m0", x_all, xm)
        mem.phase()
        mem.m = m = Buffers()
        m.lc = mem.sb("m_lc", [P, 2, C_ALL])
        m.Dp = mem.sb("m_Dp", [P, 2, 4])
        m.Wx = mem.sb("m_Wx", [P, 2, 384])
        m.stats = mem.sb("m_stats", [P, 4, 6])
        m.mv = mem.sb("m_mv", [P, 4, 2])
        m.veps = mem.sb("m_veps", [P, 4])
        m.rstd = mem.sb("m_rstd", [P, 4])
        m.xn = mem.sb("m_xn", [P, 4, P])
        m.xnT = mem.sb("m_xnT", [P, 2, 512])
        m.xc = mem.sb("m_xc", [P, 3, 512])
        m.th = mem.sb("m_th", [P, 3, 512])
        m.xs = mem.sb("m_xs", [P, 2, 3, 512])
        m.CT = mem.sb("m_CT", [64, 2, 512])
        m.zt = mem.sb("m_zt", [P, 512])
        m.g = mem.sb("m_g", [P, 2, 4, 256])
        m.x4 = mem.sb("m_x4", [P, 4, 4])
        m.ax = mem.sb("m_ax", [P, 4, 4])
        m.eu = mem.sb("m_eu", [P, 4, 4])
        m.poly = mem.sb("m_poly", [P, 4, 4])
        m.sp = mem.sb("m_sp", [P, 2, 4, 4])
        m.a = mem.sb("m_a", [P, 2, 4, 4])
        m.am = mem.sb("m_am", [P, 2, 4, P])
        m.E = mem.sb("m_E", [P, 2, 512])
        m.Gm = mem.sb("m_Gm", [P, P])
        m.M = mem.sb("m_M", [P, 2, 4, P])
        m.ec = mem.sb("m_ec", [P, 2, 8])
        m.xB = mem.sb("m_xB", [P, 2, 320])
        m.dtx = mem.sb("m_dtx", [P, 2, 256])
        m.dtxw = mem.sb("m_dtxw", [P, 256])
        m.y0 = mem.sb("m_y0", [P, 2, 256])
        m.state = mem.sb("m_state", [64, 256])
        m.yi = mem.sb("m_yi", [P, 256])
        m.y1 = mem.sb("m_y1", [P, 2, 256])
        m.y2 = mem.sb("m_y2", [P, 2, 256])
        m.junk = mem.sb("m_junk", [P, 2, 256])
        m.ssq = mem.sb("m_ssq", [P, 2, 1])
        m.rt = mem.sb("m_rt", [P, 2, 1])
        m.rs = mem.sb("m_rs", [P, 2, 1])
        m.yT = mem.sb("m_yT", [P, 2, 2, P])
        mamba(nc, mem, xm)
        mem.end_phase()
        add_layer_norm(nc, mem, "m2", xm, x_all)
        x2 = mem.tokens_b
        mem.phase()
        parts = mixture_buffers(mem, "f")
        normalise(nc, mem, "f0", x_all, x2)
        normalised_transposes(nc, mem, "f1", x2, nT, None, P,
                              [(None, mem.ident[:]), (None, w["mix_w"][:]), (w["ones"][:], w["mix_b"][:])],
                              mem.vec_in, vec_in_n, pre=(at["g1"], at["be1"]), add_to=x2)
        normalised_transposes(nc, mem, "f3", x2, nT, parts, 8, [(None, w["router1"][:])], mem.vec_in, vec_in_n,
                              pre=(at["g2"], at["be2"]))
        route(nc, mem, "f4", 8, 2, False, None, w["b2_1"][:], acc)
        gates1 = mem.gates[:, 0:NT * 8]
        mixture(nc, mem, "f5", parts, acc, t["L1_ffn_w1"].rearrange("e h (s f) -> e s h f", s=2),
                t["L1_ffn_w2"].rearrange("e (s f) h -> e s f h", s=2), cols[0][:, b1_at[1]:b1_at[1] + 36],
                lambda tok, i, u: gates1[:, bass.ds(i + tok * 8, 1)], ACT.Silu)
        add_tokens(nc, mem, "f6", acc, x2)
        add_layer_norm(nc, mem, "f7", acc, x_all)
        mem.end_phase()

        with nc.Block() as block:
            @block.sync
            def _(sp):
                sp.dma_start(out.rearrange("b (t p) d -> p (b t) d", p=P), x_all[:]).then_inc(out_done, 16)
                sp.wait_ge(out_done, 16)


_INS = ['L0_attn_X', 'L0_attn_Wq', 'L0_attn_Wk', 'L0_attn_Wv', 'L0_attn_Wpost', 'L0_ffn_router_w', 'L0_ffn_router_b',
        'L0_ffn_w1', 'L0_ffn_b1', 'L0_ffn_w2', 'L0_ffn_b2', 'L1_attn_ln_w', 'L1_attn_ln_b', 'L1_attn_in_w',
        'L1_attn_conv_w', 'L1_attn_conv_b', 'L1_attn_dt_bias', 'L1_attn_A_log', 'L1_attn_Dp', 'L1_attn_norm_w',
        'L1_attn_out_w', 'L1_ffn_g1', 'L1_ffn_be1', 'L1_ffn_mix_w', 'L1_ffn_mix_b', 'L1_ffn_g2', 'L1_ffn_be2',
        'L1_ffn_router_w', 'L1_ffn_w1', 'L1_ffn_b1', 'L1_ffn_w2', 'L1_ffn_b2']
_OUTS = [((8, 256, 128), 'float32')]


def kernel(**inputs):
    import numpy as _np
    import concourse.bacc as _bacc
    from concourse import mybir as _mybir
    from concourse.bass_utils import run_bass_kernel_spmd as _run

    nc = _bacc.Bacc("TRN2", target_bir_lowering=False, num_devices=1)
    arrays, tensors = {}, {}
    for name in _INS:
        a = _np.ascontiguousarray(inputs[name])
        arrays[f"in_{name}_dram"] = a
        tensors[name] = nc.dram_tensor(f"in_{name}_dram", a.shape, _mybir.dt.from_np(a.dtype), kind="ExternalInput").ap()
    shape, dtype = _OUTS[0]
    out = nc.dram_tensor("out_0_dram", shape, _mybir.dt.from_np(_np.dtype(dtype)), kind="ExternalOutput").ap()
    program(nc, tensors, out)
    r = _run(nc, [arrays], core_ids=[0])
    return r.results[0]["out_0_dram"]
```

```python
from contextlib import ExitStack

import concourse.bass as bass
from concourse import mybir

F32 = mybir.dt.float32
F32R = mybir.dt.float32r
ALU = mybir.AluOpType
ACT = mybir.ActivationFunctionType
AX = mybir.AxisListType

P = 128
EPS = 1e-5


def wait(eng, sem, value):
    if isinstance(value, int) and value <= 0:
        return
    eng.wait_ge(sem, value)


def rolled(eng, times, body):
    body(0)
    if times > 1:
        with eng.Fori(1, times) as i:
            body(i)


def chain(eng, sem, start=0):
    count = [start]

    def link(ins):
        count[0] += 1
        ins.then_inc(sem, 1)
        eng.wait_ge(sem, count[0])

    return link


class Memory:

    def __init__(self, nc, ctx):
        self.nc, self.ctx, self.tensors, self.sems = nc, ctx, ctx, None

    def phase(self):
        self.tensors, self.sems = ExitStack(), []

    def end_phase(self):
        self.tensors.close()
        self.nc.clear_and_free_semaphores(self.sems)
        self.nc.all_engine_barrier()
        self.tensors, self.sems = self.ctx, None

    def sb(self, name, shape, dt=F32):
        return self.tensors.enter_context(self.nc.sbuf_tensor(name, shape, dt))

    def sem(self, name):
        if self.sems is None:
            return self.ctx.enter_context(self.nc.semaphore(name))
        self.sems.append(self.nc.alloc_semaphore(name=name))
        return self.sems[-1]


def layer_norm_stats(v, mem, name, src, ready=lambda t: None):
    bn, merged = mem.sem(name + "_bn"), mem.sem(name + "_merged")
    for half in range(2):
        tiles = range(8 * half, 8 * half + 8)
        for t in tiles:
            ready(t)
            v.bn_stats(mem.stats[:, t, :], src(t)).then_inc(bn, 1)
        v.wait_ge(bn, 8 * half + 8)
        for t in tiles:
            v.bn_aggr(mem.mv[:, t, :], mem.stats[:, t, :]).then_inc(merged, 1)
        v.wait_ge(merged, 8 * half + 8)
        v.tensor_scalar(mem.var[:, 8 * half:8 * half + 8], mem.mv[:, 8 * half:8 * half + 8, 1], EPS, None,
                        ALU.add).then_inc(mem.var_ready, 1)


def layer_norm_power(g, mem, rstd_ready):
    for half in range(2):
        cols = slice(8 * half, 8 * half + 8)
        g.wait_ge(mem.var_ready, half + 1)
        g.tensor_tensor(mem.rstd[:, cols], mem.var[:, cols], mem.neg_half[:, cols], ALU.pow).then_inc(rstd_ready, 1)


class AddedNorm:

    def __init__(self, mem, name, r_all, x_all):
        self.mem, self.name, self.r_all, self.x_all = mem, name, r_all, x_all
        self.rstd_ready, self.norm_step, self.x_step = (mem.sem(name + s) for s in ("_rstd", "_norm", "_x"))
        self.var_ready = mem.sem(name + "_var")

    def add(self, eng, q):
        eng.wait_ge(self.norm_step, 4 * q + 4)
        part = slice(4 * q, 4 * q + 4)
        eng.tensor_tensor(self.x_all[:, part, :], self.x_all[:, part, :], self.r_all[:, part, :],
                          ALU.add).then_inc(self.x_step, 1)

    def vector(self, v, ready=lambda t: None):
        mem = self.mem
        mem.var_ready = self.var_ready
        layer_norm_stats(v, mem, self.name, lambda t: self.r_all[:, t, :], ready)
        for t in range(16):
            v.wait_ge(self.rstd_ready, t // 8 + 1)
            v.tensor_scalar(self.r_all[:, t, :], self.r_all[:, t, :], mem.mv[:, t, 0:1], mem.rstd[:, t:t + 1],
                            ALU.subtract, ALU.mult).then_inc(self.norm_step, 1)
        for q in (2, 3):
            self.add(v, q)
        v.wait_ge(self.x_step, 4)

    def gpsimd(self, g):
        self.mem.var_ready = self.var_ready
        layer_norm_power(g, self.mem, self.rstd_ready)
        for q in (0, 1):
            self.add(g, q)
        g.wait_ge(self.x_step, 4)


def add_layer_norm(nc, mem, name, r_all, x_all, more=None):
    norm, sum_ready = AddedNorm(mem, name, r_all, x_all), mem.sem(name + "_sum")
    with nc.Block() as block:
        @block.vector
        def _(v):
            def add_more(t):
                if more is not None and t % 4 == 0:
                    v.tensor_tensor(r_all[:, t:t + 4, :], r_all[:, t:t + 4, :], more[:, t:t + 4, :],
                                    ALU.add).then_inc(sum_ready, 1)
                    v.wait_ge(sum_ready, t // 4 + 1)

            norm.vector(v, add_more)

        @block.gpsimd
        def _(g):
            norm.gpsimd(g)


def attention(nc, mem, x_all, w, later_loads):
    NB, TPB = 8, 2
    NT = NB * TPB
    G, W, E = 4, 4, 64
    ps = mem.ps
    nT = mem.big_a[:, 0:NT * P]
    AT = mem.big_b[:].rearrange("p (c t) -> p c t", c=8)
    V = mem.big_c[:].rearrange("p (t g e) -> p t g e", t=NT, g=G)
    ident = mem.ident
    rstd = mem.rstd[:]

    normalised_transposes(nc, mem, "a0", x_all, nT, None, G * E, [w["Wv"][:]], w["attn_in"], w["attn_in_n"],
                          to=mem.big_c,
                          x_in=mem.x_in)

    STEPS = G * TPB
    S = ps[:, 0:4, :].rearrange("p b (w t) -> p (b w) t", t=256).rearrange("p (s w) t -> p s w t", s=2)
    T = ps[:, 4:6, :].rearrange("p b (w s) -> p b w s", w=W)
    O = ps[:, 6, 0:256].rearrange("p (w e) -> p w e", w=W)
    ATp = ps[:, 6, 256:512].rearrange("p (c s) -> p c s", c=2)
    Qp, Kp = ps[:, 7, 0:256].rearrange("p (c s) -> p c s", c=2), ps[:, 7, 256:512]
    Q, K = mem.Q, mem.K
    Ql, Kl = mem.Ql, mem.Kl
    pr, pT = mem.probs, mem.probsT
    At = mem.Atile
    nm, den, rden = mem.nm, mem.den, mem.rden
    names = "qk_mm q_sb k_sb s_mm max_ready p_ready t_mm pT_sb o_mm r_ready a_ready aT_mm aT_sb"
    s = {n: mem.sem("a1_" + n) for n in names.split()}
    with nc.Block() as block:
        @block.sync
        def _(sp):
            later_loads(sp)

        def steps(eng, emit, lag):
            def body(b):
                for j in range(STEPS):
                    def back(l, j=j):
                        if j >= l:
                            return b * STEPS + (j - l), j - l, b
                        if isinstance(b, int) and b == 0:
                            return None
                        return b * STEPS + (j - l), j - l + STEPS, b - 1
                    emit(back, (b, j))
            body(0)
            with eng.Fori(1, NB - 1) as b:
                body(b)
            body(NB - 1)
            for j in range(lag):
                def back(l, j=j):
                    if l <= j:
                        return None
                    return NB * STEPS + j - l, STEPS + j - l, NB - 1
                emit(back, None)

        @block.tensor
        def _(pe):
            def project(k, j, b):
                g, st = j // 2, j % 2
                wait(pe, s["q_sb"], 2 * k)
                wait(pe, s["k_sb"], b * (2 * G) + (j + 1) // 2 * 2)
                for c in range(2):
                    last = pe.matmul(Qp[:, c, :], w["Wq"][:, (g * 2 + c) * P:(g * 2 + c + 1) * P],
                                     nT[:, bass.ds(b * 256 + st * P, P)], start=True, stop=True)
                if st == 0:
                    last = pe.matmul(Kp, w["Wkk"][:, g, :, :].rearrange("p r e -> p (r e)"),
                                     nT[:, bass.ds(b * 256, 256)], start=True, stop=True)
                last.then_inc(s["qk_mm"], 1)

            def emit(back, here):
                now = back(0)
                if now:
                    k, j, b = now
                    if j + 1 < STEPS:
                        project(k + 1, j + 1, b)
                    elif not (isinstance(b, int) and b == NB - 1):
                        project(k + 1, 0, b + 1)
                if back(3):
                    k3, j3, b3 = back(3)
                    pe.wait_ge(s["a_ready"], k3 + 1)
                    for c in range(2):
                        last = pe.transpose(ATp[:, c, :], At[:, j3 % 2, c * P:(c + 1) * P], ident[:])
                    last.then_inc(s["aT_mm"], 1)
                if now:
                    pe.wait_ge(s["q_sb"], 2 * k + 2)
                    pe.wait_ge(s["k_sb"], b * (2 * G) + (j // 2 + 1) * 2)
                    wait(pe, s["p_ready"], k - 1)
                    for h in range(W):
                        o, c = 64 * (h % 2), h // 2
                        scores = S[:, j % 2, 2 * (h % 2) + c, :]
                        qh, ql = (x[o:o + 64, j % 2, c, :] for x in (Q, Ql))
                        kh, kl = (x[o:o + 64, (j // 2) % 2, :] for x in (K, Kl))
                        pe.matmul(scores, qh, kh, start=True, stop=False)
                        pe.matmul(scores, ql, kh, start=False, stop=False)
                        last = pe.matmul(scores, qh, kl, start=False, stop=True)
                    last.then_inc(s["s_mm"], 1)
                if back(2):
                    k2, j2, b2 = back(2)
                    pe.wait_ge(s["pT_sb"], k2 + 1)
                    wait(pe, s["aT_sb"], k2)
                    for h in range(W):
                        for tt in range(TPB):
                            last = pe.matmul(O[:, h, :], pT[:, j2 % 2, tt, h, :],
                                             V[:, b2 * TPB + tt, j2 // 2, :], start=(tt == 0), stop=(tt == 1))
                    last.then_inc(s["o_mm"], 1)
                if back(1):
                    k1, j1, b1 = back(1)
                    pe.wait_ge(s["p_ready"], k1 + 1)
                    wait(pe, s["pT_sb"], k1)
                    for tt in range(TPB):
                        for h in range(W):
                            last = pe.transpose(T[:, tt, h, :], pr[:, j1 % 2, h, tt * P:(tt + 1) * P], ident[:])
                    last.then_inc(s["t_mm"], 1)

            project(0, 0, 0)
            steps(pe, emit, 3)

        @block.scalar
        def _(a):
            def copy_q(k, j):
                a.wait_ge(s["qk_mm"], k + 1)
                wait(a, s["s_mm"], k - 1)
                a.copy(Q[:, j % 2, :, :], Qp).then_inc(s["q_sb"], 1)

            def emit(back, here):
                if back(0):
                    k, j, b = back(0)
                    if not (isinstance(b, int) and b == NB - 1 and j == STEPS - 1):
                        copy_q(k + 1, (j + 1) % STEPS)
                    a.wait_ge(s["max_ready"], k + 1)
                    wait(a, s["t_mm"], k - 1)
                    wait(a, s["r_ready"], k - 3)
                    for h in range(W):
                        i = 2 * (h % 2) + h // 2
                        last = a.activation(pr[:, j % 2, h, :], S[:, j % 2, i, :], ACT.Exp,
                                            bias=nm[:, j % 2, i:i + 1], accum_out=den[:, j % 4, h:h + 1])
                    last.then_inc(s["p_ready"], 1)
                if back(1):
                    k1, j1, b1 = back(1)
                    a.wait_ge(s["t_mm"], k1 + 1)
                    wait(a, s["o_mm"], k1 - 1)
                    a.copy(pT[:, j1 % 2, :, :, :], T).then_inc(s["pT_sb"], 1)
            copy_q(0, 0)
            steps(a, emit, 1)

        @block.vector
        def _(v):
            def copies(k, j, b):
                wait(v, s["s_mm"], k - 1)
                v.wait_ge(s["qk_mm"], k + 1)
                v.wait_ge(s["q_sb"], 2 * k + 1)
                v.tensor_tensor(Ql[:, j % 2, :, :], Qp, Q[:, j % 2, :, :].bitcast(F32), ALU.subtract).then_inc(s["q_sb"], 1)
                if j % 2 == 0:
                    wait(v, s["s_mm"], k - 2)
                    Kh = K[:, (j // 2) % 2, :]
                    v.tensor_scalar(Kh, Kp, E ** -0.5, None, ALU.mult).then_inc(s["k_sb"], 1)
                    v.wait_ge(s["k_sb"], b * (2 * G) + (j // 2 * 2 + 1))
                    v.scalar_tensor_tensor(out=Kl[:, (j // 2) % 2, :], in0=Kp, scalar=E ** -0.5, in1=Kh.bitcast(F32),
                                           op0=ALU.mult, op1=ALU.subtract).then_inc(s["k_sb"], 1)

            def emit(back, here):
                if back(3):
                    k3, j3, b3 = back(3)
                    v.wait_ge(s["aT_mm"], k3 + 1)
                    g, st = j3 // 2, j3 % 2
                    v.tensor_copy(AT[:, 2 * g:2 * g + 2, bass.ds(b3 * 256 + st * P, P)], ATp).then_inc(s["aT_sb"], 1)
                if back(0):
                    k, j, b = back(0)
                    v.wait_ge(s["s_mm"], k + 1)
                    wait(v, s["p_ready"], k - 1)
                    v.tensor_reduce(nm[:, j % 2, :], S[:, j % 2, :, :], AX.X, ALU.max,
                                    negate=True).then_inc(s["max_ready"], 1)
                    if j + 1 < STEPS:
                        copies(k + 1, j + 1, b)
                    elif not (isinstance(b, int) and b == NB - 1):
                        copies(k + 1, 0, b + 1)
                if back(2):
                    k2, j2, b2 = back(2)
                    v.wait_ge(s["p_ready"], k2 + 1)
                    wait(v, s["a_ready"], k2)
                    v.reciprocal(rden[:], den[:, j2 % 4, :]).then_inc(s["r_ready"], 1)
                    v.wait_ge(s["r_ready"], k2 + 1)
                    v.wait_ge(s["o_mm"], k2 + 1)
                    wait(v, s["aT_mm"], k2 - 1)
                    v.tensor_tensor(At[:, j2 % 2, :].rearrange("p (w e) -> p w e", w=W), O,
                                    rden[:].rearrange("p (w o) -> p w o", o=1).broadcast_to([P, W, E]),
                                    ALU.mult).then_inc(s["a_ready"], 1)

            copies(0, 0, 0)
            steps(v, emit, 3)

    CH = NT // 4
    PTs = mem.stage_c
    r_all = mem.tokens_a
    n = {k: mem.sem("a2_" + k) for k in "p_mm p_sb pt_mm n_sb r_sb".split()}
    last_norm = AddedNorm(mem, "a3", r_all, x_all)
    with nc.Block() as block:
        @block.tensor
        def _(pe):
            def transposes(c):
                pe.wait_ge(n["p_sb"], c + 1)
                wait(pe, n["r_sb"], c - 1)
                for u in range(4):
                    last = pe.transpose(ps[:, 2 + c % 2, u * P:(u + 1) * P], PTs[:, c % 2, u * P:(u + 1) * P], ident[:])
                last.then_inc(n["pt_mm"], 1)

            for c in range(CH):
                wait(pe, n["p_sb"], c - 1)
                for h in range(8):
                    last = pe.matmul(ps[:, c % 2, :], w["Wpost"][:, h, :], AT[:, h, c * 512:(c + 1) * 512],
                                     start=(h == 0), stop=(h == 7))
                last.then_inc(n["p_mm"], 1)
                if c:
                    transposes(c - 1)
            transposes(CH - 1)

        @block.scalar
        def _(a):
            for c in range(CH):
                a.wait_ge(n["p_mm"], c + 1)
                wait(a, n["pt_mm"], c - 1)
                a.copy(PTs[:, c % 2, :], ps[:, c % 2, :]).then_inc(n["p_sb"], 1)

        @block.vector
        def _(v):
            for t in range(NT):
                v.tensor_scalar(r_all[:, t, :], x_all[:, t, :], mem.mv[:, t, 0:1], rstd[:, t:t + 1],
                                ALU.subtract, ALU.mult).then_inc(n["n_sb"], 1)
            v.wait_ge(n["n_sb"], NT)

            def add_projected(t):
                if t % 4 == 0:
                    c = t // 4
                    v.wait_ge(n["pt_mm"], c + 1)
                    tiles = r_all[:, t:t + 4, :].rearrange("p t d -> p (t d)")
                    v.tensor_tensor(tiles, tiles, ps[:, 2 + c % 2, :], ALU.add).then_inc(n["r_sb"], 1)
                    v.wait_ge(n["r_sb"], c + 1)

            last_norm.vector(v, add_projected)

        @block.gpsimd
        def _(g):
            last_norm.gpsimd(g)


def normalised_transposes(nc, mem, name, x_all, nT, parts, width, products, weights_in, weights_n, pre=None,
                          add_to=None, shift=None, to=None, x_in=None):
    GROUPS = 4
    ps, ident = mem.ps, mem.ident
    mem.var_ready = mem.sem(name + "_var_ready")
    rstd_ready = mem.sem(name + "_rstd_ready")
    n_ready, nT_mm, nT_sb, high_sb, low_sb, l_mm, sum_sb, copy_sb, shifted = (
        mem.sem(name + "_" + s) for s in ("n_ready", "nT_mm", "nT_sb", "high_sb", "low_sb", "l_mm", "sum_sb", "copy_sb", "shifted"))
    ntile = mem.stage_a
    results = ps[:, 2:6, :].rearrange("p b t -> p (b t)")
    rounds = max(1, 16 * width // 2048)
    assert rounds <= 2

    def group(g):
        return slice(g * 512, (g + 1) * 512)

    with nc.Block() as block:
        @block.vector
        def _(v):
            def arrived(t):
                if x_in and t % 4 == 0:
                    v.wait_ge(x_in[t // 4], 16)

            layer_norm_stats(v, mem, name, lambda t: x_all[:, t, :], arrived)

            def low(g):
                v.wait_ge(nT_sb, g + 1)
                v.wait_ge(high_sb, g + 1)
                v.tensor_tensor(parts[1][:, group(g)], nT[:, group(g)], parts[0][:, group(g)].bitcast(F32),
                                ALU.subtract).then_inc(low_sb, 1)

            for g in range(GROUPS):
                v.wait_ge(rstd_ready, g // 2 + 1)
                wait(v, nT_mm, g - 1)
                for u in range(4):
                    t = 4 * g + u
                    v.tensor_scalar(ntile[:, g % 2, u, :], x_all[:, t, :], mem.mv[:, t, 0:1], mem.rstd[:, t:t + 1],
                                    ALU.subtract, ALU.mult).then_inc(n_ready, 1)
                if parts and g:
                    low(g - 1)
            if parts:
                low(GROUPS - 1)
                v.wait_ge(low_sb, GROUPS)
            if add_to is not None:
                for g in range(GROUPS):
                    v.wait_ge(l_mm, g + 1)
                    v.wait_ge(shifted, g + 1)
                    tiles = add_to[:, 4 * g:4 * g + 4, :].rearrange("p t d -> p (t d)")
                    v.tensor_tensor(tiles, tiles, results[:, group(g)], ALU.add).then_inc(sum_sb, 1)
                v.wait_ge(sum_sb, GROUPS)

        @block.gpsimd
        def _(g):
            layer_norm_power(g, mem, rstd_ready)
            if add_to is not None:
                for q in range(GROUPS):
                    g.wait_ge(n_ready, 4 * q + 4)
                    tiles = add_to[:, 4 * q:4 * q + 4, :]
                    g.tensor_tensor(tiles, tiles, shift.rearrange("p (o d) -> p o d", o=1).broadcast_to([P, 4, P]),
                                    ALU.add).then_inc(shifted, 1)

        @block.tensor
        def _(pe):
            pe.wait_ge(weights_in, weights_n)

            def product(g):
                pe.wait_ge(nT_sb, g + 1)
                if rounds > 1:
                    wait(pe, copy_sb, g - 1)
                for t in range(4 * g, 4 * g + 4):
                    for j, moving in enumerate(products):
                        at = t * width % 2048
                        last = pe.matmul(results[:, at:at + width],
                                         nT[:, t * P:(t + 1) * P], moving, start=(j == 0), stop=(j == len(products) - 1))
                last.then_inc(l_mm, 1)

            for g in range(GROUPS):
                pe.wait_ge(n_ready, 4 * g + 4)
                wait(pe, nT_sb, g - 1)
                if parts:
                    wait(pe, high_sb, g - 1)
                for u in range(4):
                    last = pe.transpose(ps[:, g % 2, u * P:(u + 1) * P], ntile[:, g % 2, u, :], ident[:])
                last.then_inc(nT_mm, 1)
                if g:
                    product(g - 1)
            product(GROUPS - 1)

        @block.scalar
        def _(a):
            def copied(dst, g, done):
                if pre is None:
                    a.copy(dst, ps[:, g % 2, :]).then_inc(done, 1)
                else:
                    a.activation(dst, ps[:, g % 2, :], ACT.Identity, bias=pre[1], scale=pre[0]).then_inc(done, 1)

            def results_out(g):
                n = 4 * width
                a.wait_ge(l_mm, g + 1)
                a.copy(to[:, g * n:(g + 1) * n], results[:, g * n % 2048:g * n % 2048 + n]).then_inc(copy_sb, 1)

            for g in range(GROUPS):
                a.wait_ge(nT_mm, g + 1)
                copied(nT[:, group(g)], g, nT_sb)
                if parts:
                    copied(parts[0][:, group(g)], g, high_sb)
                if to is not None and g:
                    results_out(g - 1)
            if to is not None:
                results_out(GROUPS - 1)


def route(nc, mem, name, experts, top, normalised, bias, b2, acc):
    NT = 16
    ps, ident = mem.ps, mem.ident
    N = NT * experts

    def tile3(x):
        return x[:, 0:N].rearrange("p (t e) -> p t e", e=experts)

    def over_experts(x):
        return x.rearrange("p (t o) -> p t o", o=1).broadcast_to([P, NT, experts])

    L, above, equal, seen, gates = (tile3(x) for x in (mem.r_logits, mem.r_above, mem.r_equal, mem.r_seen, mem.gates))
    best = mem.best
    small = mem.r_small
    centred, exp_ready, gates_ready = (mem.sem(name + "_" + s) for s in ("centred", "exp_ready", "gates_ready"))
    cT_mm, cT_sb, b_mm, acc_ready = (mem.sem(name + "_" + s) for s in ("cT_mm", "cT_sb", "b_mm", "acc_ready"))
    best_ready = mem.sem(name + "_best")
    cT = mem.gatesT
    with nc.Block() as block:
        @block.vector
        def _(v):
            link = chain(v, mem.sem(name + "_route_step"))
            flat = mem.r_logits[:, 0:N]
            if bias is not None:
                link(v.tensor_tensor(L, tile3(ps[:, 2, :]), bias.rearrange("p (o e) -> p o e", o=1).broadcast_to(
                    [P, NT, experts]), ALU.add))
            else:
                link(v.tensor_copy(flat, ps[:, 2, 0:N]))
            for t in range(NT):
                v.max(best[:, t, :], L[:, t, :]).then_inc(best_ready, 1)
            v.wait_ge(best_ready, NT)
            link(v.tensor_tensor(tile3(mem.r_exp), L, best[:, :, 0:1].broadcast_to([P, NT, experts]), ALU.subtract))
            v.sem_inc(centred, 1)
            kth = best[:, :, top - 1:top].broadcast_to([P, NT, experts])
            link(v.tensor_tensor(above, L, kth, ALU.is_gt))
            link(v.tensor_tensor(equal, L, kth, ALU.is_equal))
            link(v.tensor_reduce(small[:, 0, :], above, AX.X, ALU.add))
            link(v.tensor_scalar(small[:, 1, :], small[:, 0, :], -1.0, float(top), ALU.mult, ALU.add))
            link(v.tensor_tensor_scan(mem.r_seen[:, 0:N], mem.keep[experts][:, 0:N], mem.r_equal[:, 0:N], 0.0,
                                      ALU.mult, ALU.add))
            link(v.tensor_tensor(seen, seen, over_experts(small[:, 1, :]), ALU.is_le))
            link(v.tensor_tensor(seen, seen, equal, ALU.mult))
            link(v.tensor_tensor(seen, seen, above, ALU.add))
            v.wait_ge(exp_ready, 1)
            ex = tile3(mem.r_exp)
            link(v.tensor_tensor(gates, ex, seen, ALU.mult))
            link(v.tensor_reduce(small[:, 2, :], gates if normalised else ex, AX.X, ALU.add))
            link(v.reciprocal(small[:, 3, :], small[:, 2, :]))
            v.tensor_tensor(gates, gates, over_experts(small[:, 3, :]), ALU.mult).then_inc(gates_ready, 1)

        @block.scalar
        def _(a):
            a.wait_ge(centred, 1)
            a.activation(mem.r_exp[:, 0:N], mem.r_exp[:, 0:N], ACT.Exp).then_inc(exp_ready, 1)
            for q in range(4):
                a.wait_ge(cT_mm, q + 1)
                a.copy(cT[0:experts, q * 512:(q + 1) * 512], ps[0:experts, 3 + q % 2, :]).then_inc(cT_sb, 1)
            for q in range(4):
                a.wait_ge(b_mm, q + 1)
                a.copy(acc[:, 4 * q:4 * q + 4, :].rearrange("p t d -> p (t d)"), ps[:, 5 + q % 2, :]).then_inc(acc_ready, 1)

        @block.tensor
        def _(pe):
            pe.wait_ge(gates_ready, 1)
            for q in range(4):
                wait(pe, cT_sb, q - 1)
                for u in range(4):
                    last = pe.transpose(ps[0:experts, 3 + q % 2, u * P:(u + 1) * P], gates[:, 4 * q + u, :], ident[:])
                last.then_inc(cT_mm, 1)
            for q in range(4):
                pe.wait_ge(cT_sb, q + 1)
                wait(pe, acc_ready, q - 1)
                for u in range(4):
                    t = 4 * q + u
                    last = pe.matmul(ps[:, 5 + q % 2, u * P:(u + 1) * P], cT[0:experts, t * P:(t + 1) * P], b2,
                                     start=True, stop=True)
                last.then_inc(b_mm, 1)


def mixture(nc, mem, name, parts, acc, w1, w2, b1T, gate_of, func, first=None):
    ROUNDS, CH, HALF = 8, 4, 2
    xh, xl = parts
    W1h, W1l = mem.W1h, mem.W1l
    ps = mem.ps
    W1, W2, Hs = mem.W1, mem.W2, mem.hidden
    H = ps[:, 0:4, :].rearrange("p (s h) t -> p s h t", s=2)
    Y = ps[:, 4:6, :]
    w_in = [mem.sem(f"{name}_w_in{u}") for u in range(2)]
    h_mm, h_sb, y_mm, acc_done = (mem.sem(name + "_" + s) for s in ("h_mm", "h_sb", "y_mm", "acc_done"))
    w_split = mem.sem(name + "_w_split")
    bias, bias_ready = mem.bias, mem.sem(name + "_bias_ready")
    with nc.Block() as block:
        def steps(eng, emit):
            def body(i):
                for u in range(2):
                    for c in range(CH):
                        k = i * (2 * CH) + (u * CH + c)
                        if u == 0 and c == 0:
                            back = None if isinstance(i, int) and i == 0 else (k - 1, i - 1, 1, CH - 1)
                        else:
                            back = (k - 1, i, u if c else u - 1, c - 1 if c else CH - 1)
                        emit((k, i, u, c), back)
            body(0)
            with eng.Fori(1, ROUNDS - 1) as i:
                body(i)
            body(ROUNDS - 1)
            emit(None, (ROUNDS * 2 * CH - 1, ROUNDS - 1, 1, CH - 1))

        @block.sync
        def _(sp):
            def body(i):
                for u in range(2):
                    wait(sp, y_mm, (i - 1) * (2 * CH) + (u + 1) * CH)
                    sp.dma_start(W1[:, u, :], w1[i, u, :, :] if isinstance(i, int) else w1[bass.ds(i, 1), u, :, :].rearrange("a p f -> p (a f)")).then_inc(w_in[u], 16)
                    w2v = w2[i, u, :, :].rearrange("(h p) d -> p h d", p=P) if isinstance(i, int) else \
                        w2[bass.ds(i, 1), u, :, :].rearrange("a (h p) d -> p (a h) d", p=P)
                    sp.dma_start(W2[:, u, :, :], w2v).then_inc(w_in[u], 16)
            rolled(sp, ROUNDS, body)

        @block.tensor
        def _(pe):
            def emit(now, back):
                if now:
                    k, i, u, c = now
                    if c == 0:
                        pe.wait_ge(w_split, i * 4 + (u * 2 + 2))
                    wait(pe, h_sb, k - 1)
                    for h in range(HALF):
                        half, chunk = slice(h * P, (h + 1) * P), slice(c * 512, (c + 1) * 512)
                        pe.matmul(H[:, c % 2, h, :], W1h[:, u, half], xh[:, chunk], start=True, stop=False)
                        pe.matmul(H[:, c % 2, h, :], W1l[:, u, half], xh[:, chunk], start=False, stop=False)
                        last = pe.matmul(H[:, c % 2, h, :], W1h[:, u, half], xl[:, chunk], start=False, stop=True)
                    last.then_inc(h_mm, 1)
                if back:
                    k, i, u, c = back
                    pe.wait_ge(h_sb, k + 1)
                    wait(pe, acc_done, k - 1)
                    for t in range(4):
                        for h in range(HALF):
                            last = pe.matmul(Y[:, c % 2, t * P:(t + 1) * P], Hs[:, c % 2, h, t * P:(t + 1) * P],
                                             W2[:, u, h, :], start=(h == 0), stop=(h == HALF - 1))
                    last.then_inc(y_mm, 1)
            steps(pe, emit)

        @block.scalar
        def _(a):
            def emit(now, back):
                if now:
                    k, i, u, c = now
                    a.wait_ge(h_mm, k + 1)
                    wait(a, y_mm, k - 1)
                    a.wait_ge(bias_ready, i * 2 + (u + 1))
                    for h in range(HALF):
                        last = a.activation(Hs[:, c % 2, h, :], H[:, c % 2, h, :], func,
                                            bias=bias[:, u, h:h + 1])
                    last.then_inc(h_sb, 1)
            steps(a, emit)

        @block.vector
        def _(v):
            def split(i, u):
                v.wait_ge(w_in[u], i * 32 + 32)
                v.tensor_copy(W1h[:, u, :], W1[:, u, :]).then_inc(w_split, 1)
                v.wait_ge(w_split, i * 4 + (u * 2 + 1))
                v.tensor_tensor(W1l[:, u, :], W1[:, u, :], W1h[:, u, :].bitcast(F32), ALU.subtract).then_inc(w_split, 1)

            def copy_bias(i, u):
                v.tensor_copy(bias[:, u, :], b1T[:, bass.ds(i * 4 + u * 2, 2)]).then_inc(bias_ready, 1)

            def emit(now, back):
                if back:
                    k, i, u, c = back
                    v.wait_ge(y_mm, k + 1)
                    wait(v, acc_done, k - 3)
                    for t in range(4):
                        tok = 4 * c + t
                        last = v.scalar_tensor_tensor(out=acc[:, tok, :], in0=Y[:, c % 2, t * P:(t + 1) * P],
                                                      scalar=gate_of(tok, i, u), in1=acc[:, tok, :],
                                                      op0=ALU.mult, op1=ALU.add)
                    last.then_inc(acc_done, 1)
                    if c == 0 and not (isinstance(i, int) and i == ROUNDS - 1 and u == 1):
                        split(i + u, 1 - u)
                    if c == CH - 1:
                        copy_bias(i + 1, u)
            if first:
                first(v)
            split(0, 0)
            for u in range(2):
                copy_bias(0, u)
            steps(v, emit)


LOG1P = (0.9999999954, -0.4999990399, 0.3333000404, -0.2495455887, 0.1967811726, -0.153118631,
         0.1061426468, -0.05706420072, 0.0199071609, -0.003256378468)

C_DTB, C_A, C_DP, C_CW, C_CB, C_LNW, C_LNB = 0, 4, 8, 12, 24, 27, 28
C_ALL = 32


class Steps:

    def __init__(self, eng, sem, per):
        self.eng, self.sem, self.per = eng, sem, per

    def at(self, turn):
        self.turn, self.j = turn, 0

    def link(self, ins):
        self.mark(ins)
        self.join()

    def mark(self, ins):
        self.j += 1
        assert self.j <= self.per
        ins.then_inc(self.sem, 1)

    def join(self):
        self.eng.wait_ge(self.sem, self.turn * self.per + self.j)

    def end(self):
        assert self.j == self.per, (self.j, self.per)


def layers_in(sp, mem, t, loaded):
    for i, name in enumerate(("dt_bias", "A_log", "Dp")):
        sp.dma_start(mem.layer_rows[:, i, :, :], t["L1_attn_" + name].rearrange("(o l) h -> o l h", o=1).broadcast_to(
            [P, 4, 4])).then_inc(loaded, 16)
    sp.dma_start(mem.in_all[:], t["L1_attn_in_w"].rearrange("l d e -> d l e")).then_inc(loaded, 16)
    sp.dma_start(mem.out_all[:], t["L1_attn_out_w"].rearrange("l (c p) d -> p (l c) d", p=P)).then_inc(loaded, 16)


def columns_and_masks(nc, mem, rows, cols, vec_in_n):
    exp_ready, masks, mask_step = mem.sem("mc_exp"), mem.sem("mc_masks"), mem.sem("mc_mask_step")
    vec_mm, vec_sb = mem.sem("vec_mm"), mem.sem("vec_sb")
    with nc.Block() as block:
        @block.tensor
        def _(pe):
            pe.wait_ge(mem.vec_in, vec_in_n)
            for i in range(2):
                pe.transpose(mem.ps[:, i, 0:P], rows[i][:], mem.ident[:]).then_inc(vec_mm, 1)

        @block.scalar
        def _(a):
            for i in range(2):
                a.wait_ge(vec_mm, i + 1)
                a.copy(cols[i][:], mem.ps[:, i, 0:P]).then_inc(vec_sb, 1)
            a.wait_ge(mem.layers_loaded, 5 * 16)
            a.activation(mem.layer_rows[:, 1, :, :], mem.layer_rows[:, 1, :, :], ACT.Exp).then_inc(exp_ready, 1)
            a.wait_ge(exp_ready, 1)

        @block.gpsimd
        def _(g):
            for m in (mem.upto, mem.after):
                g.memset(m[:], 1.0).then_inc(mask_step, 1)
            g.memset(mem.eps4[:], 4 * EPS).then_inc(mask_step, 1)
            g.wait_ge(mask_step, 3)
            g.affine_select(out=mem.upto[:], in_=mem.upto[:], pattern=[[1, P]], compare_op=ALU.is_ge, fill=0.0,
                            base=0, channel_multiplier=-1).then_inc(masks, 1)
            g.affine_select(out=mem.after[:], in_=mem.after[:], pattern=[[-1, P]], compare_op=ALU.is_gt, fill=0.0,
                            base=0, channel_multiplier=1).then_inc(masks, 1)
            g.wait_ge(masks, 2)


def mamba_constants(v, mem, at, mix_w):
    L = 4
    tab, out_all, raw = mem.layers, mem.out_all, mem.layer_rows
    link = chain(v, mem.sem("mc_step"))
    link(v.memset(tab[:], 0.0))
    link(v.memset(mem.xp[:], 0.0))
    link(v.tensor_scalar(tab[:, :, C_CW:C_CW + 12], at["conv_w"].rearrange("p (l k) -> p l k", l=L), 0.5, None, ALU.mult))
    link(v.tensor_scalar(tab[:, :, C_CB:C_CB + 3], at["conv_b"].rearrange("p (l k) -> p l k", l=L), 0.5, None, ALU.mult))
    link(v.tensor_copy(tab[:, :, C_LNW], at["ln_w"]))
    link(v.tensor_copy(tab[:, :, C_LNB], at["ln_b"]))
    link(v.tensor_copy(tab[:, :, C_DTB:C_DTB + 4], raw[:, 0, :, :]))
    link(v.tensor_copy(tab[:, :, C_DP:C_DP + 4], raw[:, 2, :, :]))
    link(v.tensor_scalar(tab[:, :, C_A:C_A + 4], raw[:, 1, :, :], -1.0, None, ALU.mult))
    link(v.tensor_tensor(mix_w, mix_w, mem.ident[:], ALU.add))
    for c in range(2 * L):
        link(v.tensor_scalar(out_all[:, c, :], out_all[:, c, :], at["norm_w"][:, c:c + 1], None, ALU.mult))


def mamba(nc, mem, xm):
    UNITS, Q = 16, 4
    IN = 644
    ps, ident = mem.ps, mem.ident
    xnp, dtp = ps[:, 0, :], ps[:, 0, 0:4 * Q]
    Xp = [ps[:, 2, :], ps[:, 1, :], ps[:, 1, :]]
    Zp = [ps[:, 0, :], ps[:, 2, :]]
    Dps = ps[:, 3, :].rearrange("p (h t) -> p h t", h=4)
    Gp = ps[:, 4, 0:P]
    xBp, cump, outp = ps[:, 5, 0:320], ps[:, 5, 320:328], ps[:, 5, 384:384 + P]
    Yp, Ip = ps[:, 6, 0:256], ps[:, 6, 256:512]
    Sp, yTp = ps[0:64, 7, 0:256], ps[:, 7, 256:512]
    tab, in_all, out_all = mem.layers, mem.in_all, mem.out_all
    m = mem.m
    s = {n: mem.sem("m_" + n) for n in (
        "lc_ready dp_ready wx_ready stat_step var_ready rstd_ready xn_ready xnT_mm xnT_sb x_mm x_sb dt_mm dt_step ax_ready "
        "u_ready a_ready z_mm zt_ready g_ready conv_step conv_ready product_ready sum_step th_ready silu_ready am_ready d_mm g_mm xb_mm "
        "e_ready ec_ready xb_sb gm_ready m_ready dtx_ready dtxw_ready y0_ready y_mm state_mm s_sb y1_step y1_ready y2_even y2_odd "
        "sq_ready rs_step rs_ready yT_mm yT_sb out_mm x_done").split()}

    def heads(x, n=64):
        return x.rearrange("p (h n) -> p h n", h=4)

    def over(x, n):
        return x.rearrange("p (h o) -> p h o", o=1).broadcast_to([P, 4, n])

    def gated(eng, q, M, tiles=1):
        wait(eng, s["y2_odd" if q % 2 else "y2_even"], M * 2 + (q // 2 + tiles))

    def schedule(eng, norm, front, tile, late, norm_first=False):
        def pieces(ahead, behind, q):
            for part, unit in (((norm, behind), (front, ahead)) if norm_first else ((front, ahead), (norm, behind))):
                if unit:
                    part(*unit, q)

        for piece in range(Q):
            norm(0, 0, 0, piece)
        for piece in range(Q):
            pieces((0, 0, 0), (1, 0, 1), piece)

        def body(i):
            last = isinstance(i, int) and i == UNITS // 2 - 1
            for u in range(2):
                for q in range(Q):
                    def back(l, u=u, q=q):
                        j = u * Q + q - l
                        if j >= 0:
                            return i * 2 * Q + j, j % Q, j // Q, i * 2 + j // Q, i
                        if isinstance(i, int) and i == 0:
                            return None
                        j += 2 * Q
                        return (i - 1) * 2 * Q + j, j % Q, j // Q, (i - 1) * 2 + j // Q, i - 1
                    tile(back)
                    if u == 0:
                        pieces((i * 2 + 1, i, 1), None if last else (i * 2 + 2, i + 1, 0), q)
                    elif not last:
                        pieces((i * 2 + 2, i + 1, 0), (i * 2 + 3, i + 1, 1), q)
                    late(back)
        body(0)
        with eng.Fori(1, UNITS // 2 - 1) as i:
            body(i)
        body(UNITS // 2 - 1)
        for l0 in range(2):
            def back(l, l0=l0):
                if l <= l0:
                    return None
                k = UNITS * Q + l0 - l
                return k, k % Q, (k // Q) % 2, k // Q, UNITS // 2 - 1
            tile(back)
            late(back)

    with nc.Block() as block:
        @block.tensor
        def _(pe):
            def norm(M, i, u, piece):
                if piece == 3:
                    pe.wait_ge(s["xn_ready"], M * Q + Q)
                    wait(pe, s["g_ready"], M * 2 - 1)
                    for q in range(Q):
                        last = pe.transpose(xnp[:, q * P:(q + 1) * P], m.xn[:, q, :], ident[:])
                    last.then_inc(s["xnT_mm"], 1)

            def front(M, i, u, piece):
                l = i // 2
                if piece == 0:
                    pe.wait_ge(s["xnT_sb"], M + 1)
                    pe.wait_ge(s["wx_ready"], M + 1)
                    wait(pe, s["g_ready"], M * 2)
                    wait(pe, s["x_sb"], M * 3)
                    for c in (1, 0):
                        pe.matmul(Xp[c], m.Wx[:, u, c * P:(c + 1) * P], m.xnT[:, u, :], start=True,
                                  stop=True).then_inc(s["x_mm"], 1)
                    for q in range(Q):
                        last = pe.matmul(dtp[:, 4 * q:4 * q + 4], m.xnT[:, u, q * P:(q + 1) * P],
                                         in_all[:, l, 640:644], start=True, stop=True)
                    last.then_inc(s["dt_mm"], 1)
                if piece == 1:
                    pe.wait_ge(s["x_sb"], M * 3 + 1)
                    pe.matmul(Xp[2], m.Wx[:, u, 2 * P:3 * P], m.xnT[:, u, :], start=True, stop=True).then_inc(s["x_mm"], 1)
                if piece == 2:
                    pe.wait_ge(s["dt_step"], M + 1)
                    pe.wait_ge(s["x_sb"], M * 3 + 2)
                    for half in range(2):
                        for q in (2 * half, 2 * half + 1):
                            last = pe.matmul(Zp[half][:, (q % 2) * 256:(q % 2) * 256 + 256],
                                             m.xnT[:, u, q * P:(q + 1) * P], in_all[:, l, 0:256], start=True, stop=True)
                        last.then_inc(s["z_mm"], 1)

            def tile(back):
                if back(2):
                    k, q, u, M, i = back(2)
                    gated(pe, q, M)
                    pe.wait_ge(s["s_sb"], M * 2 + (q // 2 + 1))
                    for c in range(2):
                        last = pe.transpose(yTp[:, c * P:(c + 1) * P], m.y2[:, q % 2, c * P:(c + 1) * P], ident[:])
                    last.then_inc(s["yT_mm"], 1)
                if back(1):
                    k, q, u, M, i = back(1)
                    pe.wait_ge(s["m_ready"], k + 1)
                    pe.wait_ge(s["dtx_ready"], k + 1)
                    pe.wait_ge(s["y0_ready"], k + 1)
                    if q % 2 == 0:
                        wait(pe, s["y1_ready"], M * 2 + q // 2)
                    else:
                        gated(pe, q - 1, M)
                    pe.matmul(Yp, ident[:], m.y0[:, q % 2, :], start=True, stop=False)
                    for h in range(4):
                        last = pe.matmul(Yp[:, h * 64:(h + 1) * 64], m.M[:, q % 2, h, :],
                                         m.dtx[:, q % 2, h * 64:(h + 1) * 64], start=False, stop=(h == 3))
                    if q % 2 == 0:
                        last.then_inc(s["y_mm"], 1)
                    else:
                        pe.wait_ge(s["s_sb"], (M * 2) + (q // 2 + 1))
                        pe.matmul(Ip, m.CT[0:64, u, q * P:(q + 1) * P], m.state[:], start=True,
                                  stop=True).then_inc(s["y_mm"], 1)
                if back(0):
                    k, q, u, M, i = back(0)
                    tok = slice(q * P, (q + 1) * P)
                    pe.wait_ge(s["am_ready"], k + 1)
                    wait(pe, s["e_ready"], k)
                    for h in range(4):
                        last = pe.matmul(Dps[:, h, :], m.am[:, q % 2, h, :], mem.upto[:], start=True, stop=True)
                    last.then_inc(s["d_mm"], 1)
                if back(1):
                    k, q, u, M, i = back(1)
                    if q % 2 == 0:
                        pe.wait_ge(s["dtxw_ready"], (M * 2) + (q // 2 + 1))
                        wait(pe, s["yT_sb"], k)
                        pe.matmul(Sp, m.xB[:, q % 2, 256:320], m.dtxw[:], start=True, stop=True).then_inc(s["state_mm"], 1)
                if back(0):
                    k, q, u, M, i = back(0)
                    tok = slice(q * P, (q + 1) * P)
                    pe.wait_ge(s["silu_ready"], M * 4 + 4)
                    wait(pe, s["gm_ready"], k)
                    pe.matmul(Gp, m.xs[0:64, u, 2, tok], m.CT[0:64, u, tok], start=True, stop=True).then_inc(s["g_mm"], 1)
                    wait(pe, s["xb_sb"], k)
                    wait(pe, s["x_done"], k - 2)
                    for c in range(2):
                        pe.transpose(xBp[:, c * P:(c + 1) * P], m.xs[:, u, c, tok], ident[:])
                    pe.transpose(xBp[:, 256:320], m.xs[0:64, u, 2, tok], ident[0:64, 0:64])
                    pe.matmul(cump[:, 0:4], mem.upto[:], m.a[:, u, q, :], start=True, stop=True)
                    pe.matmul(cump[:, 4:8], mem.after[:], m.a[:, u, q, :], start=True, stop=True).then_inc(s["xb_mm"], 1)

            def late(back):
                if back(2):
                    k, q, u, M, i = back(2)
                    l = i // 2
                    pe.wait_ge(s["yT_sb"], k + 1)
                    if not back(0):
                        pe.wait_ge(s["x_done"], k)
                    pe.wait_ge(s["xb_sb"], k + 3 if back(0) else UNITS * Q)
                    for c in range(2):
                        last = pe.matmul(outp, m.yT[:, q % 2, c, :],
                                         out_all[:, l * 2 + c, :],
                                         start=(c == 0), stop=(c == 1))
                    last.then_inc(s["out_mm"], 1)
            schedule(pe, norm, front, tile, late)

        @block.scalar
        def _(a):
            def norm(M, i, u, piece):
                if piece == 3:
                    lc = m.lc[:, u, :]
                    a.wait_ge(s["xnT_mm"], M + 1)
                    a.wait_ge(s["lc_ready"], M + 1)
                    a.activation(m.xnT[:, u, :], xnp, ACT.Identity, bias=lc[:, C_LNB:C_LNB + 1],
                                 scale=lc[:, C_LNW:C_LNW + 1]).then_inc(s["xnT_sb"], 1)

            def front(M, i, u, piece):
                lc = m.lc[:, u, :]

                def evacuate(c):
                    a.wait_ge(s["x_mm"], M * 3 + (2, 1, 3)[c])
                    if c == 1:
                        wait(a, s["silu_ready"], M * 4)
                    src = Xp[c]
                    a.activation(m.xc[:, c, :], src, ACT.Identity, bias=lc[:, C_CB + c:C_CB + c + 1],
                                 scale=lc[:, C_CW + 9 + c:C_CW + 10 + c])
                    a.copy(mem.xp[:, c, :, 3:259], src.rearrange("p (b t) -> p b t", b=2)).then_inc(s["x_sb"], 1)

                def tanh(c):
                    if c:
                        a.wait_ge(s["conv_ready"], M * 2 + c)
                    else:
                        a.wait_ge(s["sum_step"], M * 3 + 3)
                    a.activation(m.th[:, c, :], m.xc[:, c, :], ACT.Tanh).then_inc(s["th_ready"], 1)

                def tanh_z(half):
                    a.wait_ge(s["z_mm"], M * 2 + (half + 1))
                    wait(a, s["g_ready"], M * 2 + half - 1)
                    a.activation(m.zt[:, half, :], Zp[half], ACT.Tanh, scale=0.5).then_inc(s["zt_ready"], 1)

                if piece == 0:
                    evacuate(1)
                if piece == 1:
                    evacuate(0)
                    a.wait_ge(s["ax_ready"], M + 1)
                    a.activation(m.eu[:], m.ax[:], ACT.Exp, scale=-1.0).then_inc(s["u_ready"], 1)
                    wait(a, s["sum_step"], M * 3)
                    a.wait_ge(s["x_sb"], M * 3 + 2)
                    for tap in range(3):
                        a.activation(m.taps[:, tap, :].rearrange("p (b t) -> p b t", b=2), mem.xp[:, 0, :, tap:tap + 256],
                                     ACT.Copy, scale=lc[:, C_CW + tap * 3:C_CW + tap * 3 + 1]).then_inc(s["product_ready"], 1)
                if piece == 2:
                    evacuate(2)
                    tanh(1)
                    tanh_z(0)
                    tanh_z(1)
                if piece == 3:
                    tanh(2)
                    tanh(0)

            def tile(back):
                if back(2):
                    k, q, u, M, i = back(2)
                    a.wait_ge(s["yT_mm"], k + 1)
                    wait(a, s["out_mm"], k - 1)
                    a.copy(m.yT[:, q % 2, :, :].rearrange("p c t -> p (c t)"), yTp).then_inc(s["yT_sb"], 1)
                if back(0):
                    k, q, u, M, i = back(0)
                    a.wait_ge(s["d_mm"], k + 1)
                    wait(a, s["m_ready"], k - 1)
                    a.activation(m.E[:, q % 2, :], ps[:, 3, :], ACT.Exp).then_inc(s["e_ready"], 1)
                if back(1):
                    k, q, u, M, i = back(1)
                    if q % 2 == 0:
                        a.wait_ge(s["state_mm"], M * 2 + (q // 2 + 1))
                        wait(a, s["y_mm"], k)
                        a.copy(m.state[:], Sp).then_inc(s["s_sb"], 1)
                if back(0):
                    k, q, u, M, i = back(0)
                    a.wait_ge(s["xb_mm"], k + 1)
                    if q % 2 == 0:
                        wait(a, s["state_mm"], M * 2 + q // 2)
                    else:
                        wait(a, s["y1_ready"], M * 2 + q // 2)
                    a.activation(m.ec[:, q % 2, :], cump, ACT.Exp).then_inc(s["ec_ready"], 1)
                    wait(a, s["y_mm"], k - 1)
                    if q % 2 == 0:
                        wait(a, s["state_mm"], M * 2 + q // 2)
                    wait(a, s["y0_ready"], k - 1)
                    a.copy(m.xB[:, q % 2, :], xBp).then_inc(s["xb_sb"], 1)
                if back(2):
                    k, q, u, M, i = back(2)
                    wait(a, s["rs_ready"], k - 1)
                    a.activation(m.junk[:, q % 2, :], m.y2[:, q % 2, :], ACT.Square, scale=1.0 / 16,
                                 accum_out=m.ssq[:, q % 2, :]).then_inc(s["sq_ready"], 1)
            schedule(a, norm, front, tile, lambda back: None)

        @block.vector
        def _(v):
            st = Steps(v, s["stat_step"], 8)
            cs = Steps(v, s["conv_step"], 4)
            dt = Steps(v, mem.sem("m_dt_chain"), 11)
            ys = Steps(v, s["y1_step"], 1)

            def norm(M, i, u, piece):
                l, base = i // 2, (i % 2) * 8 + u * 4
                if piece == 0:
                    st.at(M)
                    wait(v, s["x_done"], M * Q - 12)
                    wait(v, s["a_ready"], M - 1)
                    v.tensor_scalar(m.lc[:, u, :], tab[:, l, :], 1.0, None, ALU.mult).then_inc(s["lc_ready"], 1)
                    for q in range(Q):
                        st.mark(v.bn_stats(m.stats[:, q, :], xm[:, base + q, :]))
                    st.join()
                    wait(v, s["x_mm"], M * 3 - 3)
                    v.tensor_scalar(m.Wx[:, u, :], in_all[:, l, 256:640], 1.0, None, ALU.mult).then_inc(s["wx_ready"], 1)
                    for q in range(Q):
                        st.mark(v.bn_aggr(m.mv[:, q, :], m.stats[:, q, :]))
                    st.join()
                    v.tensor_scalar(m.veps[:], m.mv[:, :, 1], EPS, None, ALU.add).then_inc(s["var_ready"], 1)
                    st.end()
                if piece == 1:
                    wait(v, s["xnT_mm"], M)
                    v.wait_ge(s["rstd_ready"], M + 1)
                    for q in range(Q):
                        v.tensor_scalar(m.xn[:, q, :], xm[:, base + q, :], m.mv[:, q, 0:1], m.rstd[:, q:q + 1],
                                        ALU.subtract, ALU.mult).then_inc(s["xn_ready"], 1)

            def front(M, i, u, piece):
                lc = m.lc[:, u, :]
                l = i // 2

                def tap_sum(c, tap):
                    xc = m.xc[:, c, :].rearrange("p (b t) -> p b t", b=2)
                    ins = v.scalar_tensor_tensor(out=xc, in0=mem.xp[:, c, :, tap:tap + 256],
                                                 scalar=lc[:, C_CW + tap * 3 + c:C_CW + tap * 3 + c + 1], in1=xc,
                                                 op0=ALU.mult, op1=ALU.add)
                    if tap < 2:
                        cs.mark(ins)
                    else:
                        ins.then_inc(s["conv_ready"], 1)

                def silu(c, rows, out):
                    v.scalar_tensor_tensor(out=out, in0=m.th[rows, c, :], scalar=1.0, in1=m.xc[rows, c, :],
                                           op0=ALU.add, op1=ALU.mult).then_inc(s["silu_ready"], 1)

                def gate(half):
                    v.wait_ge(s["zt_ready"], M * 2 + (half + 1))
                    v.scalar_tensor_tensor(out=m.g[:, u, 2 * half:2 * half + 2, :].rearrange("p q e -> p (q e)"),
                                           in0=m.zt[:, half, :], scalar=1.0, in1=Zp[half], op0=ALU.add,
                                           op1=ALU.mult).then_inc(s["g_ready"], 1)

                if piece == 0:
                    wait(v, s["y0_ready"], M * Q - 4)
                    v.tensor_scalar(m.Dp[:, u, :], tab[:, l, C_DP:C_DP + 4], 1.0, None, ALU.mult).then_inc(s["dp_ready"], 1)
                if piece == 1:
                    v.wait_ge(s["dt_mm"], M + 1)
                    v.tensor_tensor(m.x4[:], dtp.rearrange("p (q h) -> p q h", q=Q),
                                    lc[:, C_DTB:C_DTB + 4].rearrange("p (o h) -> p o h", o=1).broadcast_to([P, Q, 4]),
                                    ALU.add).then_inc(s["dt_step"], 1)
                    v.wait_ge(s["dt_step"], M + 1)
                    v.scalar_tensor_tensor(out=m.ax[:], in0=m.x4[:], scalar=-1.0, in1=m.x4[:], op0=ALU.mult,
                                           op1=ALU.max).then_inc(s["ax_ready"], 1)
                    cs.at(M)
                    v.wait_ge(s["x_sb"], M * 3 + 1)
                    for tap in range(3):
                        tap_sum(1, tap)
                        if tap < 2:
                            cs.join()
                if piece == 2:
                    dt.at(M)
                    v.wait_ge(s["u_ready"], M + 1)
                    dt.link(v.tensor_scalar(m.poly[:], m.eu[:], LOG1P[9], None, ALU.mult))
                    for n, c in enumerate(LOG1P[8::-1]):
                        dt.mark(v.scalar_tensor_tensor(out=m.poly[:], in0=m.poly[:], scalar=c, in1=m.eu[:],
                                                       op0=ALU.add, op1=ALU.mult))
                        if n >= 6:
                            if n == 6:
                                v.wait_ge(s["x_sb"], M * 3 + 3)
                            else:
                                cs.join()
                            tap_sum(2, n - 6)
                        dt.join()
                    dt.link(v.scalar_tensor_tensor(out=m.sp[:, u, :, :], in0=m.x4[:], scalar=0.0, in1=m.poly[:],
                                                   op0=ALU.max, op1=ALU.add))
                    dt.end()
                    wait(v, s["am_ready"], M * Q - 4)
                    v.tensor_tensor(m.a[:, u, :, :], m.sp[:, u, :, :],
                                    lc[:, C_A:C_A + 4].rearrange("p (o h) -> p o h", o=1).broadcast_to([P, Q, 4]),
                                    ALU.mult).then_inc(s["a_ready"], 1)
                    v.wait_ge(s["th_ready"], M * 3 + 1)
                    wait(v, s["y_mm"], M * Q - 4)
                    silu(1, slice(0, P), m.xs[:, u, 1, :])
                    for q in (2, 3):
                        gated(v, q, M - 2)
                    gate(0)
                if piece == 3:
                    gate(1)
                    v.wait_ge(s["th_ready"], M * 3 + 2)
                    silu(2, slice(0, 64), m.xs[0:64, u, 2, :])
                    silu(2, slice(64, P), m.CT[0:64, u, :])
                    v.wait_ge(s["th_ready"], M * 3 + 3)
                    silu(0, slice(0, P), m.xs[:, u, 0, :])

            def tile(back):
                if back(1):
                    k, q, u, M, i = back(1)
                    v.wait_ge(s["y_mm"], k + 1)
                    if q % 2 == 0:
                        wait(v, s["sq_ready"], k - 1)
                        v.tensor_tensor(m.y2[:, 0, :], Yp, m.g[:, u, q, :], ALU.mult).then_inc(s["y2_even"], 1)
                    else:
                        ys.at(M * 2 + q // 2)
                        gated(v, q, M, tiles=0)
                        ys.link(v.tensor_tensor(heads(m.yi[:]), heads(Ip), over(m.ec[:, 1, 0:4], 64), ALU.mult))
                        v.tensor_tensor(m.y1[:], m.yi[:], Yp, ALU.add).then_inc(s["y1_ready"], 1)
                if back(0):
                    k, q, u, M, i = back(0)
                    v.wait_ge(s["g_mm"], k + 1)
                    v.tensor_tensor(m.Gm[:], Gp, mem.upto[:], ALU.mult).then_inc(s["gm_ready"], 1)
                    v.wait_ge(s["gm_ready"], k + 1)
                    v.wait_ge(s["e_ready"], k + 1)
                    wait(v, s["y_mm"], k - 1)
                    v.tensor_tensor(m.M[:, q % 2, :, :], heads(m.E[:, q % 2, :]),
                                    m.Gm[:].rearrange("p (o t) -> p o t", o=1).broadcast_to([P, 4, P]),
                                    ALU.mult).then_inc(s["m_ready"], 1)

            def late(back):
                if back(2):
                    k, q, u, M, i = back(2)
                    v.wait_ge(s["out_mm"], k + 1)
                    v.wait_ge(s["rs_ready"], k + 1)
                    tok = (i % 2) * 8 + (u * 4 + q)
                    v.scalar_tensor_tensor(out=xm[:, tok, :], in0=outp, scalar=m.rs[:, q % 2, :], in1=xm[:, tok, :],
                                           op0=ALU.mult, op1=ALU.add).then_inc(s["x_done"], 1)
            schedule(v, norm, front, tile, late, norm_first=True)
            v.wait_ge(s["x_done"], UNITS * Q)

        @block.gpsimd
        def _(g):
            rs = Steps(g, s["rs_step"], 1)

            def scale_decays(k, q, u, M):
                g.wait_ge(s["a_ready"], M + 1)
                wait(g, s["d_mm"], k - 1)
                g.tensor_tensor(m.am[:, q % 2, :, :], mem.after[:].rearrange("p (o t) -> p o t", o=1).broadcast_to([P, 4, P]),
                                over(m.a[:, u, q, :], P), ALU.mult).then_inc(s["am_ready"], 1)

            def norm(M, i, u, piece):
                if piece == 0:
                    g.wait_ge(s["var_ready"], M + 1)
                    wait(g, s["xn_ready"], M * Q)
                    g.tensor_tensor(m.rstd[:], m.veps[:], mem.neg_half[:, 0:Q], ALU.pow).then_inc(s["rstd_ready"], 1)

            def front(M, i, u, piece):
                taps = (0, 1, 2) if piece == 2 else ()
                for tap in taps:
                    g.wait_ge(s["product_ready"], M * 3 + (tap + 1))
                    wait(g, s["sum_step"], M * 3 + tap)
                    g.tensor_tensor(m.xc[:, 0, :], m.xc[:, 0, :], m.taps[:, tap, :], ALU.add).then_inc(s["sum_step"], 1)
                if piece == 3:
                    scale_decays(M * Q, 0, u, M)

            def tile(back):
                if back(1):
                    k, q, u, M, i = back(1)
                    if q % 2 == 1:
                        g.wait_ge(s["y1_ready"], M * 2 + (q // 2 + 1))
                        wait(g, s["sq_ready"], k - 1)
                        g.tensor_tensor(m.y2[:, 1, :], m.y1[:], m.g[:, u, q, :], ALU.mult).then_inc(s["y2_odd"], 1)
                if back(0):
                    k, q, u, M, i = back(0)
                    if q < Q - 1:
                        scale_decays(k + 1, q + 1, u, M)
                    g.wait_ge(s["xb_sb"], k + 1)
                    wait(g, s["y_mm"], k - 1)
                    g.tensor_tensor(heads(m.dtx[:, q % 2, :]), heads(m.xB[:, q % 2, 0:256]), over(m.sp[:, u, q, :], 64),
                                    ALU.mult).then_inc(s["dtx_ready"], 1)
                    g.wait_ge(s["dp_ready"], M + 1)
                    wait(g, s["y_mm"], k - 1)
                    g.tensor_tensor(heads(m.y0[:, q % 2, :]), heads(m.xB[:, q % 2, 0:256]),
                                    over(m.Dp[:, u, :], 64), ALU.mult).then_inc(s["y0_ready"], 1)
                    if q % 2 == 0:
                        g.wait_ge(s["dtx_ready"], k + 1)
                        g.wait_ge(s["ec_ready"], k + 1)
                        wait(g, s["state_mm"], M * 2 + q // 2)
                        g.tensor_tensor(heads(m.dtxw[:]), heads(m.dtx[:, q % 2, :]), over(m.ec[:, q % 2, 4:8], 64),
                                        ALU.mult).then_inc(s["dtxw_ready"], 1)
                if back(2):
                    k, q, u, M, i = back(2)
                    rs.at(k)
                    g.wait_ge(s["sq_ready"], k + 1)
                    wait(g, s["x_done"], k - 1)
                    rs.link(g.tensor_tensor(m.rt[:, q % 2, :], m.ssq[:, q % 2, :], mem.eps4[:, 0:1], ALU.add))
                    g.tensor_tensor(m.rs[:, q % 2, :], m.rt[:, q % 2, :], mem.neg_half[:, 0:1], ALU.pow).then_inc(s["rs_ready"], 1)
            schedule(g, norm, front, tile, lambda back: None)


def normalise(nc, mem, name, src, dst):
    rstd_ready, done = mem.sem(name + "_rstd"), mem.sem(name + "_done")
    mem.var_ready = mem.sem(name + "_var")
    with nc.Block() as block:
        @block.vector
        def _(v):
            layer_norm_stats(v, mem, name, lambda t: src[:, t, :])
            for t in range(16):
                v.wait_ge(rstd_ready, t // 8 + 1)
                v.tensor_scalar(dst[:, t, :], src[:, t, :], mem.mv[:, t, 0:1], mem.rstd[:, t:t + 1],
                                ALU.subtract, ALU.mult).then_inc(done, 1)
            v.wait_ge(done, 16)

        @block.gpsimd
        def _(g):
            layer_norm_power(g, mem, rstd_ready)


class Buffers:
    pass


def mixture_buffers(mem, name):
    mem.hidden = mem.sb(name + "_hidden", [P, 2, 2, 512])
    mem.W1h, mem.W1l = mem.sb(name + "_W1h", [P, 2, 256], F32R), mem.sb(name + "_W1l", [P, 2, 256], F32R)
    return mem.sb(name + "_high", [P, 2048], F32R), mem.sb(name + "_low", [P, 2048], F32R)


def program(nc, t, out):
    with ExitStack() as ctx:
        mem = Memory(nc, ctx)
        NT = 16
        x_all = mem.sb("x_all", [P, NT, P])
        mem.ps = ctx.enter_context(nc.psum_tensor("ps", [P, 8, 512], F32))
        mem.big_a = mem.sb("big_a", [P, 2048])
        mem.tokens_b = mem.sb("tokens_b", [P, NT, P])
        mem.tokens_a = mem.sb("tokens_a", [P, NT, P])
        mem.ident = mem.sb("ident", [P, P])
        mem.neg_half = mem.sb("neg_half", [P, NT])
        mem.stats = mem.sb("stats", [P, NT, 6])
        mem.mv, mem.var, mem.rstd = mem.sb("mv", [P, NT, 2]), mem.sb("var", [P, NT]), mem.sb("rstd", [P, NT])
        mem.stage_a = mem.sb("stage_a", [P, 2, 4, P])
        w = {}
        mem.r_logits, mem.r_above, mem.r_equal, mem.r_seen, mem.r_exp, mem.gates = (
            mem.sb(n, [P, 256]) for n in ("r_logits", "r_above", "r_equal", "r_seen", "r_exp", "gates"))
        mem.best, mem.r_small, mem.gatesT = mem.sb("best", [P, NT, 8]), mem.sb("r_small", [P, 4, NT]), mem.sb("gatesT", [16, NT * P])
        mem.keep = {e: mem.sb(f"keep{e}", [P, NT * e]) for e in (16, 8)}
        mem.layers, mem.layer_rows = mem.sb("layers", [P, 4, C_ALL]), mem.sb("layer_rows", [P, 3, 4, 4])
        mem.in_all, mem.out_all = mem.sb("in_all", [P, 4, 644]), mem.sb("out_all", [P, 8, P])
        mem.upto, mem.after, mem.eps4 = mem.sb("upto", [P, P]), mem.sb("after", [P, P]), mem.sb("eps4", [P, 1])
        mem.xp = mem.sb("xp", [P, 3, 2, 259])
        mem.W1, mem.W2 = mem.sb("W1", [P, 2, 256]), mem.sb("W2", [P, 2, 2, P])

        mem.bias = mem.sb("bias", [P, 2, 2])
        w["router0"], w["router1"] = mem.sb("router0", [P, 16]), mem.sb("router1", [P, 8])
        w["mix_w"], w["mix_b"] = mem.sb("mix_w", [P, P]), mem.sb("mix_b", [P, P])
        w["rb0"] = mem.sb("rb0", [P, 16])
        w["b2_0"], w["b2_1"] = mem.sb("b2_0", [16, P]), mem.sb("b2_1", [8, P])
        rows = [mem.sb(f"rows{i}", [P, P]) for i in range(2)]
        cols = [mem.sb(f"cols{i}", [P, P]) for i in range(2)]
        mem.vec_in, mem.layers_loaded = mem.sem("vec_in"), mem.sem("layers_loaded")
        rows_zero, keep_zero = mem.sem("rows_zero"), mem.sem("keep_zero")
        mem.x_in, mem.consts_ready = [mem.sem(f"x_in{g}") for g in range(4)], mem.sem("consts_ready")
        w["attn_in"], w["attn_in_n"] = mem.sem("attn_in"), 5 * 16
        ident_zero = mem.sem("ident_zero")
        out_done = mem.sem("out_done")

        mem.phase()
        w["Wq"] = mem.sb("Wq", [P, 1024])
        w["Wkk"] = mem.sb("Wkk", [P, 4, 2, 64])
        w["Wv"] = mem.sb("Wv", [P, 256])
        w["Wpost"] = mem.sb("Wpost", [P, 8, P])
        mem.stage_c = mem.sb("stage_c", [P, 2, 512])
        mem.Q, mem.K = mem.sb("Q", [P, 2, 2, P], F32R), mem.sb("K", [P, 2, 256], F32R)
        mem.Ql, mem.Kl = mem.sb("Ql", [P, 2, 2, P], F32R), mem.sb("Kl", [P, 2, 256], F32R)
        mem.probs, mem.probsT = mem.sb("probs", [P, 2, 4, 256]), mem.sb("probsT", [P, 2, 2, 4, P])
        mem.Atile = mem.sb("Atile", [P, 2, 256])
        mem.nm, mem.den, mem.rden = mem.sb("nm", [P, 2, 4]), mem.sb("den", [P, 4, 4]), mem.sb("rden", [P, 4])
        mem.big_b, mem.big_c = mem.sb("big_b", [P, 8 * 2048]), mem.sb("big_c", [P, 4096])
        vector_rows, at = [], {}
        place = [0, 0]

        def vector(name, tile, src):
            n = src.shape[0]
            vector_rows.append((tile, place[tile], src))
            at[name] = cols[tile][:, place[tile]:place[tile] + n]
            place[tile] += n

        vector("b1_0", 0, t["L0_ffn_b1"].rearrange("e (h p) -> (e h) p", p=P))
        vector("b1_1", 0, t["L1_ffn_b1"].rearrange("e (h p) -> (e h) p", p=P))
        for n in ("g1", "be1", "g2", "be2"):
            vector(n, 1, t["L1_ffn_" + n].rearrange("(o d) -> o d", o=1))
        vector("conv_w", 1, t["L1_attn_conv_w"].rearrange("l k (c p) -> (l k c) p", p=P))
        vector("conv_b", 1, t["L1_attn_conv_b"].rearrange("l (c p) -> (l c) p", p=P))
        vector("ln_w", 1, t["L1_attn_ln_w"])
        vector("ln_b", 1, t["L1_attn_ln_b"])
        vector("norm_w", 1, t["L1_attn_norm_w"].rearrange("l (c p) -> (l c) p", p=P))
        b1_at = [0, 32]
        vec_in_n = 16 * (len(vector_rows) + 7)

        def later_loads(sp):
            sp.wait_ge(rows_zero, 2)
            for tile, at, src in vector_rows:
                n = src.shape[0]
                sp.dma_start(rows[tile][at:at + n, :], src).then_inc(mem.vec_in, 16)
            sp.dma_start(w["router0"][:], t["L0_ffn_router_w"]).then_inc(mem.vec_in, 16)
            sp.dma_start(w["router1"][:], t["L1_ffn_router_w"]).then_inc(mem.vec_in, 16)
            sp.dma_start(w["rb0"][:], t["L0_ffn_router_b"].rearrange("(o e) -> o e", o=1).broadcast_to([P, 16])).then_inc(mem.vec_in, 16)
            sp.dma_start(w["b2_0"][:], t["L0_ffn_b2"]).then_inc(mem.vec_in, 16)
            sp.dma_start(w["mix_w"][:], t["L1_ffn_mix_w"]).then_inc(mem.vec_in, 16)
            sp.dma_start(w["mix_b"][:], t["L1_ffn_mix_b"].rearrange("(o d) -> o d", o=1).broadcast_to([P, P])).then_inc(mem.vec_in, 16)
            sp.dma_start(w["b2_1"][:], t["L1_ffn_b2"]).then_inc(mem.vec_in, 16)
            layers_in(sp, mem, t, mem.layers_loaded)

        with nc.Block() as block:
            @block.sync
            def _(sp):
                x = t["L0_attn_X"].rearrange("b (t p) d -> p (b t) d", p=P)
                for g in range(4):
                    sp.dma_start(x_all[:, 4 * g:4 * g + 4, :], x[:, 4 * g:4 * g + 4, :]).then_inc(mem.x_in[g], 16)
                sp.dma_start(w["Wv"][:], t["L0_attn_Wv"]).then_inc(w["attn_in"], 16)
                wk = t["L0_attn_Wk"].rearrange("d (g e) -> d g e", g=4)
                for r in range(2):
                    sp.dma_start(w["Wkk"][:, :, r, :], wk).then_inc(w["attn_in"], 16)
                sp.dma_start(w["Wq"][:], t["L0_attn_Wq"]).then_inc(w["attn_in"], 16)
                sp.dma_start(w["Wpost"][:], t["L0_attn_Wpost"].rearrange("(c p) d -> p c d", p=P)).then_inc(w["attn_in"], 16)

            @block.vector
            def _(v):
                for i in range(2):
                    v.memset(rows[i][:], 0.0).then_inc(rows_zero, 1)
                for e in (16, 8):
                    v.memset(mem.keep[e][:], 1.0).then_inc(keep_zero, 1)
                v.wait_ge(keep_zero, 2)
                for e in (16, 8):
                    v.memset(mem.keep[e][:].rearrange("p (t e) -> p t e", e=e)[:, :, 0:1], 0.0).then_inc(keep_zero, 1)
                v.wait_ge(keep_zero, 4)

            @block.gpsimd
            def _(g):
                g.memset(mem.neg_half[:], -0.5)
                g.memset(mem.ident[:], 0.0).then_inc(ident_zero, 1)
                g.wait_ge(ident_zero, 1)
                g.affine_select(out=mem.ident[:], in_=mem.ident[:], pattern=[[-1, P]], compare_op=ALU.not_equal,
                                fill=1.0, base=0, channel_multiplier=1).then_inc(mem.consts_ready, 1)

        attention(nc, mem, x_all, w, later_loads)
        mem.end_phase()
        nT, acc = mem.big_a[:], mem.tokens_a
        mem.phase()
        columns_and_masks(nc, mem, rows, cols, vec_in_n)
        parts = mixture_buffers(mem, "e")
        normalised_transposes(nc, mem, "e0", x_all, nT, parts, 16, [w["router0"][:]], mem.vec_in, vec_in_n)
        route(nc, mem, "e1", 16, 4, True, w["rb0"][:], w["b2_0"][:], acc)
        gates0 = mem.gates[:, 0:NT * 16]
        mixture(nc, mem, "e2", parts, acc, t["L0_ffn_w1"].rearrange("(i u) h f -> i u h f", u=2),
                t["L0_ffn_w2"].rearrange("(i u) f h -> i u f h", u=2), cols[0][:, b1_at[0]:b1_at[0] + 36],
                lambda tok, i, u: gates0[:, bass.ds(i * 2 + (tok * 16 + u), 1)], ACT.Gelu,
                first=lambda v: mamba_constants(v, mem, at, w["mix_w"][:]))
        add_layer_norm(nc, mem, "e3", acc, x_all)
        mem.end_phase()
        xm = mem.tokens_a
        normalise(nc, mem, "m0", x_all, xm)
        mem.phase()
        mem.m = m = Buffers()
        m.lc = mem.sb("m_lc", [P, 2, C_ALL])
        m.Dp = mem.sb("m_Dp", [P, 2, 4])
        m.Wx = mem.sb("m_Wx", [P, 2, 384])
        m.stats = mem.sb("m_stats", [P, 4, 6])
        m.mv = mem.sb("m_mv", [P, 4, 2])
        m.veps = mem.sb("m_veps", [P, 4])
        m.rstd = mem.sb("m_rstd", [P, 4])
        m.xn = mem.sb("m_xn", [P, 4, P])
        m.xnT = mem.sb("m_xnT", [P, 2, 512])
        m.xc = mem.sb("m_xc", [P, 3, 512])
        m.taps = mem.sb("m_taps", [P, 3, 512])
        m.th = mem.sb("m_th", [P, 3, 512])
        m.xs = mem.sb("m_xs", [P, 2, 3, 512])
        m.CT = mem.sb("m_CT", [64, 2, 512])
        m.zt = mem.sb("m_zt", [P, 2, 512])
        m.g = mem.sb("m_g", [P, 2, 4, 256])
        m.x4 = mem.sb("m_x4", [P, 4, 4])
        m.ax = mem.sb("m_ax", [P, 4, 4])
        m.eu = mem.sb("m_eu", [P, 4, 4])
        m.poly = mem.sb("m_poly", [P, 4, 4])
        m.sp = mem.sb("m_sp", [P, 2, 4, 4])
        m.a = mem.sb("m_a", [P, 2, 4, 4])
        m.am = mem.sb("m_am", [P, 2, 4, P])
        m.E = mem.sb("m_E", [P, 2, 512])
        m.Gm = mem.sb("m_Gm", [P, P])
        m.M = mem.sb("m_M", [P, 2, 4, P])
        m.ec = mem.sb("m_ec", [P, 2, 8])
        m.xB = mem.sb("m_xB", [P, 2, 320])
        m.dtx = mem.sb("m_dtx", [P, 2, 256])
        m.dtxw = mem.sb("m_dtxw", [P, 256])
        m.y0 = mem.sb("m_y0", [P, 2, 256])
        m.state = mem.sb("m_state", [64, 256])
        m.yi = mem.sb("m_yi", [P, 256])
        m.y1 = mem.sb("m_y1", [P, 256])
        m.y2 = mem.sb("m_y2", [P, 2, 256])
        m.junk = mem.sb("m_junk", [P, 2, 256])
        m.ssq = mem.sb("m_ssq", [P, 2, 1])
        m.rt = mem.sb("m_rt", [P, 2, 1])
        m.rs = mem.sb("m_rs", [P, 2, 1])
        m.yT = mem.sb("m_yT", [P, 2, 2, P])
        mamba(nc, mem, xm)
        mem.end_phase()
        add_layer_norm(nc, mem, "m2", xm, x_all)
        x2 = mem.tokens_b
        mem.phase()
        parts = mixture_buffers(mem, "f")
        normalise(nc, mem, "f0", x_all, x2)
        normalised_transposes(nc, mem, "f1", x2, nT, None, P,
                              [w["mix_w"][:]], mem.vec_in, vec_in_n, pre=(at["g1"], at["be1"]), add_to=x2,
                              shift=w["mix_b"][:])
        normalised_transposes(nc, mem, "f3", x2, nT, parts, 8, [w["router1"][:]], mem.vec_in, vec_in_n,
                              pre=(at["g2"], at["be2"]))
        route(nc, mem, "f4", 8, 2, False, None, w["b2_1"][:], acc)
        gates1 = mem.gates[:, 0:NT * 8]
        mixture(nc, mem, "f5", parts, acc, t["L1_ffn_w1"].rearrange("e h (s f) -> e s h f", s=2),
                t["L1_ffn_w2"].rearrange("e (s f) h -> e s f h", s=2), cols[0][:, b1_at[1]:b1_at[1] + 36],
                lambda tok, i, u: gates1[:, bass.ds(i + tok * 8, 1)], ACT.Silu)
        add_layer_norm(nc, mem, "f7", acc, x_all, more=x2)
        mem.end_phase()

        with nc.Block() as block:
            @block.sync
            def _(sp):
                sp.dma_start(out.rearrange("b (t p) d -> p (b t) d", p=P), x_all[:]).then_inc(out_done, 16)
                sp.wait_ge(out_done, 16)


_INS = ['L0_attn_X', 'L0_attn_Wq', 'L0_attn_Wk', 'L0_attn_Wv', 'L0_attn_Wpost', 'L0_ffn_router_w', 'L0_ffn_router_b',
        'L0_ffn_w1', 'L0_ffn_b1', 'L0_ffn_w2', 'L0_ffn_b2', 'L1_attn_ln_w', 'L1_attn_ln_b', 'L1_attn_in_w',
        'L1_attn_conv_w', 'L1_attn_conv_b', 'L1_attn_dt_bias', 'L1_attn_A_log', 'L1_attn_Dp', 'L1_attn_norm_w',
        'L1_attn_out_w', 'L1_ffn_g1', 'L1_ffn_be1', 'L1_ffn_mix_w', 'L1_ffn_mix_b', 'L1_ffn_g2', 'L1_ffn_be2',
        'L1_ffn_router_w', 'L1_ffn_w1', 'L1_ffn_b1', 'L1_ffn_w2', 'L1_ffn_b2']
_OUTS = [((8, 256, 128), 'float32')]


def kernel(**inputs):
    import numpy as _np
    import concourse.bacc as _bacc
    from concourse import mybir as _mybir
    from concourse.bass_utils import run_bass_kernel_spmd as _run

    nc = _bacc.Bacc("TRN2", target_bir_lowering=False, num_devices=1)
    arrays, tensors = {}, {}
    for name in _INS:
        a = _np.ascontiguousarray(inputs[name])
        arrays[f"in_{name}_dram"] = a
        tensors[name] = nc.dram_tensor(f"in_{name}_dram", a.shape, _mybir.dt.from_np(a.dtype), kind="ExternalInput").ap()
    shape, dtype = _OUTS[0]
    out = nc.dram_tensor("out_0_dram", shape, _mybir.dt.from_np(_np.dtype(dtype)), kind="ExternalOutput").ap()
    program(nc, tensors, out)
    r = _run(nc, [arrays], core_ids=[0])
    return r.results[0]["out_0_dram"]
```
